# Optimizing a Trainium2 kernel written in Bass

```python
import numpy as np
import jax
import jax.numpy as jnp

def _softmax(x, axis=-1):
    return jax.nn.softmax(x, axis=axis)

def _gelu(x):
    return jax.nn.gelu(x, approximate=True)

def _silu(x):
    return jax.nn.silu(x)

def _sigmoid(x):
    return jax.nn.sigmoid(x)

def _layernorm(x, axis=-1, eps=1e-05):
    m = jnp.mean(x, axis=axis, keepdims=True)
    v = jnp.var(x, axis=axis, keepdims=True)
    return (x - m) / jnp.sqrt(v + eps)

def _scatter_add(tgt, idx, src, axis=0):
    return tgt.at[idx].add(src)

def _segment_sum(src, seg, n):
    return jax.ops.segment_sum(src, seg, n)
kernel_name = 'mk_xattn_ffn_d2_seqx_r4_6f7d33'

def setup_inputs(seed: int=0):
    np.random.seed(seed)
    _w = jnp.asarray

    def _rec_inputs():
        import jax
        import jax.numpy as jnp
        _rk = jax.random.key(seed)
        x = -0.0003929 + 0.9999 * jax.random.normal(jax.random.fold_in(_rk, 1), (32, 128, 1024), jnp.float32)
        _lenS = 128 - jax.random.randint(jax.random.fold_in(_rk, 7), (32,), 0, max(1, 128 // 4) + 1, jnp.int32)
        _lenS2 = 128 - jax.random.randint(jax.random.fold_in(_rk, 8), (32,), 0, max(1, 128 // 4) + 1, jnp.int32)
        _ctx_4096P = jax.random.normal(jax.random.fold_in(_rk, 11), (32, 16, 1024), jnp.float32)
        _ctx_4096c = jax.random.dirichlet(jax.random.fold_in(_rk, 511), 0.3 * jnp.ones((16,), jnp.float32), (32, 128))
        _ctx_4096t = jnp.einsum('bsk,bkd->bsd', _ctx_4096c, _ctx_4096P)
        _ctx_4096t = _ctx_4096t * jax.lax.rsqrt(jnp.mean(jnp.square(_ctx_4096t)) + 1e-12) * 0.953939
        ctx_4096 = 2.81802e-05 + 1.00001 * (_ctx_4096t + 0.3 * jax.random.normal(jax.random.fold_in(_rk, 611), (32, 128, 1024), jnp.float32))
        return (x, ctx_4096)
    x, ctx_4096 = _rec_inputs()

    def _L0_xattn_setup():
        import jax, jax.numpy as jnp
        import numpy as np
        DIM = 128
        HEADS = 8
        DIM_HEAD = 64
        HIDDEN = HEADS * DIM_HEAD
        SCALE = DIM_HEAD ** (-0.5)
        key = jax.random.key(seed)
        ks = jax.random.split(key, 9)
        b, n = (8, 1024)
        std = 1.0 / np.sqrt(DIM)
        return {'q': jax.random.normal(ks[0], (b, DIM, n), jnp.float32), 'k': jax.random.normal(ks[1], (b, DIM, n), jnp.float32), 'v': jax.random.normal(ks[2], (b, DIM, n), jnp.float32), 'Wq': jax.random.normal(ks[3], (HIDDEN, DIM), jnp.float32) * std, 'Wk': jax.random.normal(ks[4], (HIDDEN, DIM), jnp.float32) * std, 'Wv': jax.random.normal(ks[5], (HIDDEN, DIM), jnp.float32) * std, 'Wo': jax.random.normal(ks[6], (DIM, HIDDEN), jnp.float32) * (1.0 / np.sqrt(HIDDEN)), 'bo': jax.random.normal(ks[7], (DIM,), jnp.float32) * 0.01, 'g': jnp.ones((1, DIM, 1), jnp.float32)}
    _L0_xattn_all = _L0_xattn_setup()
    _L0_xattn_in = {k: v for k, v in _L0_xattn_all.items() if k in ('Wq', 'Wk', 'Wv', 'Wo', 'bo', 'g')}
    del _L0_xattn_all

    def _L0_ffn_setup():
        import jax, jax.numpy as jnp
        import numpy as np
        HID, BOT, RDIM, NSLOT, K, VB = (1024, 64, 48, 256, 8, 64)
        TAU_LOW, TAU_HIGH, EARLY_EXIT = (0.5, 2.0, 0.05)

        def _uncertainty(h, Wu1, bu1, Wu2, bu2):
            var = jnp.var(h, axis=-1)
            log_var = jnp.log1p(var)
            norm_var = log_var / (jnp.mean(log_var) + 1e-06)
            learned = (jax.nn.gelu(h @ Wu1.T + bu1) @ Wu2.T + bu2)[..., 0]
            return jnp.clip(norm_var * 0.5 + jax.nn.sigmoid(learned) * 2.5, 0.0, 5.0)
        key = jax.random.key(seed)
        ks = jax.random.split(key, 12)
        B, S = (2, 512)
        return {'hidden_states': jax.random.normal(ks[0], (B, S, HID), dtype=jnp.float32), 'Wq': jax.random.normal(ks[1], (BOT, HID), dtype=jnp.float32) / np.sqrt(HID), 'Wr': jax.random.normal(ks[2], (RDIM, BOT), dtype=jnp.float32) / np.sqrt(BOT), 'aux_keys': jax.random.normal(ks[3], (NSLOT, BOT), dtype=jnp.float32) * 0.01, 'aux_values': jax.random.normal(ks[4], (NSLOT, HID), dtype=jnp.float32) * 0.02, 'Wvd': jax.random.normal(ks[5], (VB, HID), dtype=jnp.float32) * 0.1 / np.sqrt(HID), 'Wvu': jax.random.normal(ks[6], (HID, VB), dtype=jnp.float32) * 0.1 / np.sqrt(VB), 'Wu1': jax.random.normal(ks[7], (HID // 4, HID), dtype=jnp.float32) / np.sqrt(HID), 'bu1': jnp.zeros((HID // 4,), dtype=jnp.float32), 'Wu2': jax.random.normal(ks[8], (1, HID // 4), dtype=jnp.float32) * 0.01, 'bu2': jnp.zeros((1,), dtype=jnp.float32), 'gate_w1': jnp.float32(0.5), 'gate_bias': jnp.float32(-1.0), 'log_rel': jnp.zeros((NSLOT,), dtype=jnp.float32)}
    _L0_ffn_all = _L0_ffn_setup()
    _L0_ffn_in = {k: v for k, v in _L0_ffn_all.items() if k in ('Wq', 'Wr', 'aux_keys', 'aux_values', 'Wvd', 'Wvu', 'Wu1', 'bu1', 'Wu2', 'bu2', 'gate_w1', 'gate_bias', 'log_rel')}
    del _L0_ffn_all

    def _L1_xattn_setup():
        import jax, jax.numpy as jnp
        import numpy as np
        DIM = 1024
        NUM_HEADS = 32
        NUM_KV_HEADS = 8
        HEAD_DIM = DIM // NUM_HEADS
        KV_DIM = DIM // (NUM_HEADS // NUM_KV_HEADS)
        B, S = (1, 512)
        key = jax.random.key(seed)
        ks = jax.random.split(key, 7)
        w_scale = DIM ** (-0.5)
        return {'query': jax.random.normal(ks[0], (B, S, DIM), jnp.float32), 'key': jax.random.normal(ks[1], (B, S, DIM), jnp.float32), 'value': jax.random.normal(ks[2], (B, S, DIM), jnp.float32), 'Wq': jax.random.normal(ks[3], (DIM, DIM), jnp.float32) * w_scale, 'Wk': jax.random.normal(ks[4], (DIM, KV_DIM), jnp.float32) * w_scale, 'Wv': jax.random.normal(ks[5], (DIM, KV_DIM), jnp.float32) * w_scale, 'Wo': jax.random.normal(ks[6], (DIM, DIM), jnp.float32) * w_scale}
    _L1_xattn_all = _L1_xattn_setup()
    _L1_xattn_in = {k: v for k, v in _L1_xattn_all.items() if k in ('Wq', 'Wk', 'Wv', 'Wo')}
    del _L1_xattn_all

    def _L1_ffn_setup():
        import jax, jax.numpy as jnp
        import numpy as np
        D_IN, D_OUT = (1024, 1024)
        B, S = (2, 512)
        key = jax.random.key(seed)
        kx, kw = jax.random.split(key)
        x = jax.random.normal(kx, (B, S, D_IN), dtype=jnp.float32)
        w = jax.random.normal(kw, (D_IN, D_OUT), dtype=jnp.float32)
        sign = jnp.where(w >= 0, 1.0, -1.0).astype(jnp.float32)
        scale = jnp.abs(w).mean().astype(jnp.float32)
        return {'x': x, 'sign': sign, 'scale': scale}
    _L1_ffn_all = _L1_ffn_setup()
    _L1_ffn_in = {k: v for k, v in _L1_ffn_all.items() if k in ('sign', 'scale')}
    del _L1_ffn_all
    return {'x': x, 'ctx_4096': ctx_4096, 'L0_xattn_Wq': _L0_xattn_in['Wq'], 'L0_xattn_Wk': _L0_xattn_in['Wk'], 'L0_xattn_Wv': _L0_xattn_in['Wv'], 'L0_xattn_Wo': _L0_xattn_in['Wo'], 'L0_xattn_bo': _L0_xattn_in['bo'], 'L0_xattn_g': _L0_xattn_in['g'], 'L0_ffn_Wq': _L0_ffn_in['Wq'], 'L0_ffn_Wr': _L0_ffn_in['Wr'], 'L0_ffn_aux_keys': _L0_ffn_in['aux_keys'], 'L0_ffn_aux_values': _L0_ffn_in['aux_values'], 'L0_ffn_Wvd': _L0_ffn_in['Wvd'], 'L0_ffn_Wvu': _L0_ffn_in['Wvu'], 'L0_ffn_Wu1': _L0_ffn_in['Wu1'], 'L0_ffn_bu1': _L0_ffn_in['bu1'], 'L0_ffn_Wu2': _L0_ffn_in['Wu2'], 'L0_ffn_bu2': _L0_ffn_in['bu2'], 'L0_ffn_gate_w1': _L0_ffn_in['gate_w1'], 'L0_ffn_gate_bias': _L0_ffn_in['gate_bias'], 'L0_ffn_log_rel': _L0_ffn_in['log_rel'], 'L1_xattn_Wq': _L1_xattn_in['Wq'], 'L1_xattn_Wk': _L1_xattn_in['Wk'], 'L1_xattn_Wv': _L1_xattn_in['Wv'], 'L1_xattn_Wo': _L1_xattn_in['Wo'], 'L1_ffn_sign': _L1_ffn_in['sign'], 'L1_ffn_scale': _L1_ffn_in['scale']}

def reference(x, ctx_4096, L0_xattn_Wq, L0_xattn_Wk, L0_xattn_Wv, L0_xattn_Wo, L0_xattn_bo, L0_xattn_g, L0_ffn_Wq, L0_ffn_Wr, L0_ffn_aux_keys, L0_ffn_aux_values, L0_ffn_Wvd, L0_ffn_Wvu, L0_ffn_Wu1, L0_ffn_bu1, L0_ffn_Wu2, L0_ffn_bu2, L0_ffn_gate_w1, L0_ffn_gate_bias, L0_ffn_log_rel, L1_xattn_Wq, L1_xattn_Wk, L1_xattn_Wv, L1_xattn_Wo, L1_ffn_sign, L1_ffn_scale):
    import jax
    import jax.numpy as jnp

    def _L0_xattn_ref(q, k, v, Wq, Wk, Wv, Wo, bo, g):
        import jax, jax.numpy as jnp
        import numpy as np
        DIM = 128
        HEADS = 8
        DIM_HEAD = 64
        HIDDEN = HEADS * DIM_HEAD
        SCALE = DIM_HEAD ** (-0.5)
        b = q.shape[0]
        qh = jnp.einsum('bcn,oc->bon', q, Wq).reshape(b, HEADS, DIM_HEAD, -1)
        kh = jnp.einsum('bcn,oc->bon', k, Wk).reshape(b, HEADS, DIM_HEAD, -1)
        vh = jnp.einsum('bcn,oc->bon', v, Wv).reshape(b, HEADS, DIM_HEAD, -1)
        qh = jax.nn.softmax(qh, axis=-2) * SCALE
        kh = jax.nn.softmax(kh, axis=-1)
        context = jnp.einsum('bhdn,bhen->bhde', kh, vh)
        out = jnp.einsum('bhde,bhdn->bhen', context, qh)
        out = out.reshape(b, HIDDEN, -1)
        out = jnp.einsum('bcn,oc->bon', out, Wo) + bo[None, :, None]
        norm = jnp.maximum(jnp.sqrt(jnp.sum(out * out, axis=1, keepdims=True)), 1e-12)
        return out / norm * g * np.sqrt(DIM)

    def _L0_ffn_ref(hidden_states, Wq, Wr, aux_keys, aux_values, Wvd, Wvu, Wu1, bu1, Wu2, bu2, gate_w1, gate_bias, log_rel):
        import jax, jax.numpy as jnp
        import numpy as np
        HID, BOT, RDIM, NSLOT, K, VB = (1024, 64, 48, 256, 8, 64)
        TAU_LOW, TAU_HIGH, EARLY_EXIT = (0.5, 2.0, 0.05)

        def _uncertainty(h, Wu1, bu1, Wu2, bu2):
            var = jnp.var(h, axis=-1)
            log_var = jnp.log1p(var)
            norm_var = log_var / (jnp.mean(log_var) + 1e-06)
            learned = (jax.nn.gelu(h @ Wu1.T + bu1) @ Wu2.T + bu2)[..., 0]
            return jnp.clip(norm_var * 0.5 + jax.nn.sigmoid(learned) * 2.5, 0.0, 5.0)
        query = hidden_states @ Wq.T
        rq = query @ Wr.T
        rk = aux_keys @ Wr.T
        router_scores = jnp.einsum('bsr,nr->bsn', rq, rk) / np.sqrt(RDIM) + log_rel
        top_scores, top_idx = jax.lax.top_k(router_scores, K)
        sel_keys = aux_keys[top_idx]
        attn = jnp.einsum('bsd,bskd->bsk', query, sel_keys) / np.sqrt(BOT) + log_rel[top_idx]
        w = jax.nn.softmax(attn, axis=-1)
        sel_vals = aux_values[top_idx]
        aux_out = jnp.einsum('bsk,bskh->bsh', w, sel_vals)
        aux_out = aux_out @ Wvd.T @ Wvu.T
        u = _uncertainty(hidden_states, Wu1, bu1, Wu2, bu2)
        u_norm = jnp.clip((u - TAU_LOW) / (TAU_HIGH - TAU_LOW), 0.0, 1.0)
        gate = jax.nn.sigmoid(gate_w1 * u_norm + gate_bias)
        gate = jnp.where(gate < EARLY_EXIT, 0.0, gate)
        return hidden_states + gate[..., None] * aux_out

    def _L1_xattn_ref(query, key, value, Wq, Wk, Wv, Wo):
        import jax, jax.numpy as jnp
        import numpy as np
        DIM = 1024
        NUM_HEADS = 32
        NUM_KV_HEADS = 8
        HEAD_DIM = DIM // NUM_HEADS
        KV_DIM = DIM // (NUM_HEADS // NUM_KV_HEADS)
        B, S = (1, 512)
        b, sq, _ = query.shape
        _, sk, _ = key.shape
        rep = NUM_HEADS // NUM_KV_HEADS
        q = (query @ Wq).reshape(b, sq, NUM_HEADS, HEAD_DIM).transpose(0, 2, 1, 3)
        k = (key @ Wk).reshape(b, sk, NUM_KV_HEADS, HEAD_DIM).transpose(0, 2, 1, 3)
        v = (value @ Wv).reshape(b, sk, NUM_KV_HEADS, HEAD_DIM).transpose(0, 2, 1, 3)
        k = jnp.repeat(k, rep, axis=1)
        v = jnp.repeat(v, rep, axis=1)
        scale = HEAD_DIM ** (-0.5)
        scores = jnp.einsum('bhqd,bhkd->bhqk', q, k) * scale
        probs = jax.nn.softmax(scores, axis=-1)
        out = jnp.einsum('bhqk,bhkd->bhqd', probs, v)
        out = out.transpose(0, 2, 1, 3).reshape(b, sq, DIM)
        return out @ Wo

    def _L1_ffn_ref(x, sign, scale):
        import jax, jax.numpy as jnp
        import numpy as np
        D_IN, D_OUT = (1024, 1024)
        B, S = (2, 512)
        s = jax.nn.softplus(scale)
        return jnp.einsum('bsi,io->bso', x, sign) * s
    x = x + _L0_xattn_ref(_layernorm(x, axis=-1), ctx_4096, ctx_4096, L0_xattn_Wq, L0_xattn_Wk, L0_xattn_Wv, L0_xattn_Wo, L0_xattn_bo, L0_xattn_g)
    x = x + _L0_ffn_ref(_layernorm(x, axis=-1), L0_ffn_Wq, L0_ffn_Wr, L0_ffn_aux_keys, L0_ffn_aux_values, L0_ffn_Wvd, L0_ffn_Wvu, L0_ffn_Wu1, L0_ffn_bu1, L0_ffn_Wu2, L0_ffn_bu2, L0_ffn_gate_w1, L0_ffn_gate_bias, L0_ffn_log_rel)
    x = x + _L1_xattn_ref(_layernorm(x, axis=-1), ctx_4096, ctx_4096, L1_xattn_Wq, L1_xattn_Wk, L1_xattn_Wv, L1_xattn_Wo)
    x = x + _L1_ffn_ref(_layernorm(x, axis=-1), L1_ffn_sign, L1_ffn_scale)
    return x

_drawn_inputs = setup_inputs


def setup_inputs(seed=0):
    import zlib

    import numpy as np

    out = dict(_drawn_inputs(seed))
    spreads = {'L0_xattn_g': (1.0, 0.2), 'L0_ffn_bu1': (0.0, 2.0), 'L0_ffn_log_rel': (0.0, 2.0)}
    factors = {'L0_ffn_Wq': 60.789,
     'L0_ffn_Wr': 64.0,
     'L0_ffn_aux_keys': 59.763,
     'L0_ffn_aux_values': 59.473,
     'L0_ffn_Wvd': 60.083,
     'L0_ffn_Wvu': 59.124,
     'L0_ffn_Wu1': 64.0,
     'L0_ffn_Wu2': 64.0,
     'L1_xattn_Wq': 3.556,
     'L1_xattn_Wk': 3.551}
    for name, (base, spread) in spreads.items():
        noise = np.random.default_rng([zlib.crc32(name.encode()), seed]).standard_normal(out[name].shape)
        drawn = base * np.exp(spread * noise) if base else spread * noise
        out[name] = jnp.asarray(drawn.astype(out[name].dtype))
    for name, factor in factors.items():
        out[name] = (out[name] * factor).astype(out[name].dtype)
    return out
```

```python
from contextlib import ExitStack

import concourse.bass as bass
from concourse import mybir

F32 = mybir.dt.float32
F32R = mybir.dt.float32r
ALU = mybir.AluOpType
ACT = mybir.ActivationFunctionType
AX = mybir.AxisListType

P = 128
B = 32
DM = 1024
KT = DM // P
HALF = 512
EPS = 1e-5
H0, D0 = 8, 64
HD0 = H0 * D0
T0 = HD0 // P
SLOTS, BOT, RDIM, UH = 256, 64, 48, 256
TOPK = 8
TAU_LOW, TAU_HIGH, EARLY_EXIT = 0.5, 2.0, 0.05
H1, KV1, D1 = 32, 8, 32
REP = H1 // KV1
KVD = KV1 * D1
UQ = UH + BOT
MASKED = 1e30
GELU_C = 0.7978845608028654
GELU_A = 0.044715


class Batch:

    def __init__(self, pair, odd):
        self.pair, self.odd = pair, odd

    def count(self, per_batch, k):
        return self.pair * (2 * per_batch) + (self.odd * per_batch + k)

    def before(self, n):
        at = self.odd - n
        return Batch(self.pair + (at // 2) if at // 2 else self.pair, at % 2)

    def after(self):
        return Batch(self.pair + 1, 0) if self.odd else Batch(self.pair, 1)

    @property
    def index(self):
        return self.pair * 2 + self.odd


class Signal:

    def __init__(self, sem, per_batch):
        self.sem, self.per_batch = sem, per_batch


class DmaSignal:

    def __init__(self, sems, per_batch):
        self.sems, self.per_batch = sems, per_batch


def need(eng, signal, batch, k):
    if isinstance(signal, DmaSignal):
        value = batch.pair * (16 * signal.per_batch) + 16 * k
        sem = signal.sems[batch.odd]
    else:
        value = batch.count(signal.per_batch, k)
        sem = signal.sem
    if isinstance(value, int) and value <= 0:
        return
    if isinstance(batch.pair, int) and batch.pair < 0:
        return
    eng.wait_ge(sem, value)


def product(nc, out, lhs, rhs, first, last):
    nc.tensor.matmul(out, lhs[0], rhs[0], start=first, stop=False)
    nc.tensor.matmul(out, lhs[0], rhs[1], start=False, stop=False)
    return nc.tensor.matmul(out, lhs[1], rhs[0], start=False, stop=last)


def make_identity(nc, eng, ident, made):
    nc.gpsimd.memset(ident[:, :], 0.0).then_inc(made, 1)
    eng.wait_ge(made, 1)
    nc.gpsimd.affine_select(out=ident[:, :], in_=ident[:, :], compare_op=ALU.not_equal, fill=1.0, base=0,
                            pattern=[[-1, P]], channel_multiplier=1).then_inc(made, 1)


def rows_of(ap, n):
    return ap.partition_broadcast(n)


def layer0_attention(nc, sems, x, ctx_in, w, keep, x1_dram, kv_dram):
    with ExitStack() as ctx:
        def sb(name, shape, dt=F32):
            return ctx.enter_context(nc.sbuf_tensor(f"a_{name}", shape, dt))

        def sem(name):
            return sems.new(nc.semaphore(f"a_{name}"))

        def signal(name, n):
            return Signal(sem(name), n)

        def dma_signal(name, n=1):
            return DmaSignal([sem(f"{name}_{p}") for p in "eo"], n)

        def both(name, shape):
            return sb(f"{name}_hi", shape, F32R), sb(f"{name}_lo", shape, F32R)

        bank = [ctx.enter_context(nc.psum_tensor(f"a_ps{i}", [P, HALF], F32)) for i in range(8)]

        ident = sb("ident", [P, P])
        ones = sb("ones", [P, P])
        w_rows = sb("w_rows", [P, 4, T0, P])
        wqT = both("wqT", [P, HD0])
        wkT = both("wkT", [P, HD0])
        woT = sb("woT", [P, T0, P])
        vo = sb("vo", [P, H0, P])
        wkv_raw = sb("wkv_raw", [P, KT, 2 * KVD])
        wkv = both("wkv", [P, KT, 2 * KVD])
        bo = sb("bo", [P, 1])
        g = sb("g", [P, 1])
        g_scaled = sb("g_scaled", [P, 1])
        minus_half = sb("minus_half", [P, KT])
        consts = sb("consts", [P, 2])
        carrier = sb("carrier", [P, 1])

        x_sb = [sb(f"x{p}", [P, DM]) for p in range(2)]
        ctx_sb = [sb(f"ctx{p}", [P, DM]) for p in range(2)]
        ctx_hl = both("ctx_hl", [P, DM])
        ctxT = sb("ctxT", [P, KT, P])
        ctxT_hl = both("ctxT_hl", [P, KT, P])
        xn = sb("xn", [P, DM])
        xn_hl = both("xn_hl", [P, DM])
        ln_stats = sb("ln_stats", [P, 2, 6])
        ln_mv = sb("ln_mv", [P, 2])
        ln_ve = sb("ln_ve", [P, 1])
        ln_r = sb("ln_r", [P, 1])
        ln_nmr = sb("ln_nmr", [P, 1])
        k_two = sb("k_two", [P, 2 * T0])
        k_half = [sb(f"k_half{p}", [P, 2, T0]) for p in range(2)]
        x1_mv = [sb(f"x1_mv{p}", [P, 2]) for p in range(2)]
        k_neg = sb("k_neg", [P, T0])
        k_sum = [sb(f"k_sum{p}", [P, T0]) for p in range(2)]
        k_inv = sb("k_inv", [P, T0])
        k_exp = sb("k_exp", [P, T0, DM])
        k_expT = [sb(f"k_expT{r}", [P, HD0]) for r in range(2)]
        kv_sb = [sb(f"kv{p}", [P, 2 * KVD]) for p in range(2)]
        q_max = [sb(f"q_max{r}", [P, H0]) for r in range(2)]
        q_sm = [sb(f"q_sm{r}", [P, HD0]) for r in range(3)]
        q_sum = [sb(f"q_sum{r}", [P, H0]) for r in range(2)]
        q_inv = [sb(f"q_inv{r}", [P, H0]) for r in range(2)]
        q_T = sb("q_T", [P, T0, DM])
        c_sb = sb("c_sb", [P, HD0])
        mix = sb("mix", [P, T0, P])
        o_sb = sb("o_sb", [P, DM])
        sq = sb("sq", [P, DM])
        n_max = sb("n_max", [P, KT])
        n_inv = sb("n_inv", [P, KT])
        n_diag = sb("n_diag", [P, KT, P])
        x1_sb = [sb(f"x1_{p}", [P, DM]) for p in range(2)]
        x1_stats = sb("x1_stats", [P, 2, 6])

        s_load = sem("weights_loaded")
        s_ident = sem("ident_made")
        s_const = sem("constants_made")
        s_wT = sem("weights_transposed")
        s_wev = sem("weights_copied")
        s_whi = sem("weights_high")
        s_wlo = sem("weights_low")
        s_vo = sem("vo_made")

        x_in = dma_signal("x_in")
        ctx_read = dma_signal("ctx_in")
        x1_out = dma_signal("x1_out")
        kv_out = dma_signal("kv_out")
        ln_step = signal("ln_step", 3)
        ln_rs = signal("ln_rs", 3)
        ln_nm = signal("ln_nm", 1)
        xn_made = signal("xn_made", 2)
        xn_low = signal("xn_low", 1)
        ctx_high = signal("ctx_high", 1)
        ctx_low = signal("ctx_low", 1)
        ctx_turned = signal("ctx_turned", 2)
        ctxT_copied = signal("ctxT_copied", 2)
        ctxT_split = signal("ctxT_split", 2)
        k_ready = signal("k_ready", T0)
        k_maxed = signal("k_maxed", T0)
        k_negated = signal("k_negated", T0)
        k_exped = signal("k_exped", T0)
        kv_ready = signal("kv_ready", 1)
        kv_copied = signal("kv_copied", 1)
        q_ready = signal("q_ready", KT)
        q_maxed = signal("q_maxed", KT)
        q_less = signal("q_less", KT)
        q_exped = signal("q_exped", KT)
        q_summed = signal("q_summed", KT)
        q_inverted = signal("q_inverted", KT)
        q_normed = signal("q_normed", KT)
        q_turned = signal("q_turned", KT)
        q_stored = signal("q_stored", KT)
        kx_turned = signal("kx_turned", KT)
        kx_stored = signal("kx_stored", KT)
        c_step = signal("c_step", KT)
        c_copied = signal("c_copied", 1)
        k_inverted = signal("k_inverted", 2)
        mix_ready = signal("mix_ready", 1)
        mix_scaled = signal("mix_scaled", 1)
        o_ready = signal("o_ready", 2)
        o_biased = signal("o_biased", 2)
        o_squared = signal("o_squared", 2)
        n_ready = signal("n_ready", 1)
        n_floored = signal("n_floored", 1)
        n_powed = signal("n_powed", 1)
        n_placed = signal("n_placed", 1)
        n_spread = signal("n_spread", 2)
        o_normed = signal("o_normed", 2)
        x1_added = signal("x1_added", 1)
        x1_seen = signal("x1_seen", 3)

        block = ctx.enter_context(nc.Block())

        def schedule(steps, head):
            def run(eng):
                head(eng, Batch(0, 0))
                steps(eng, 0, False)
                with eng.Fori(1, B // 2 - 1) as pair:
                    steps(eng, pair, False)
                steps(eng, B // 2 - 1, True)
            return run

        def two_batches(front, middle, back):
            def steps(eng, pair, last):
                even, odd = Batch(pair, 0), Batch(pair, 1)
                middle(eng, even)
                front(eng, odd)
                back(eng, even)
                middle(eng, odd)
                if not last:
                    front(eng, odd.after())
                back(eng, odd)
            return steps

        @block.sync
        def _(sp):
            for n, name in enumerate(("L0_xattn_Wq", "L0_xattn_Wk", "L0_xattn_Wv")):
                sp.dma_start(w_rows[:, n], w[name].rearrange("(t p) c -> p t c", p=P)).then_inc(s_load, 16)
            sp.dma_start(w_rows[:, 3], w["L0_xattn_Wo"].rearrange("o (t e) -> o t e", e=P)).then_inc(s_load, 16)
            sp.dma_start(wkv_raw[:, :, 0:KVD], w["L1_xattn_Wk"].rearrange("(t p) m -> p t m", p=P)).then_inc(s_load, 16)
            sp.dma_start(wkv_raw[:, :, KVD:2 * KVD], w["L1_xattn_Wv"].rearrange("(t p) m -> p t m", p=P)).then_inc(s_load, 16)
            sp.dma_start(bo[:, :], w["L0_xattn_bo"].rearrange("(p a) -> p a", a=1)).then_inc(s_load, 16)
            sp.dma_start(g[:, :], w["L0_xattn_g"].rearrange("a p b -> p (a b)")).then_inc(s_load, 16)

            def load(i):
                need(sp, x1_added, i.before(2), 1)
                sp.dma_start(x_sb[i.odd][:, :], x[i.index]).then_inc(x_in.sems[i.odd], 16)
                need(sp, ctx_low, i.before(2), 1)
                need(sp, ctx_turned, i.before(2), 2)
                sp.dma_start(ctx_sb[i.odd][:, :], ctx_in[i.index]).then_inc(ctx_read.sems[i.odd], 16)

            def store_kv(i):
                need(sp, kv_copied, i, 1)
                sp.dma_start(kv_dram[i.index], kv_sb[i.odd][:, :]).then_inc(kv_out.sems[i.odd], 16)

            def store_x1(i):
                need(sp, x1_added, i, 1)
                sp.dma_start(x1_dram[i.index], x1_sb[i.odd][:, :]).then_inc(x1_out.sems[i.odd], 16)

            def turn(pair, first, last):
                even, odd = Batch(pair, 0), Batch(pair, 1)
                load(odd)
                store_kv(even)
                if not last:
                    load(odd.after())
                store_x1(even)
                store_kv(odd)
                store_x1(odd)

            load(Batch(0, 0))
            turn(0, True, False)
            with sp.Fori(1, B // 2 - 1) as pair:
                turn(pair, False, False)
            turn(B // 2 - 1, False, True)
            for p in range(2):
                sp.wait_ge(x1_out.sems[p], 16 * (B // 2))
                sp.wait_ge(kv_out.sems[p], 16 * (B // 2))

        @block.gpsimd
        def _(pool):
            make_identity(nc, pool, ident, s_ident)
            nc.gpsimd.memset(ones[:, :], 1.0).then_inc(s_const, 1)
            nc.gpsimd.memset(minus_half[:, :], -0.5).then_inc(s_const, 1)
            nc.gpsimd.memset(consts[:, 0:1], EPS).then_inc(s_const, 1)
            nc.gpsimd.memset(consts[:, 1:2], -1.0).then_inc(s_const, 1)
            pool.wait_ge(s_load, 16 * 8)
            nc.gpsimd.tensor_scalar(g_scaled[:, :], g[:, :], float(P) ** 0.5, None, ALU.mult).then_inc(s_const, 1)
            pool.wait_ge(s_const, 5)

            def front(eng, i):
                need(pool, ln_step, i, 3)
                need(pool, xn_made, i.before(1), 2)
                nc.gpsimd.tensor_tensor(ln_ve[:, :], ln_mv[:, 1:2], consts[:, 0:1], ALU.add).then_inc(ln_rs.sem, 1)
                need(pool, ln_rs, i, 1)
                nc.gpsimd.tensor_tensor(ln_r[:, :], ln_ve[:, :], minus_half[:, 0:1], ALU.pow).then_inc(ln_rs.sem, 1)
                need(pool, ln_rs, i, 2)
                nc.gpsimd.tensor_tensor(ln_nmr[:, :], ln_mv[:, 0:1], consts[:, 1:2], ALU.mult).then_inc(ln_rs.sem, 1)
                need(pool, ln_rs, i, 3)
                nc.gpsimd.tensor_tensor(ln_nmr[:, :], ln_nmr[:, :], ln_r[:, :], ALU.mult).then_inc(ln_nm.sem, 1)
                need(pool, ctx_high, i, 1)
                need(pool, k_ready, i.before(1), T0)
                nc.gpsimd.tensor_tensor(ctx_hl[1][:, :], ctx_sb[i.odd][:, :], ctx_hl[0][:, :].bitcast(F32),
                                        ALU.subtract).then_inc(ctx_low.sem, 1)
                need(pool, xn_made, i, 2)
                need(pool, q_ready, i.before(1), KT)
                nc.gpsimd.tensor_tensor(xn_hl[1][:, :], xn[:, :], xn_hl[0][:, :].bitcast(F32),
                                        ALU.subtract).then_inc(xn_low.sem, 1)

            def middle(eng, i):
                pass

            def back(eng, i):
                need(pool, n_floored, i, 1)
                nc.gpsimd.tensor_tensor(n_inv[:, :], n_max[:, :], minus_half[:, :], ALU.pow).then_inc(n_powed.sem, 1)

            schedule(two_batches(front, middle, back), front)(pool)

        @block.tensor
        def _(pe):
            pe.wait_ge(s_load, 16 * 8)
            pe.wait_ge(s_ident, 2)
            for n, at in ((0, 0), (1, 1), (3, 2)):
                for t in range(T0):
                    mm = nc.tensor.transpose(bank[at][:, t * P:(t + 1) * P], w_rows[:, n, t], ident[:, :])
                mm.then_inc(s_wT, 1)
            pe.wait_ge(s_wev, 1)
            for h in range(H0):
                lo = D0 * (h % 2)
                mm = nc.tensor.matmul(bank[4 + h % 2][:, (h // 2) * P:(h // 2 + 1) * P], w_rows[lo:lo + D0, 2, h // 2],
                                      woT[lo:lo + D0, h // 2], start=True, stop=True)
            mm.then_inc(s_wT, 1)
            pe.wait_ge(s_whi, 3)
            pe.wait_ge(s_wlo, 3)
            pe.wait_ge(s_vo, 2)

            def front(eng, i):
                need(pe, ctx_read, i, 1)
                need(pe, q_less, i.before(1), KT)
                for j in range(KT):
                    mm = nc.tensor.transpose(bank[j // 4][:, (j % 4) * P:(j % 4 + 1) * P],
                                             ctx_sb[i.odd][:, j * P:(j + 1) * P], ident[:, :])
                    if j % 4 == 3:
                        mm.then_inc(ctx_turned.sem, 1)
                need(pe, ctx_low, i, 1)
                need(pe, kx_stored, i.before(1), KT)
                for t in range(T0):
                    pair = 2 - 2 * (t % 2)
                    if t == 1:
                        need(pe, ctxT_copied, i, 2)
                    if t >= 2:
                        need(pe, k_exped, i, t - 1)
                    for half in range(2):
                        cols = slice(half * HALF, (half + 1) * HALF)
                        mm = product(nc, bank[pair + half][:, :], [m[:, t * P:(t + 1) * P] for m in wkT],
                                     [m[:, cols] for m in ctx_hl], True, True)
                    mm.then_inc(k_ready.sem, 1)
                    if t == 0:
                        need(pe, ctxT_split, i, 2)
                        need(pe, o_normed, i.before(2), 2)
                    for j in range(2 * t, 2 * t + 2):
                        mm = product(nc, bank[5][:, :], [m[:, j] for m in ctxT_hl], [m[:, j] for m in wkv],
                                     j == 0, j == KT - 1)
                mm.then_inc(kv_ready.sem, 1)

            def middle(eng, i):
                need(pe, xn_low, i, 1)
                for j in range(KT + 2):
                    if j < KT:
                        if j < 2:
                            need(pe, k_exped, i, T0)
                        else:
                            need(pe, q_less, i, j - 1)
                        mm = product(nc, bank[j % 2][:, :], [m[:, j * P:(j + 1) * P] for m in xn_hl],
                                     [m[:, :] for m in wqT], True, True)
                        mm.then_inc(q_ready.sem, 1)
                        if j >= 2:
                            need(pe, kx_stored, i, j - 1)
                        for t in range(T0):
                            mm = nc.tensor.transpose(bank[2 + j % 2][:, t * P:(t + 1) * P],
                                                     k_exp[:, t, j * P:(j + 1) * P], ident[:, :])
                        mm.then_inc(kx_turned.sem, 1)
                    if 1 <= j <= KT:
                        m = j - 1
                        need(pe, kx_stored, i, m + 1)
                        if m == 0:
                            need(pe, o_normed, i.before(1), 1)
                        nc.tensor.matmul(bank[4][:, :], ctxT[:, m], k_expT[m % 2][:, :], start=(m == 0),
                                         stop=(m == KT - 1)).then_inc(c_step.sem, 1)
                    if j >= 2:
                        m = j - 2
                        need(pe, q_normed, i, m + 1)
                        if m < 2:
                            need(pe, o_squared, i.before(1), 2)
                        else:
                            need(pe, q_stored, i, m - 1)
                        for t in range(T0):
                            mm = nc.tensor.transpose(bank[6 + m % 2][:, t * P:(t + 1) * P],
                                                     q_sm[m % 3][:, t * P:(t + 1) * P], ident[:, :])
                        mm.then_inc(q_turned.sem, 1)

            def back(eng, i):
                need(pe, c_copied, i, 1)
                for h in range(H0):
                    lo = D0 * (h % 2)
                    mm = nc.tensor.matmul(bank[4][lo:lo + D0, (h // 2) * P:(h // 2 + 1) * P],
                                          c_sb[:, h * D0:(h + 1) * D0], vo[:, h], start=True, stop=True)
                mm.then_inc(mix_ready.sem, 1)
                need(pe, q_stored, i, KT)
                need(pe, mix_scaled, i, 1)
                for half in range(2):
                    cols = slice(half * HALF, (half + 1) * HALF)
                    for t in range(T0):
                        mm = nc.tensor.matmul(bank[6 + half][:, :], mix[:, t], q_T[:, t, cols], start=(t == 0),
                                              stop=(t == T0 - 1))
                    mm.then_inc(o_ready.sem, 1)
                need(pe, o_squared, i, 2)
                for j in range(KT):
                    mm = nc.tensor.matmul(bank[4][:, j:j + 1], sq[:, j * P:(j + 1) * P], ones[:, 0:1], start=True, stop=True)
                mm.then_inc(n_ready.sem, 1)
                need(pe, n_placed, i, 1)
                last_kv = i.after() if not (isinstance(i.pair, int) and i.pair == B // 2 - 1 and i.odd) else i
                need(pe, kv_copied, last_kv, 1)
                for half in range(2):
                    nc.tensor.matmul(bank[4 + half][:, :], ones[:, :], n_diag[:, 4 * half:4 * half + 4].rearrange("p a b -> p (a b)"),
                                     start=True, stop=True).then_inc(n_spread.sem, 1)

            schedule(two_batches(front, middle, back), front)(pe)

        @block.scalar
        def _(act):
            act.wait_ge(s_load, 16 * 8)
            act.wait_ge(s_wT, 1)
            nc.scalar.copy(wqT[0][:, :], bank[0][:, :]).then_inc(s_whi, 1)
            act.wait_ge(s_wT, 2)
            nc.scalar.copy(wkT[0][:, :], bank[1][:, :]).then_inc(s_whi, 1)
            act.wait_ge(s_wT, 3)
            nc.scalar.copy(woT[:, :, :].rearrange("p t o -> p (t o)"), bank[2][:, :]).then_inc(s_wev, 1)
            nc.scalar.copy(wkv[0][:, :, :], wkv_raw[:, :, :]).then_inc(s_whi, 1)
            act.wait_ge(s_wT, 4)
            for n in range(2):
                nc.scalar.copy(vo[:, n::2], bank[4 + n][:, :].rearrange("p (h o) -> p h o", o=P)).then_inc(s_vo, 1)

            def front(eng, i):
                need(act, ctx_read, i, 1)
                need(act, k_ready, i.before(1), T0)
                nc.scalar.copy(ctx_hl[0][:, :], ctx_sb[i.odd][:, :]).then_inc(ctx_high.sem, 1)
                need(act, c_step, i.before(1), KT)
                need(act, ctxT_split, i.before(1), 2)
                for half in range(2):
                    need(act, ctx_turned, i, half + 1)
                    nc.scalar.copy(ctxT[:, 4 * half:4 * half + 4].rearrange("p a b -> p (a b)"),
                                   bank[half][:, :]).then_inc(ctxT_copied.sem, 1)
                need(act, ln_nm, i, 1)
                need(act, x_in, i, 1)
                need(act, xn_low, i.before(1), 1)
                nc.scalar.activation(xn[:, :], x_sb[i.odd][:, :], ACT.Identity, bias=ln_nmr[:, :],
                                     scale=ln_r[:, :]).then_inc(xn_made.sem, 1)
                need(act, q_ready, i.before(1), KT)
                nc.scalar.activation(xn_hl[0][:, :], x_sb[i.odd][:, :], ACT.Identity, bias=ln_nmr[:, :],
                                     scale=ln_r[:, :]).then_inc(xn_made.sem, 1)
                need(act, kx_turned, i.before(1), KT)
                for t in range(T0):
                    pair = 2 - 2 * (t % 2)
                    need(act, k_negated, i, t + 1)
                    if t == 0:
                        need(act, k_inverted, i.before(2), 2)
                    nc.scalar.activation(k_exp[:, t, 0:HALF], bank[pair][:, :], ACT.Exp, bias=k_neg[:, t:t + 1],
                                         accum_out=k_half[i.odd][:, 0, t:t + 1])
                    nc.scalar.activation(k_exp[:, t, HALF:DM], bank[pair + 1][:, :], ACT.Exp, bias=k_neg[:, t:t + 1],
                                         accum_out=k_half[i.odd][:, 1, t:t + 1]).then_inc(k_exped.sem, 1)
                need(act, kv_ready, i, 1)
                need(act, kv_out, i.before(2), 1)
                nc.scalar.copy(kv_sb[i.odd][:, :], bank[5][:, :]).then_inc(kv_copied.sem, 1)

            def middle(eng, i):
                for j in range(KT + 2):
                    if j < KT:
                        need(act, kx_turned, i, j + 1)
                        if j < 2:
                            need(act, c_step, i.before(1), KT)
                        else:
                            need(act, c_step, i, j - 1)
                        nc.scalar.copy(k_expT[j % 2][:, :], bank[2 + j % 2][:, :]).then_inc(kx_stored.sem, 1)
                        need(act, q_less, i, j + 1)
                        nc.scalar.activation(q_sm[j % 3][:, :], q_sm[j % 3][:, :], ACT.Exp).then_inc(q_exped.sem, 1)
                    if j >= 2:
                        m = j - 2
                        need(act, q_turned, i, m + 1)
                        if m == 0:
                            need(act, o_ready, i.before(1), 2)
                        nc.scalar.copy(q_T[:, :, m * P:(m + 1) * P],
                                       bank[6 + m % 2][:, :].rearrange("p (t n) -> p t n", t=T0)).then_inc(q_stored.sem, 1)

            def back(eng, i):
                need(act, c_step, i, KT)
                need(act, mix_ready, i.before(1), 1)
                nc.scalar.copy(c_sb[:, :], bank[4][:, :]).then_inc(c_copied.sem, 1)
                for half in range(2):
                    cols = slice(half * HALF, (half + 1) * HALF)
                    need(act, o_ready, i, half + 1)
                    if half == 0:
                        need(act, x1_added, i.before(1), 1)
                        need(act, n_ready, i.before(1), 1)
                    nc.scalar.activation(o_sb[:, cols], bank[6 + half][:, :], ACT.Identity, bias=bo[:, :]).then_inc(o_biased.sem, 1)
                    nc.scalar.activation(sq[:, cols], bank[6 + half][:, :], ACT.Square, bias=bo[:, :]).then_inc(o_squared.sem, 1)

            schedule(two_batches(front, middle, back), front)(act)

        @block.vector
        def _(dve):
            dve.wait_ge(s_whi, 1)
            nc.vector.tensor_tensor(wqT[1][:, :], bank[0][:, :], wqT[0][:, :].bitcast(F32), ALU.subtract).then_inc(s_wlo, 1)
            dve.wait_ge(s_whi, 2)
            nc.vector.tensor_tensor(wkT[1][:, :], bank[1][:, :], wkT[0][:, :].bitcast(F32), ALU.subtract).then_inc(s_wlo, 1)
            dve.wait_ge(s_whi, 3)
            nc.vector.tensor_tensor(wkv[1][:, :, :], wkv_raw[:, :, :], wkv[0][:, :, :].bitcast(F32), ALU.subtract).then_inc(s_wlo, 1)
            dve.wait_ge(s_const, 5)

            def front(eng, i):
                need(dve, x_in, i, 1)
                need(dve, ln_nm, i.before(1), 1)
                for half in range(2):
                    nc.vector.bn_stats(ln_stats[:, half], x_sb[i.odd][:, half * HALF:(half + 1) * HALF]).then_inc(ln_step.sem, 1)
                need(dve, ln_step, i, 2)
                nc.vector.memset(carrier[:, :], 0.0)
                nc.vector.bn_aggr(ln_mv[:, :], ln_stats[:, :, :]).then_inc(ln_step.sem, 1)
                need(dve, ctxT_copied, i, 2)
                need(dve, kv_ready, i.before(1), 1)
                nc.vector.tensor_copy(ctxT_hl[0][:, :, :], ctxT[:, :, :]).then_inc(ctxT_split.sem, 1)
                need(dve, ctxT_split, i, 1)
                nc.vector.tensor_tensor(ctxT_hl[1][:, :, :], ctxT[:, :, :], ctxT_hl[0][:, :, :].bitcast(F32),
                                        ALU.subtract).then_inc(ctxT_split.sem, 1)
                for t in range(T0):
                    pair = 2 - 2 * (t % 2)
                    need(dve, k_ready, i, t + 1)
                    need(dve, k_exped, i.before(1), t + 1)
                    nc.vector.tensor_reduce(k_two[:, 2 * t:2 * t + 1], bank[pair][:, :], AX.X, ALU.max)
                    nc.vector.tensor_reduce(k_two[:, 2 * t + 1:2 * t + 2], bank[pair + 1][:, :], AX.X, ALU.max).then_inc(k_maxed.sem, 1)
                    need(dve, k_maxed, i, t + 1)
                    nc.vector.tensor_scalar(k_neg[:, t:t + 1], k_two[:, 2 * t:2 * t + 1], k_two[:, 2 * t + 1:2 * t + 2],
                                            -1.0, ALU.max, ALU.mult).then_inc(k_negated.sem, 1)

            def middle(eng, i):
                for j in range(KT + 1):
                    if j < KT:
                        need(dve, q_ready, i, j + 1)
                        qv = bank[j % 2][:, :].rearrange("p (h d) -> p h d", d=D0)
                        nc.vector.tensor_reduce(q_max[j % 2][:, :], qv, AX.X, ALU.max).then_inc(q_maxed.sem, 1)
                        need(dve, q_maxed, i, j + 1)
                        if j < 3:
                            need(dve, q_turned, i.before(1), KT)
                        else:
                            need(dve, q_turned, i, j - 2)
                        nc.vector.tensor_tensor(q_sm[j % 3][:, :].rearrange("p (h d) -> p h d", d=D0), qv,
                                                q_max[j % 2][:, :].unsqueeze(2).to_broadcast([P, H0, D0]),
                                                ALU.subtract).then_inc(q_less.sem, 1)
                    if j >= 1:
                        m = j - 1
                        sm = q_sm[m % 3][:, :].rearrange("p (h d) -> p h d", d=D0)
                        need(dve, q_exped, i, m + 1)
                        nc.vector.tensor_reduce(q_sum[m % 2][:, :], sm, AX.X, ALU.add).then_inc(q_summed.sem, 1)
                        need(dve, q_summed, i, m + 1)
                        nc.vector.reciprocal(q_inv[m % 2][:, :], q_sum[m % 2][:, :]).then_inc(q_inverted.sem, 1)
                        need(dve, q_inverted, i, m + 1)
                        nc.vector.tensor_tensor(sm, sm, q_inv[m % 2][:, :].unsqueeze(2).to_broadcast([P, H0, D0]),
                                                ALU.mult).then_inc(q_normed.sem, 1)
                need(dve, k_exped, i, T0)
                nc.vector.tensor_tensor(k_sum[i.odd][:, :], k_half[i.odd][:, 0], k_half[i.odd][:, 1], ALU.add).then_inc(k_inverted.sem, 1)
                need(dve, k_inverted, i, 1)
                need(dve, mix_scaled, i.before(1), 1)
                nc.vector.reciprocal(k_inv[:, :], k_sum[i.odd][:, :]).then_inc(k_inverted.sem, 1)

            def back(eng, i):
                need(dve, mix_ready, i, 1)
                need(dve, k_inverted, i, 2)
                need(dve, o_ready, i.before(1), 2)
                for t in range(T0):
                    op = nc.vector.tensor_scalar(mix[:, t], bank[4][:, t * P:(t + 1) * P], k_inv[:, t:t + 1],
                                                 float(D0) ** -0.5, ALU.mult, ALU.mult)
                op.then_inc(mix_scaled.sem, 1)
                need(dve, n_ready, i, 1)
                nc.vector.tensor_scalar(n_max[:, :], bank[4][:, 0:KT], 1e-24, None, ALU.max).then_inc(n_floored.sem, 1)
                need(dve, n_powed, i, 1)
                need(dve, n_spread, i.before(1), 2)
                nc.vector.tensor_tensor(n_diag[:, :, :], ident[:, :].unsqueeze(1).to_broadcast([P, KT, P]),
                                        n_inv[:, :].unsqueeze(2).to_broadcast([P, KT, P]), ALU.mult).then_inc(n_placed.sem, 1)
                for half in range(2):
                    cols = slice(half * HALF, (half + 1) * HALF)
                    need(dve, n_spread, i, half + 1)
                    need(dve, o_biased, i, half + 1)
                    nc.vector.scalar_tensor_tensor(o_sb[:, cols], o_sb[:, cols], g_scaled[:, :], bank[4 + half][:, :],
                                                   ALU.mult, ALU.mult).then_inc(o_normed.sem, 1)
                need(dve, o_normed, i, 2)
                need(dve, x1_out, i.before(2), 1)
                nc.vector.tensor_tensor(x1_sb[i.odd][:, :], x_sb[i.odd][:, :], o_sb[:, :], ALU.add).then_inc(x1_added.sem, 1)
                need(dve, x1_added, i, 1)
                for half in range(2):
                    nc.vector.bn_stats(x1_stats[:, half], x1_sb[i.odd][:, half * HALF:(half + 1) * HALF]).then_inc(x1_seen.sem, 1)
                need(dve, x1_seen, i, 2)
                nc.vector.memset(carrier[:, :], 0.0)
                nc.vector.bn_aggr(x1_mv[i.odd][:, :], x1_stats[:, :, :]).then_inc(x1_seen.sem, 1)
                need(dve, x1_seen, i, 3)
                nc.vector.tensor_copy(keep[:, i_slice(i), :], x1_mv[i.odd][:, :].unsqueeze(1))

            def i_slice(i):
                return bass.ds(i.index, 1) if not isinstance(i.pair, int) else slice(i.index, i.index + 1)

            schedule(two_batches(front, middle, back), front)(dve)


def between_layers(nc, sems, keep, rows, w):
    with ExitStack() as ctx:
        def sb(name, shape, dt=F32):
            return ctx.enter_context(nc.sbuf_tensor(f"m_{name}", shape, dt))

        def sem(name):
            return sems.new(nc.semaphore(f"m_{name}"))

        total = ctx.enter_context(nc.psum_tensor("m_total", [P, 1], F32))
        var_eps = sb("var_eps", [P, B])
        minus_half = sb("minus_half", [P, B])
        inv_var = sb("inv_var", [P, B])
        var_n = sb("var_n", [P, B])
        log_var = sb("log_var", [P, B])
        log_sum = sb("log_sum", [P, 1])
        mean_n = sb("mean_n", [P, 1])
        inv_mean = sb("inv_mean", [P, 1])
        ones = sb("ones", [P, P])
        s_pool, s_dve, s_act, s_pe = sem("pool"), sem("dve"), sem("act"), sem("pe")
        block = ctx.enter_context(nc.Block())

        @block.gpsimd
        def _(pool):
            nc.gpsimd.memset(minus_half[:, :], -0.5).then_inc(s_pool, 1)
            nc.gpsimd.memset(ones[:, :], 1.0).then_inc(s_pool, 1)
            pool.wait_ge(s_pool, 2)
            pool.wait_ge(s_dve, 1)
            nc.gpsimd.tensor_tensor(rows[:, :, 0], var_eps[:, :], minus_half[:, :], ALU.pow).then_inc(s_pool, 1)

        @block.vector
        def _(dve):
            nc.vector.tensor_scalar(var_eps[:, :], keep[:, :, 1], EPS, None, ALU.add).then_inc(s_dve, 1)
            dve.wait_ge(s_pool, 3)
            nc.vector.scalar_tensor_tensor(rows[:, :, 1], keep[:, :, 0], -1.0, rows[:, :, 0], ALU.mult, ALU.mult).then_inc(s_dve, 1)
            dve.wait_ge(s_dve, 1)
            nc.vector.reciprocal(inv_var[:, :], var_eps[:, :]).then_inc(s_dve, 1)
            dve.wait_ge(s_dve, 3)
            nc.vector.tensor_tensor(var_n[:, :], keep[:, :, 1], inv_var[:, :], ALU.mult).then_inc(s_dve, 1)
            dve.wait_ge(s_pe, 1)
            nc.vector.tensor_scalar(mean_n[:, :], total[:, :], 1.0 / (B * P), 1e-6, ALU.mult, ALU.add).then_inc(s_dve, 1)
            dve.wait_ge(s_dve, 5)
            nc.vector.reciprocal(inv_mean[:, :], mean_n[:, :]).then_inc(s_dve, 1)
            dve.wait_ge(s_dve, 6)
            nc.vector.tensor_scalar(rows[:, :, 2], log_var[:, :], inv_mean[:, :], 0.5, ALU.mult, ALU.mult).then_inc(s_dve, 1)

        @block.scalar
        def _(act):
            act.wait_ge(s_dve, 4)
            nc.scalar.activation(log_var[:, :], var_n[:, :], ACT.Ln, bias=1.0, accum_out=log_sum[:, :]).then_inc(s_act, 1)

        @block.tensor
        def _(pe):
            pe.wait_ge(s_act, 1)
            pe.wait_ge(s_pool, 2)
            nc.tensor.matmul(total[:, :], ones[:, :], log_sum[:, :], start=True, stop=True).then_inc(s_pe, 1)


def layer0_ffn_layer1_heads(nc, sems, w, rows, x1_dram, kv_dram, x2_dram, o_dram):
    with ExitStack() as ctx:
        def sb(name, shape, dt=F32):
            return ctx.enter_context(nc.sbuf_tensor(f"b_{name}", shape, dt))

        def sem(name):
            return sems.new(nc.semaphore(f"b_{name}"))

        def signal(name, n):
            return Signal(sem(name), n)

        def dma_signal(name, n=1):
            return DmaSignal([sem(f"{name}_{p}") for p in "eo"], n)

        def both(name, shape):
            return sb(f"{name}_hi", shape, F32R), sb(f"{name}_lo", shape, F32R)

        score_bank = [ctx.enter_context(nc.psum_tensor(f"b_score{i}", [P, HALF], F32)) for i in range(2)]
        turn_bank = [ctx.enter_context(nc.psum_tensor(f"b_turn{i}", [P, HALF], F32)) for i in range(2)]
        out_bank = [ctx.enter_context(nc.psum_tensor(f"b_out{i}", [P, HALF], F32)) for i in range(2)]
        wide = ctx.enter_context(nc.psum_tensor("b_wide", [P, DM], F32))
        GCOL = REP * P
        NG = KV1

        ident = sb("ident", [P, P])
        wq = both("wq", [P, KT, DM])
        wuq = both("wuq", [P, KT, UQ])
        route = sb("route", [BOT + 1, 2 * SLOTS])
        values = sb("values", [P, 2, BOT])
        wvuT = sb("wvuT", [BOT, DM])
        bu1 = sb("bu1", [P, UH])
        wu2 = sb("wu2", [P, UH])
        tiny = sb("tiny", [P, 6])

        x1 = [sb(f"x1_{p}", [P, DM]) for p in range(2)]
        kv = [sb(f"kv{p}", [P, 2 * KVD]) for p in range(2)]
        row = [sb(f"row{p}", [P, 3]) for p in range(2)]
        h = sb("h", [P, DM])
        xh = sb("xh", [P, DM])
        hT = both("hT", [P, KT, P])
        z = sb("z", [P, UH])
        zt = sb("zt", [P, UH])
        query = sb("query", [P, P])
        queryT = sb("queryT", [BOT + 1, P])
        top = sb("top", [P, TOPK])
        left = sb("left", [P, SLOTS])
        picked = sb("picked", [P, SLOTS])
        pickedT = sb("pickedT", [P, 2, P])
        mixT = sb("mixT", [BOT, P])
        peak = sb("peak", [P, 2])
        esum = sb("esum", [P, 2])
        gate = sb("gate", [P, 12])
        x2 = [sb(f"x2_{p}", [P, DM]) for p in range(2)]
        ln_stats = sb("ln_stats", [P, 2, 6])
        ln_mv = sb("ln_mv", [P, 2])
        ln = sb("ln", [P, 4])
        consts = sb("consts", [P, 3])
        carrier = sb("carrier", [P, 1])
        q = sb("q", [P, DM])
        qT = both("qT", [P, NG, P])
        k_rep = sb("k_rep", [P, NG, REP, D1])
        k_diag = both("k_diag", [P, NG, GCOL])
        s_max = [sb(f"s_max{r}", [P, REP]) for r in range(2)]
        s_sum = [sb(f"s_sum{r}", [P, REP]) for r in range(2)]
        s_inv = [sb(f"s_inv{r}", [P, REP]) for r in range(2)]
        prob = [sb(f"prob{r}", [P, GCOL]) for r in range(3)]
        probT = [sb(f"probT{r}", [P, GCOL]) for r in range(4)]
        o_sb = [sb(f"o{p}", [P, 2, HALF]) for p in range(1)]

        s_load = sem("loaded")
        s_raw = [sem(f"raw_loaded{n}") for n in range(2)]
        s_const = sem("consts_made")
        s_ident = sem("ident_made")
        s_high = sem("weights_high")
        s_low = sem("weights_low")
        s_turned = sem("weights_turned")
        s_setup = sem("weights_placed")
        s_zero = sem("diag_zeroed")
        s_tiny = sem("tiny_halved")

        x1_in, kv_in = dma_signal("x1_in"), dma_signal("kv_in")
        x2_out, o_out = dma_signal("x2_out"), dma_signal("o_out")
        row_taken = signal("row_taken", 1)
        h_made = signal("h_made", 1)
        xh_added = signal("xh_added", 1)
        h_turned = signal("h_turned", 1)
        hT_high, hT_low = signal("hT_high", 1), signal("hT_low", 1)
        uq_ready = signal("uq_ready", 1)
        z_step = signal("z_step", 5)
        query_copied = signal("query_copied", 1)
        z_tanh = signal("z_tanh", 1)
        learned = signal("learned", 1)
        learned_tanh = signal("learned_tanh", 1)
        u_step = signal("u_step", 5)
        gate_tanh = signal("gate_tanh", 1)
        g_step = signal("g_step", 5)
        query_turned = signal("query_turned", 1)
        queryT_copied = signal("queryT_copied", 1)
        scored = signal("scored", 1)
        pick_step = signal("pick_step", 6)
        picked_exp = signal("picked_exp", 1)
        picked_turned = signal("picked_turned", 1)
        pickedT_copied = signal("pickedT_copied", 1)
        mixed = signal("mixed", 1)
        mixT_copied = signal("mixT_copied", 1)
        aux_ready = signal("aux_ready", 1)
        x2_made = signal("x2_made", 1)
        ln_step = signal("ln_step", 3)
        ln_rs = signal("ln_rs", 4)
        h2_made = signal("h2_made", 1)
        h2_turned = signal("h2_turned", 1)
        h2T_high, h2T_low = signal("h2T_high", 1), signal("h2T_low", 1)
        k_repeated = signal("k_repeated", 1)
        k_turned = signal("k_turned", 2)
        k_high, k_low = signal("k_high", 1), signal("k_low", 1)
        q_ready = signal("q_ready", 2)
        q_copied = signal("q_copied", 1)
        q_turned = signal("q_turned", 1)
        qT_high, qT_low = signal("qT_high", 1), signal("qT_low", 1)
        s_ready = signal("s_ready", NG)
        s_maxed = signal("s_maxed", NG)
        s_less = signal("s_less", NG)
        s_exped = signal("s_exped", NG)
        s_summed = signal("s_summed", NG)
        s_inverted = signal("s_inverted", NG)
        s_normed = signal("s_normed", NG)
        p_turned = signal("p_turned", NG)
        p_stored = signal("p_stored", NG)
        o_ready = signal("o_ready", 2)
        o_copied = signal("o_copied", 2)

        raw = [x1[0], x1[1]]
        block = ctx.enter_context(nc.Block())

        def schedule(fill, step):
            def run(eng):
                fill(eng, Batch(0, 0))
                step(eng, Batch(0, 0), Batch(0, 1))
                step(eng, Batch(0, 1), Batch(1, 0))
                with eng.Fori(1, B // 2 - 1) as pair:
                    step(eng, Batch(pair, 0), Batch(pair, 1))
                    step(eng, Batch(pair, 1), Batch(pair + 1, 0))
                step(eng, Batch(B // 2 - 1, 0), Batch(B // 2 - 1, 1))
                step(eng, Batch(B // 2 - 1, 1), None)
            return run

        small = [("L0_ffn_Wu1", 2), ("L0_ffn_Wq", 1), ("L0_ffn_Wvd", 1), ("L0_ffn_aux_values", 2)]
        pieces = []
        for name, n in small:
            height = w[name].shape[0] // n
            pieces += [(w[name][k * height:(k + 1) * height, :], height) for k in range(n)]
        NT = len(pieces)
        pieces += [(w["L1_xattn_Wq"][k * P:(k + 1) * P, :], P) for k in range(KT)]

        @block.sync
        def _(sp):
            sp.dma_start(q[:, 0:BOT], w["L0_ffn_aux_keys"][0:P, :]).then_inc(s_load, 16)
            sp.dma_start(q[:, BOT:2 * BOT], w["L0_ffn_aux_keys"][P:2 * P, :]).then_inc(s_load, 16)
            sp.dma_start(q[0:RDIM, 2 * BOT:3 * BOT], w["L0_ffn_Wr"]).then_inc(s_load, 16)
            sp.dma_start(q[:, 4 * BOT:12 * BOT].rearrange("p (t b) -> p t b", b=BOT),
                         w["L0_ffn_Wvu"].rearrange("(t p) b -> p t b", p=P)).then_inc(s_load, 16)
            for half in range(2):
                sp.dma_start(route[BOT:BOT + 1, half * SLOTS:(half + 1) * SLOTS],
                             w["L0_ffn_log_rel"].rearrange("(a s) -> a s", a=1)).then_inc(s_load, 16)
            sp.dma_start(bu1[:, :], w["L0_ffn_bu1"].partition_broadcast(P)).then_inc(s_load, 16)
            sp.dma_start(wu2[:, :], w["L0_ffn_Wu2"][0].partition_broadcast(P)).then_inc(s_load, 16)
            for n, name in enumerate(("L0_ffn_bu2", "L0_ffn_gate_w1", "L0_ffn_gate_bias")):
                sp.dma_start(tiny[:, n:n + 1], w[name].partition_broadcast(P)).then_inc(s_load, 16)
            for n, (src, height) in enumerate(pieces):
                if n >= 2:
                    if n - 2 < NT:
                        sp.wait_ge(s_turned, n - 1)
                    else:
                        sp.wait_ge(s_low, 3 + (n - 2 - NT + 1))
                sp.dma_start(raw[n % 2][0:height, :], src).then_inc(s_raw[n % 2], 16)
            sp.wait_ge(s_low, 3 + KT)

            def load(i):
                need(sp, xh_added, i.before(2), 1)
                need(sp, h_made, i.before(2), 1)
                sp.dma_start(x1[i.odd][:, :], x1_dram[i.index]).then_inc(x1_in.sems[i.odd], 16)
                need(sp, o_ready, i.before(2), 2)
                need(sp, k_repeated, i.before(2), 1)
                sp.dma_start(kv[i.odd][:, :], kv_dram[i.index]).then_inc(kv_in.sems[i.odd], 16)

            def fill(eng, i):
                load(i)
                load(i.after())
                need(sp, x2_made, i, 1)
                sp.dma_start(x2_dram[i.index], x2[i.odd][:, :]).then_inc(x2_out.sems[i.odd], 16)

            def step(eng, i, nxt):
                if nxt is not None:
                    need(sp, x2_made, nxt, 1)
                    sp.dma_start(x2_dram[nxt.index], x2[nxt.odd][:, :]).then_inc(x2_out.sems[nxt.odd], 16)
                need(sp, o_copied, i, 2)
                sp.dma_start(o_dram[i.index], o_sb[0][:, :, :].rearrange("p a b -> p (a b)")).then_inc(o_out.sems[i.odd], 16)
                if nxt is not None and not (isinstance(nxt.pair, int) and nxt.pair == B // 2 - 1 and nxt.odd):
                    load(nxt.after())

            schedule(fill, step)(sp)
            for p in range(2):
                sp.wait_ge(x2_out.sems[p], 16 * (B // 2))
                sp.wait_ge(o_out.sems[p], 16 * (B // 2))

        @block.gpsimd
        def _(pool):
            make_identity(nc, pool, ident, s_ident)
            for n, value in enumerate((EPS, -0.5, -1.0)):
                nc.gpsimd.memset(consts[:, n:n + 1], value).then_inc(s_const, 1)
            pool.wait_ge(s_const, 3)

            def ffn(i):
                need(pool, h_made, i, 1)
                need(pool, x1_in, i, 1)
                need(pool, x2_made, i.before(1), 1)
                nc.gpsimd.tensor_tensor(xh[:, :], x1[i.odd][:, :], h[:, :], ALU.add).then_inc(xh_added.sem, 1)

            def second(i):
                need(pool, ln_step, i, 3)
                need(pool, h2_made, i.before(1), 1)
                nc.gpsimd.tensor_tensor(ln[:, 0:1], ln_mv[:, 1:2], consts[:, 0:1], ALU.add).then_inc(ln_rs.sem, 1)
                need(pool, ln_rs, i, 1)
                nc.gpsimd.tensor_tensor(ln[:, 1:2], ln[:, 0:1], consts[:, 1:2], ALU.pow).then_inc(ln_rs.sem, 1)
                need(pool, ln_rs, i, 2)
                nc.gpsimd.tensor_tensor(ln[:, 2:3], ln_mv[:, 0:1], consts[:, 2:3], ALU.mult).then_inc(ln_rs.sem, 1)
                need(pool, ln_rs, i, 3)
                nc.gpsimd.tensor_tensor(ln[:, 3:4], ln[:, 2:3], ln[:, 1:2], ALU.mult).then_inc(ln_rs.sem, 1)

            def fill(eng, i):
                ffn(i)
                second(i)

            def step(eng, i, nxt):
                for g in range(NG):
                    need(pool, s_inverted, i, g + 1)
                    pr = prob[g % 3][:, :].rearrange("p (r k) -> p r k", r=REP)
                    nc.gpsimd.tensor_tensor(pr, pr, s_inv[g % 2][:, :].unsqueeze(2).to_broadcast([P, REP, P]),
                                            ALU.mult).then_inc(s_normed.sem, 1)
                    if nxt is not None and g == 0:
                        ffn(nxt)
                if nxt is not None:
                    second(nxt)

            schedule(fill, step)(pool)

        @block.tensor
        def _(pe):
            pe.wait_ge(s_ident, 2)
            for n in range(NT):
                height = pieces[n][1]
                pe.wait_ge(s_raw[n % 2], 16 * (n // 2 + 1))
                if n in (1, 2, 3):
                    pe.wait_ge(s_low, n)
                elif n > 3:
                    pe.wait_ge(s_setup, n - 3)
                for t in range(KT):
                    mm = nc.tensor.transpose(wide[:, t * P:t * P + height], raw[n % 2][0:height, t * P:(t + 1) * P],
                                             ident[0:height, 0:height])
                mm.then_inc(s_turned, 1)
            pe.wait_ge(s_setup, 3)
            for s in range(2):
                for t in range(KT):
                    mm = nc.tensor.matmul(score_bank[0][:, s * BOT:(s + 1) * BOT],
                                          probT[2 * s + t // 4][:, (t % 4) * P:(t % 4 + 1) * P],
                                          k_rep[:, t].rearrange("p r d -> p (r d)")[:, 0:BOT], start=(t == 0), stop=(t == KT - 1))
            mm.then_inc(s_turned, 1)
            pe.wait_ge(s_load, 16 * 11)
            for s in range(2):
                nc.tensor.transpose(turn_bank[0][0:BOT, s * P:(s + 1) * P], q[:, s * BOT:(s + 1) * BOT], ident[:, :])
            mm = nc.tensor.transpose(turn_bank[0][0:BOT, 2 * P:2 * P + RDIM], q[0:RDIM, 2 * BOT:3 * BOT], ident[0:RDIM, 0:RDIM])
            for t in range(KT):
                mm = nc.tensor.transpose(wide[0:BOT, t * P:(t + 1) * P], q[:, (4 + t) * BOT:(5 + t) * BOT], ident[:, :])
            mm.then_inc(s_turned, 1)
            pe.wait_ge(s_setup, 6)
            nc.tensor.matmul(score_bank[1][0:RDIM, 0:SLOTS], h[0:BOT, SLOTS:SLOTS + RDIM], h[0:BOT, 0:SLOTS],
                             start=True, stop=True).then_inc(s_turned, 1)
            pe.wait_ge(s_setup, 7)
            nc.tensor.matmul(turn_bank[1][0:BOT, 0:SLOTS], q[0:RDIM, 2 * BOT:3 * BOT], h[0:RDIM, HALF:HALF + SLOTS],
                             start=True, stop=True).then_inc(s_turned, 1)
            pe.wait_ge(s_setup, 8)
            pe.wait_ge(s_low, 3 + KT)
            pe.wait_ge(s_high, 3 + KT)
            pe.wait_ge(s_zero, 4)

            def ffn(i):
                def turn_h():
                    need(pe, h_made, i, 1)
                    need(pe, qT_low, i.before(1), 1)
                    need(pe, qT_high, i.before(1), 1)
                    for t in range(KT):
                        mm = nc.tensor.transpose(wide[:, t * P:(t + 1) * P], h[:, t * P:(t + 1) * P], ident[:, :])
                    mm.then_inc(h_turned.sem, 1)

                def up_and_query():
                    need(pe, hT_low, i, 1)
                    for t in range(KT):
                        mm = product(nc, wide[:, 0:UQ], [m[:, t] for m in hT], [m[:, t] for m in wuq], t == 0, t == KT - 1)
                    mm.then_inc(uq_ready.sem, 1)

                def turn_query():
                    need(pe, query_copied, i, 1)
                    nc.tensor.transpose(wide[:, HALF:HALF + P], query[:, :], ident[:, :]).then_inc(query_turned.sem, 1)

                def score_slots():
                    need(pe, queryT_copied, i, 1)
                    nc.tensor.matmul(wide[:, HALF:DM], queryT[:, :], route[:, :], start=True, stop=True).then_inc(scored.sem, 1)

                def turn_picked():
                    need(pe, picked_exp, i, 1)
                    need(pe, z_step, i, 1)
                    for s in range(2):
                        mm = nc.tensor.transpose(wide[:, s * P:(s + 1) * P], picked[:, s * P:(s + 1) * P], ident[:, :])
                    mm.then_inc(picked_turned.sem, 1)

                def mix_values():
                    need(pe, pickedT_copied, i, 1)
                    for s in range(2):
                        mm = nc.tensor.matmul(wide[0:BOT, HALF:HALF + P], values[:, s], pickedT[:, s], start=(s == 0), stop=(s == 1))
                    mm.then_inc(mixed.sem, 1)

                def up_values():
                    need(pe, mixT_copied, i, 1)
                    for half in range(2):
                        cols = slice(half * HALF, (half + 1) * HALF)
                        mm = nc.tensor.matmul(wide[:, cols], mixT[:, :], wvuT[:, cols], start=True, stop=True)
                    mm.then_inc(aux_ready.sem, 1)

                return [turn_h, up_and_query, turn_query, score_slots, turn_picked, mix_values, up_values]

            def second(i):
                need(pe, k_repeated, i, 1)
                need(pe, s_less, i.before(1), NG)
                for g in range(NG):
                    mm = nc.tensor.transpose(score_bank[g // 4][:, (g % 4) * P:(g % 4 + 1) * P],
                                             k_rep[:, g].rearrange("p r d -> p (r d)"), ident[:, :])
                    if g % 4 == 3:
                        mm.then_inc(k_turned.sem, 1)
                need(pe, h2_made, i, 1)
                for t in range(KT):
                    mm = nc.tensor.transpose(wide[:, t * P:(t + 1) * P], h[:, t * P:(t + 1) * P], ident[:, :])
                mm.then_inc(h2_turned.sem, 1)
                need(pe, h2T_low, i, 1)
                need(pe, p_stored, i.before(1), NG)
                for half in range(2):
                    cols = slice(half * HALF, (half + 1) * HALF)
                    for t in range(KT):
                        mm = product(nc, turn_bank[half][:, :], [m[:, t] for m in hT], [m[:, t, cols] for m in wq],
                                     t == 0, t == KT - 1)
                    mm.then_inc(q_ready.sem, 1)
                need(pe, q_copied, i, 1)
                for g in range(NG):
                    mm = nc.tensor.transpose(wide[:, g * P:(g + 1) * P], q[:, g * P:(g + 1) * P], ident[:, :])
                mm.then_inc(q_turned.sem, 1)

            def fill(eng, i):
                for part in ffn(i):
                    part()
                second(i)

            LAG = 3

            def step(eng, i, nxt):
                parts = ffn(nxt) if nxt is not None else []
                need(pe, qT_low, i, 1)
                need(pe, k_low, i, 1)
                for s in range(NG + LAG):
                    if s < NG:
                        if s >= 2:
                            need(pe, s_less, i, s - 1)
                        product(nc, score_bank[s % 2][:, :], [m[:, s] for m in qT], [m[:, s] for m in k_diag],
                                True, True).then_inc(s_ready.sem, 1)
                    if parts and s >= 1:
                        parts.pop(0)()
                    if s >= LAG:
                        g = s - LAG
                        need(pe, s_normed, i, g + 1)
                        if g >= 2:
                            need(pe, p_stored, i, g - 1)
                        else:
                            need(pe, q_copied, i, 1)
                        for r in range(REP):
                            mm = nc.tensor.transpose(turn_bank[g % 2][:, r * P:(r + 1) * P],
                                                     prob[g % 3][:, r * P:(r + 1) * P], ident[:, :])
                        mm.then_inc(p_turned.sem, 1)
                        if g % 4 == 3:
                            need(pe, p_stored, i, g + 1)
                            need(pe, o_copied, i.before(1), g // 4 + 1)
                            for c in range(4):
                                grp = g - 3 + c
                                mm = nc.tensor.matmul(out_bank[g // 4][c * D1:(c + 1) * D1, :],
                                                      kv[i.odd][:, KVD + grp * D1:KVD + (grp + 1) * D1],
                                                      probT[grp % 4][:, :], start=True, stop=True,
                                                      tile_position=(0, c * D1))
                            mm.then_inc(o_ready.sem, 1)
                while parts:
                    parts.pop(0)()
                if nxt is not None:
                    second(nxt)

            schedule(fill, step)(pe)

        @block.scalar
        def _(act):
            wuq_at = [(0, 0, P), (0, P, P), (0, UH, BOT)]
            for n in range(NT):
                act.wait_ge(s_turned, n + 1)
                src = wide[:, :].rearrange("p (t c) -> p t c", t=KT)
                if n < 3:
                    _, at, height = wuq_at[n]
                    nc.scalar.copy(wuq[0][:, :, at:at + height], src[:, :, 0:height]).then_inc(s_high, 1)
                elif n == 3:
                    nc.scalar.copy(k_rep[:, :, :, :].rearrange("p t r d -> p t (r d)")[:, :, 0:BOT], src[:, :, 0:BOT]).then_inc(s_setup, 1)
                else:
                    s = n - 4
                    nc.scalar.copy(probT[2 * s][:, :], wide[:, 0:HALF])
                    nc.scalar.copy(probT[2 * s + 1][:, :], wide[:, HALF:DM]).then_inc(s_setup, 1)
            act.wait_ge(s_turned, NT + 1)
            nc.scalar.copy(values[:, :, :].rearrange("p s b -> p (s b)"), score_bank[0][:, 0:2 * BOT]).then_inc(s_setup, 1)
            act.wait_ge(s_turned, NT + 2)
            nc.scalar.copy(h[0:BOT, 0:SLOTS + RDIM], turn_bank[0][0:BOT, 0:SLOTS + RDIM]).then_inc(s_setup, 1)
            nc.scalar.copy(wvuT[:, :], wide[0:BOT, :]).then_inc(s_setup, 1)
            act.wait_ge(s_turned, NT + 3)
            nc.scalar.copy(h[0:RDIM, HALF:HALF + SLOTS], score_bank[1][0:RDIM, 0:SLOTS]).then_inc(s_setup, 1)
            act.wait_ge(s_turned, NT + 4)
            nc.scalar.mul(route[0:BOT, 0:SLOTS], turn_bank[1][0:BOT, 0:SLOTS], float(RDIM) ** -0.5)
            nc.scalar.mul(route[0:BOT, SLOTS:2 * SLOTS], turn_bank[0][0:BOT, 0:SLOTS], float(BOT) ** -0.5).then_inc(s_setup, 1)
            for n in range(KT):
                act.wait_ge(s_raw[(NT + n) % 2], 16 * ((NT + n) // 2 + 1))
                nc.scalar.copy(wq[0][:, n], raw[(NT + n) % 2][:, :]).then_inc(s_high, 1)
            act.wait_ge(s_tiny, 1)

            def ffn(i):
                def make_h():
                    need(act, row_taken, i, 1)
                    need(act, x1_in, i, 1)
                    need(act, h2_turned, i.before(1), 1)
                    nc.scalar.activation(h[:, :], x1[i.odd][:, :], ACT.Identity, bias=row[i.odd][:, 1:2],
                                         scale=row[i.odd][:, 0:1]).then_inc(h_made.sem, 1)

                def high_h():
                    need(act, h_turned, i, 1)
                    need(act, q_ready, i.before(1), 2)
                    nc.scalar.copy(hT[0][:, :, :].rearrange("p t c -> p (t c)"), wide[:, :]).then_inc(hT_high.sem, 1)

                def copy_query():
                    need(act, z_step, i, 1)
                    nc.scalar.copy(query[:, 0:BOT], wide[:, UH:UQ]).then_inc(query_copied.sem, 1)
                    need(act, query_turned, i, 1)
                    nc.scalar.copy(queryT[:, :], wide[0:BOT + 1, HALF:HALF + P]).then_inc(queryT_copied.sem, 1)

                def tanhs():
                    need(act, z_step, i, 4)
                    nc.scalar.activation(zt[:, :], zt[:, :], ACT.Tanh, scale=GELU_C).then_inc(z_tanh.sem, 1)

                def exp_picked():
                    need(act, pick_step, i, 6)
                    nc.scalar.activation(picked[:, :], picked[:, :], ACT.Exp, bias=peak[:, 1:2],
                                         accum_out=esum[:, 0:1]).then_inc(picked_exp.sem, 1)
                    need(act, learned, i, 1)
                    nc.scalar.activation(gate[:, 1:2], gate[:, 0:1], ACT.Tanh, bias=tiny[:, 3:4], scale=0.5).then_inc(learned_tanh.sem, 1)

                def copy_picked():
                    need(act, picked_turned, i, 1)
                    nc.scalar.copy(pickedT[:, :, :].rearrange("p s c -> p (s c)"), wide[:, 0:SLOTS]).then_inc(pickedT_copied.sem, 1)
                    need(act, u_step, i, 5)
                    nc.scalar.activation(gate[:, 7:8], gate[:, 6:7], ACT.Tanh, bias=tiny[:, 5:6], scale=tiny[:, 4:5]).then_inc(gate_tanh.sem, 1)

                def copy_mix():
                    need(act, mixed, i, 1)
                    nc.scalar.copy(mixT[:, :], wide[0:BOT, HALF:HALF + P]).then_inc(mixT_copied.sem, 1)

                return [make_h, high_h, copy_query, tanhs, exp_picked, copy_picked, copy_mix]

            def second(i):
                need(act, kv_in, i, 1)
                need(act, k_turned, i.before(1), 2)
                nc.scalar.copy(k_rep[:, :, :, :],
                               kv[i.odd][:, 0:KVD].rearrange("p (g d) -> p g d", d=D1).unsqueeze(2).to_broadcast([P, NG, REP, D1])
                               ).then_inc(k_repeated.sem, 1)
                need(act, ln_rs, i, 4)
                need(act, xh_added, i, 1)
                need(act, h_turned, i, 1)
                nc.scalar.activation(h[:, :], x2[i.odd][:, :], ACT.Identity, bias=ln[:, 3:4], scale=ln[:, 1:2]).then_inc(h2_made.sem, 1)
                need(act, k_turned, i, 2)
                need(act, s_ready, i.before(1), NG)
                for n in range(2):
                    for r in range(REP):
                        rows_r = slice(r * D1, (r + 1) * D1)
                        op = nc.scalar.copy(k_diag[0][rows_r, 4 * n:4 * n + 4, r * P:(r + 1) * P],
                                            score_bank[n][rows_r, :].rearrange("p (g k) -> p g k", k=P))
                op.then_inc(k_high.sem, 1)
                need(act, h2_turned, i, 1)
                need(act, uq_ready, i, 1)
                nc.scalar.copy(hT[0][:, :, :].rearrange("p t c -> p (t c)"), wide[:, :]).then_inc(h2T_high.sem, 1)
                need(act, q_ready, i, 2)
                need(act, q_turned, i.before(1), 1)
                nc.scalar.copy(q[:, 0:HALF], turn_bank[0][:, :])
                nc.scalar.copy(q[:, HALF:DM], turn_bank[1][:, :]).then_inc(q_copied.sem, 1)
                need(act, q_turned, i, 1)
                nc.scalar.copy(qT[0][:, :, :].rearrange("p t c -> p (t c)"), wide[:, :]).then_inc(qT_high.sem, 1)

            def fill(eng, i):
                for part in ffn(i):
                    part()
                second(i)

            LAG = 3

            def step(eng, i, nxt):
                parts = ffn(nxt) if nxt is not None else []
                if parts:
                    parts.pop(0)()
                for s in range(NG + LAG):
                    if s < NG:
                        need(act, s_less, i, s + 1)
                        nc.scalar.activation(prob[s % 3][:, :], prob[s % 3][:, :], ACT.Exp, scale=float(D1) ** -0.5).then_inc(s_exped.sem, 1)
                    if parts and s >= 1:
                        parts.pop(0)()
                    if s >= LAG:
                        g = s - LAG
                        need(act, p_turned, i, g + 1)
                        if g == 4:
                            need(act, o_ready, i, 1)
                        elif g == 0:
                            need(act, o_ready, i.before(1), 2)
                        nc.scalar.copy(probT[g % 4][:, :], turn_bank[g % 2][:, :]).then_inc(p_stored.sem, 1)
                        if g % 4 == 3:
                            need(act, o_ready, i, g // 4 + 1)
                            need(act, o_out, i.before(1), 1)
                            nc.scalar.copy(o_sb[0][:, g // 4], out_bank[g // 4][:, :]).then_inc(o_copied.sem, 1)
                while parts:
                    parts.pop(0)()
                if nxt is not None:
                    second(nxt)

            schedule(fill, step)(act)

        @block.vector
        def _(dve):
            for n in range(3):
                at, height = (0, P, UH)[n], (P, P, BOT)[n]
                dve.wait_ge(s_high, n + 1)
                nc.vector.tensor_tensor(wuq[1][:, :, at:at + height],
                                        wide[:, :].rearrange("p (t c) -> p t c", t=KT)[:, :, 0:height],
                                        wuq[0][:, :, at:at + height].bitcast(F32), ALU.subtract).then_inc(s_low, 1)
            dve.wait_ge(s_load, 16 * 11)
            nc.vector.tensor_scalar(tiny[:, 3:6], tiny[:, 0:3], 0.5, None, ALU.mult).then_inc(s_tiny, 1)
            nc.vector.tensor_scalar(wu2[:, :], wu2[:, :], 0.5, None, ALU.mult).then_inc(s_tiny, 1)
            for part in range(2):
                nc.vector.memset(k_diag[part][:, :, :].bitcast(F32), 0.0).then_inc(s_zero, 1)
            nc.vector.memset(query[:, BOT:P], 0.0).then_inc(s_zero, 1)
            dve.wait_ge(s_zero, 3)
            nc.vector.memset(query[:, BOT:BOT + 1], 1.0).then_inc(s_zero, 1)
            for n in range(KT):
                dve.wait_ge(s_high, 3 + n + 1)
                nc.vector.tensor_tensor(wq[1][:, n], raw[(NT + n) % 2][:, :], wq[0][:, n].bitcast(F32), ALU.subtract).then_inc(s_low, 1)
            dve.wait_ge(s_tiny, 2)

            def ffn(i):
                def take_row():
                    nc.vector.tensor_copy(row[i.odd][:, :].unsqueeze(1), rows[:, index_of(i), :]).then_inc(row_taken.sem, 1)

                def low_h():
                    need(dve, hT_high, i, 1)
                    nc.vector.tensor_tensor(hT[1][:, :, :].rearrange("p t c -> p (t c)"), wide[:, :],
                                            hT[0][:, :, :].rearrange("p t c -> p (t c)").bitcast(F32), ALU.subtract).then_inc(hT_low.sem, 1)

                def gelu():
                    need(dve, uq_ready, i, 1)
                    nc.vector.tensor_tensor(z[:, :], wide[:, 0:UH], bu1[:, :], ALU.add).then_inc(z_step.sem, 1)
                    need(dve, z_step, i, 1)
                    nc.vector.tensor_tensor(zt[:, :], z[:, :], z[:, :], ALU.mult).then_inc(z_step.sem, 1)
                    need(dve, z_step, i, 2)
                    nc.vector.tensor_scalar(zt[:, :], zt[:, :], GELU_A, 1.0, ALU.mult, ALU.add).then_inc(z_step.sem, 1)
                    need(dve, z_step, i, 3)
                    nc.vector.tensor_tensor(zt[:, :], zt[:, :], z[:, :], ALU.mult).then_inc(z_step.sem, 1)

                def pick():
                    need_first(scored, i, 1)
                    nc.vector.max(top[:, :], wide[:, HALF:HALF + SLOTS]).then_inc(pick_step.sem, 1)
                    need_first(pick_step, i, 1)
                    nc.vector.match_replace(left[:, :], top[:, :], wide[:, HALF:HALF + SLOTS], -3e38).then_inc(pick_step.sem, 1)
                    need(dve, pick_step, i, 2)
                    nc.vector.tensor_tensor(left[:, :], left[:, :], wide[:, HALF:HALF + SLOTS], ALU.is_equal).then_inc(pick_step.sem, 1)
                    need(dve, pick_step, i, 3)
                    nc.vector.scalar_tensor_tensor(picked[:, :], left[:, :], -MASKED, wide[:, HALF + SLOTS:DM],
                                                   ALU.mult, ALU.add).then_inc(pick_step.sem, 1)
                    need(dve, pick_step, i, 4)
                    nc.vector.tensor_reduce(peak[:, 0:1], picked[:, :], AX.X, ALU.max).then_inc(pick_step.sem, 1)
                    need(dve, pick_step, i, 5)
                    nc.vector.tensor_scalar(peak[:, 1:2], peak[:, 0:1], -1.0, None, ALU.mult).then_inc(pick_step.sem, 1)

                def learn():
                    need(dve, z_tanh, i, 1)
                    nc.vector.scalar_tensor_tensor(z[:, :], zt[:, :], 1.0, z[:, :], ALU.add, ALU.mult).then_inc(z_step.sem, 1)
                    need(dve, z_step, i, 5)
                    nc.vector.tensor_tensor_reduce(zt[:, :], z[:, :], wu2[:, :], 1.0, 0.0, ALU.mult, ALU.add,
                                                   gate[:, 0:1]).then_inc(learned.sem, 1)

                def uncertainty():
                    need(dve, learned_tanh, i, 1)
                    nc.vector.tensor_scalar(gate[:, 2:3], gate[:, 1:2], 1.25, 1.25, ALU.mult, ALU.add).then_inc(u_step.sem, 1)
                    need(dve, u_step, i, 1)
                    nc.vector.tensor_scalar(gate[:, 3:4], gate[:, 2:3], row[i.odd][:, 2:3], 0.0, ALU.add, ALU.max).then_inc(u_step.sem, 1)
                    need(dve, u_step, i, 2)
                    nc.vector.tensor_scalar(gate[:, 4:5], gate[:, 3:4], 5.0, -TAU_LOW, ALU.min, ALU.add).then_inc(u_step.sem, 1)
                    need(dve, u_step, i, 3)
                    nc.vector.tensor_scalar(gate[:, 5:6], gate[:, 4:5], 1.0 / (TAU_HIGH - TAU_LOW), 0.0, ALU.mult, ALU.max).then_inc(u_step.sem, 1)
                    need(dve, u_step, i, 4)
                    nc.vector.tensor_scalar(gate[:, 6:7], gate[:, 5:6], 1.0, None, ALU.min).then_inc(u_step.sem, 1)

                def gates():
                    need(dve, gate_tanh, i, 1)
                    nc.vector.tensor_scalar(gate[:, 8:9], gate[:, 7:8], 0.5, 0.5, ALU.mult, ALU.add).then_inc(g_step.sem, 1)
                    need(dve, g_step, i, 1)
                    nc.vector.tensor_scalar(gate[:, 9:10], gate[:, 8:9], EARLY_EXIT, None, ALU.is_ge).then_inc(g_step.sem, 1)
                    need(dve, picked_exp, i, 1)
                    nc.vector.reciprocal(esum[:, 1:2], esum[:, 0:1]).then_inc(g_step.sem, 1)
                    need(dve, g_step, i, 3)
                    nc.vector.tensor_tensor(gate[:, 10:11], gate[:, 8:9], gate[:, 9:10], ALU.mult).then_inc(g_step.sem, 1)
                    need(dve, g_step, i, 4)
                    nc.vector.tensor_tensor(gate[:, 11:12], gate[:, 10:11], esum[:, 1:2], ALU.mult).then_inc(g_step.sem, 1)

                return [take_row, low_h, gelu, pick, learn, uncertainty, gates]

            def index_of(i):
                return slice(i.index, i.index + 1) if isinstance(i.pair, int) else bass.ds(i.index, 1)

            def need_first(signal, i, k):
                need(dve, signal, i, k)
                nc.vector.memset(carrier[:, :], 0.0)

            def second(i):
                need(dve, aux_ready, i, 1)
                need(dve, xh_added, i, 1)
                need(dve, x2_out, i.before(2), 1)
                need(dve, g_step, i, 5)
                nc.vector.scalar_tensor_tensor(x2[i.odd][:, :], wide[:, :], gate[:, 11:12], xh[:, :], ALU.mult, ALU.add).then_inc(x2_made.sem, 1)
                need(dve, x2_made, i, 1)
                need(dve, ln_rs, i.before(1), 4)
                for half in range(2):
                    nc.vector.bn_stats(ln_stats[:, half], x2[i.odd][:, half * HALF:(half + 1) * HALF]).then_inc(ln_step.sem, 1)
                need_first(ln_step, i, 2)
                nc.vector.bn_aggr(ln_mv[:, :], ln_stats[:, :, :]).then_inc(ln_step.sem, 1)
                need(dve, k_high, i, 1)
                for n in range(2):
                    for r in range(REP):
                        rows_r = slice(r * D1, (r + 1) * D1)
                        blk = [m[rows_r, 4 * n:4 * n + 4, r * P:(r + 1) * P] for m in k_diag]
                        op = nc.vector.tensor_tensor(blk[1], score_bank[n][rows_r, :].rearrange("p (g k) -> p g k", k=P),
                                                     blk[0].bitcast(F32), ALU.subtract)
                op.then_inc(k_low.sem, 1)
                need(dve, h2T_high, i, 1)
                nc.vector.tensor_tensor(hT[1][:, :, :].rearrange("p t c -> p (t c)"), wide[:, :],
                                        hT[0][:, :, :].rearrange("p t c -> p (t c)").bitcast(F32), ALU.subtract).then_inc(h2T_low.sem, 1)
                need(dve, qT_high, i, 1)
                nc.vector.tensor_tensor(qT[1][:, :, :].rearrange("p t c -> p (t c)"), wide[:, :],
                                        qT[0][:, :, :].rearrange("p t c -> p (t c)").bitcast(F32), ALU.subtract).then_inc(qT_low.sem, 1)

            def fill(eng, i):
                for part in ffn(i):
                    part()
                second(i)

            def step(eng, i, nxt):
                parts = ffn(nxt) if nxt is not None else []
                if parts:
                    parts.pop(0)()
                for s in range(NG + 1):
                    if s < NG:
                        need(dve, s_ready, i, s + 1)
                        sv = score_bank[s % 2][:, :].rearrange("p (r k) -> p r k", r=REP)
                        nc.vector.tensor_reduce(s_max[s % 2][:, :], sv, AX.X, ALU.max).then_inc(s_maxed.sem, 1)
                        need(dve, s_maxed, i, s + 1)
                        if s >= 3:
                            need(dve, p_turned, i, s - 2)
                        else:
                            need(dve, p_turned, i.before(1), NG)
                        nc.vector.tensor_tensor(prob[s % 3][:, :].rearrange("p (r k) -> p r k", r=REP), sv,
                                                s_max[s % 2][:, :].unsqueeze(2).to_broadcast([P, REP, P]),
                                                ALU.subtract).then_inc(s_less.sem, 1)
                    if s >= 1:
                        g = s - 1
                        need(dve, s_exped, i, g + 1)
                        nc.vector.tensor_reduce(s_sum[g % 2][:, :], prob[g % 3][:, :].rearrange("p (r k) -> p r k", r=REP),
                                                AX.X, ALU.add).then_inc(s_summed.sem, 1)
                        need(dve, s_summed, i, g + 1)
                        if g >= 2:
                            need(dve, s_normed, i, g - 1)
                        nc.vector.reciprocal(s_inv[g % 2][:, :], s_sum[g % 2][:, :]).then_inc(s_inverted.sem, 1)
                    if parts and s >= 1:
                        parts.pop(0)()
                while parts:
                    parts.pop(0)()
                if nxt is not None:
                    second(nxt)

            schedule(fill, step)(dve)


def layer1_out_and_ffn(nc, sems, w, x2_dram, o_dram, out):
    with ExitStack() as ctx:
        def sb(name, shape, dt=F32):
            return ctx.enter_context(nc.sbuf_tensor(f"c_{name}", shape, dt))

        def sem(name):
            return sems.new(nc.semaphore(f"c_{name}"))

        def signal(name, n):
            return Signal(sem(name), n)

        def dma_signal(name, n=1):
            return DmaSignal([sem(f"{name}_{p}") for p in "eo"], n)

        def both(name, shape):
            return sb(f"{name}_hi", shape, F32R), sb(f"{name}_lo", shape, F32R)

        def wide_bank(name):
            return ctx.enter_context(nc.psum_tensor(f"c_{name}", [P, DM], F32))

        o_wide, t_wide, s_wide = wide_bank("o_wide"), wide_bank("t_wide"), wide_bank("s_wide")
        ident = sb("ident", [P, P])
        consts = sb("consts", [P, 3])
        wo = both("wo", [P, KT, DM])
        sign = both("sign", [P, KT, DM])
        soft = sb("soft", [P, 5])
        raw = [sb(f"raw{n}", [P, DM]) for n in range(2)]
        carrier = sb("carrier", [P, 1])

        o_in_sb = [sb(f"o{p}", [P, DM]) for p in range(2)]
        o_hl = both("o_hl", [P, KT, P])
        x2 = [sb(f"x2_{p}", [P, DM]) for p in range(2)]
        x3 = [sb(f"x3_{p}", [P, DM]) for p in range(2)]
        h = sb("h", [P, DM])
        hT = both("hT", [P, KT, P])
        ln_stats = sb("ln_stats", [P, 2, 6])
        ln_mv = sb("ln_mv", [P, 2])
        ln = sb("ln", [P, 4])
        y = [sb(f"y{p}", [P, DM]) for p in range(2)]

        s_raw = [sem(f"raw_loaded{n}") for n in range(2)]
        s_scale = sem("scale_loaded")
        s_ident, s_const = sem("ident_made"), sem("consts_made")
        s_high, s_low = sem("weights_high"), sem("weights_low")
        s_soft_dve, s_soft_act = sem("softplus_dve"), sem("softplus_act")
        o_in, x2_in, y_out = dma_signal("o_in"), dma_signal("x2_in"), dma_signal("y_out")
        o_high, o_low = signal("o_high", 1), signal("o_low", 1)
        o_ready = signal("o_ready", 1)
        x3_made = signal("x3_made", 1)
        ln_step = signal("ln_step", 3)
        ln_rs = signal("ln_rs", 4)
        h_made = signal("h_made", 1)
        h_turned = signal("h_turned", 1)
        hT_high, hT_low = signal("hT_high", 1), signal("hT_low", 1)
        f_ready = signal("f_ready", 1)
        y_made = signal("y_made", 1)
        block = ctx.enter_context(nc.Block())

        def schedule(fill, step):
            def run(eng):
                fill(eng, Batch(0, 0))
                step(eng, Batch(0, 0), Batch(0, 1))
                step(eng, Batch(0, 1), Batch(1, 0))
                with eng.Fori(1, B // 2 - 1) as pair:
                    step(eng, Batch(pair, 0), Batch(pair, 1))
                    step(eng, Batch(pair, 1), Batch(pair + 1, 0))
                step(eng, Batch(B // 2 - 1, 0), Batch(B // 2 - 1, 1))
                step(eng, Batch(B // 2 - 1, 1), None)
            return run

        @block.sync
        def _(sp):
            sp.dma_start(soft[:, 0:1], w["L1_ffn_scale"].partition_broadcast(P)).then_inc(s_scale, 16)

            def load(i):
                need(sp, o_low, i.before(2), 1)
                need(sp, o_high, i.before(2), 1)
                sp.dma_start(o_in_sb[i.odd][:, :], o_dram[i.index]).then_inc(o_in.sems[i.odd], 16)
                need(sp, x3_made, i.before(2), 1)
                sp.dma_start(x2[i.odd][:, :], x2_dram[i.index]).then_inc(x2_in.sems[i.odd], 16)

            for n in range(2 * KT):
                if n >= 2:
                    sp.wait_ge(s_low, n - 1)
                if n < KT:
                    src = w["L1_xattn_Wo"].rearrange("(a g r d) n -> a r g d n", a=2, g=4, r=REP)[n // 4, n % 4]
                    for grp in range(4):
                        sp.dma_start(raw[n % 2][grp * D1:(grp + 1) * D1, :], src[grp]).then_inc(s_raw[n % 2], 16)
                else:
                    sp.dma_start(raw[n % 2][:, :], w["L1_ffn_sign"][(n - KT) * P:(n - KT + 1) * P, :]).then_inc(s_raw[n % 2], 64)

            def fill(eng, i):
                load(i)
                load(i.after())

            def step(eng, i, nxt):
                if nxt is not None and not (isinstance(nxt.pair, int) and nxt.pair == B // 2 - 1 and nxt.odd):
                    load(nxt.after())
                need(sp, y_made, i, 1)
                sp.dma_start(out[i.index], y[i.odd][:, :]).then_inc(y_out.sems[i.odd], 16)

            schedule(fill, step)(sp)
            for p in range(2):
                sp.wait_ge(y_out.sems[p], 16 * (B // 2))

        @block.gpsimd
        def _(pool):
            make_identity(nc, pool, ident, s_ident)
            for n, value in enumerate((EPS, -0.5, -1.0)):
                nc.gpsimd.memset(consts[:, n:n + 1], value).then_inc(s_const, 1)
            pool.wait_ge(s_const, 3)

            def split_o(i):
                need(pool, o_high, i, 1)
                need(pool, o_in, i, 1)
                need(pool, o_ready, i.before(1), 1)
                nc.gpsimd.tensor_tensor(o_hl[1][:, :, :].rearrange("p t c -> p (t c)"), o_in_sb[i.odd][:, :],
                                        o_hl[0][:, :, :].rearrange("p t c -> p (t c)").bitcast(F32), ALU.subtract).then_inc(o_low.sem, 1)

            def norm(i):
                need(pool, ln_step, i, 3)
                need(pool, h_made, i.before(1), 1)
                nc.gpsimd.tensor_tensor(ln[:, 0:1], ln_mv[:, 1:2], consts[:, 0:1], ALU.add).then_inc(ln_rs.sem, 1)
                need(pool, ln_rs, i, 1)
                nc.gpsimd.tensor_tensor(ln[:, 1:2], ln[:, 0:1], consts[:, 1:2], ALU.pow).then_inc(ln_rs.sem, 1)
                need(pool, ln_rs, i, 2)
                nc.gpsimd.tensor_tensor(ln[:, 2:3], ln_mv[:, 0:1], consts[:, 2:3], ALU.mult).then_inc(ln_rs.sem, 1)
                need(pool, ln_rs, i, 3)
                nc.gpsimd.tensor_tensor(ln[:, 3:4], ln[:, 2:3], ln[:, 1:2], ALU.mult).then_inc(ln_rs.sem, 1)

            def fill(eng, i):
                split_o(i)

            def step(eng, i, nxt):
                norm(i)
                if nxt is not None:
                    split_o(nxt)

            schedule(fill, step)(pool)

        @block.tensor
        def _(pe):
            pe.wait_ge(s_ident, 2)
            pe.wait_ge(s_low, 2 * KT)

            def out_proj(i, half):
                if half == 0:
                    need(pe, o_low, i, 1)
                    need(pe, x3_made, i.before(1), 1)
                cols = slice(half * HALF, (half + 1) * HALF)
                for t in range(KT):
                    mm = product(nc, o_wide[:, cols], [m[:, t] for m in o_hl], [m[:, t, cols] for m in wo],
                                 t == 0, t == KT - 1)
                if half:
                    mm.then_inc(o_ready.sem, 1)

            def fill(eng, i):
                out_proj(i, 0)
                out_proj(i, 1)

            def step(eng, i, nxt):
                if nxt is not None:
                    out_proj(nxt, 0)
                need(pe, h_made, i, 1)
                need(pe, hT_low, i.before(1), 1)
                for t in range(KT):
                    mm = nc.tensor.transpose(t_wide[:, t * P:(t + 1) * P], h[:, t * P:(t + 1) * P], ident[:, :])
                mm.then_inc(h_turned.sem, 1)
                if nxt is not None:
                    out_proj(nxt, 1)
                need(pe, hT_low, i, 1)
                need(pe, y_made, i.before(1), 1)
                for half in range(2):
                    cols = slice(half * HALF, (half + 1) * HALF)
                    for t in range(KT):
                        mm = product(nc, s_wide[:, cols], [m[:, t] for m in hT], [m[:, t, cols] for m in sign],
                                     t == 0, t == KT - 1)
                mm.then_inc(f_ready.sem, 1)

            schedule(fill, step)(pe)

        @block.scalar
        def _(act):
            act.wait_ge(s_soft_dve, 2)
            nc.scalar.activation(soft[:, 2:3], soft[:, 1:2], ACT.Exp, scale=-1.0).then_inc(s_soft_act, 1)
            act.wait_ge(s_soft_act, 1)
            nc.scalar.activation(soft[:, 3:4], soft[:, 2:3], ACT.Ln, bias=1.0).then_inc(s_soft_act, 1)
            for n in range(2 * KT):
                act.wait_ge(s_raw[n % 2], 64 * (n // 2 + 1))
                nc.scalar.copy((wo if n < KT else sign)[0][:, n % KT], raw[n % 2][:, :]).then_inc(s_high, 1)

            def split_o(i):
                need(act, o_in, i, 1)
                need(act, o_ready, i.before(1), 1)
                nc.scalar.copy(o_hl[0][:, :, :].rearrange("p t c -> p (t c)"), o_in_sb[i.odd][:, :]).then_inc(o_high.sem, 1)

            def fill(eng, i):
                split_o(i)

            def step(eng, i, nxt):
                need(act, ln_rs, i, 4)
                need(act, h_turned, i.before(1), 1)
                nc.scalar.activation(h[:, :], x3[i.odd][:, :], ACT.Identity, bias=ln[:, 3:4], scale=ln[:, 1:2]).then_inc(h_made.sem, 1)
                if nxt is not None:
                    split_o(nxt)
                need(act, h_turned, i, 1)
                need(act, f_ready, i.before(1), 1)
                nc.scalar.copy(hT[0][:, :, :].rearrange("p t c -> p (t c)"), t_wide[:, :]).then_inc(hT_high.sem, 1)

            schedule(fill, step)(act)

        @block.vector
        def _(dve):
            dve.wait_ge(s_scale, 16)
            nc.vector.tensor_scalar(soft[:, 4:5], soft[:, 0:1], -1.0, None, ALU.mult).then_inc(s_soft_dve, 1)
            dve.wait_ge(s_soft_dve, 1)
            nc.vector.tensor_tensor(soft[:, 1:2], soft[:, 0:1], soft[:, 4:5], ALU.max).then_inc(s_soft_dve, 1)
            dve.wait_ge(s_soft_act, 2)
            nc.vector.tensor_scalar(soft[:, 4:5], soft[:, 0:1], 0.0, soft[:, 3:4], ALU.max, ALU.add).then_inc(s_soft_dve, 1)
            for n in range(2 * KT):
                dve.wait_ge(s_high, n + 1)
                pair = wo if n < KT else sign
                nc.vector.tensor_tensor(pair[1][:, n % KT], raw[n % 2][:, :], pair[0][:, n % KT].bitcast(F32),
                                        ALU.subtract).then_inc(s_low, 1)
            dve.wait_ge(s_soft_dve, 3)

            def add_o(i):
                need(dve, o_ready, i, 1)
                need(dve, x2_in, i, 1)
                need(dve, y_made, i.before(2), 1)
                nc.vector.tensor_tensor(x3[i.odd][:, :], o_wide[:, :], x2[i.odd][:, :], ALU.add).then_inc(x3_made.sem, 1)
                need(dve, x3_made, i, 1)
                need(dve, ln_rs, i.before(1), 4)
                for half in range(2):
                    nc.vector.bn_stats(ln_stats[:, half], x3[i.odd][:, half * HALF:(half + 1) * HALF]).then_inc(ln_step.sem, 1)
                need(dve, ln_step, i, 2)
                nc.vector.memset(carrier[:, :], 0.0)
                nc.vector.bn_aggr(ln_mv[:, :], ln_stats[:, :, :]).then_inc(ln_step.sem, 1)

            def fill(eng, i):
                add_o(i)

            def step(eng, i, nxt):
                need(dve, hT_high, i, 1)
                nc.vector.tensor_tensor(hT[1][:, :, :].rearrange("p t c -> p (t c)"), t_wide[:, :],
                                        hT[0][:, :, :].rearrange("p t c -> p (t c)").bitcast(F32), ALU.subtract).then_inc(hT_low.sem, 1)
                if nxt is not None:
                    add_o(nxt)
                need(dve, f_ready, i, 1)
                need(dve, y_out, i.before(2), 1)
                nc.vector.scalar_tensor_tensor(y[i.odd][:, :], s_wide[:, :], soft[:, 4:5], x3[i.odd][:, :],
                                               ALU.mult, ALU.add).then_inc(y_made.sem, 1)

            schedule(fill, step)(dve)


_INS = ['x', 'ctx_4096', 'L0_xattn_Wq', 'L0_xattn_Wk', 'L0_xattn_Wv', 'L0_xattn_Wo', 'L0_xattn_bo', 'L0_xattn_g',
        'L0_ffn_Wq', 'L0_ffn_Wr', 'L0_ffn_aux_keys', 'L0_ffn_aux_values', 'L0_ffn_Wvd', 'L0_ffn_Wvu', 'L0_ffn_Wu1',
        'L0_ffn_bu1', 'L0_ffn_Wu2', 'L0_ffn_bu2', 'L0_ffn_gate_w1', 'L0_ffn_gate_bias', 'L0_ffn_log_rel',
        'L1_xattn_Wq', 'L1_xattn_Wk', 'L1_xattn_Wv', 'L1_xattn_Wo', 'L1_ffn_sign', 'L1_ffn_scale']


class Semaphores:

    def __init__(self):
        self.stack, self.all = ExitStack(), []

    def new(self, made):
        self.all.append(self.stack.enter_context(made))
        return self.all[-1]

    def zero_and_free(self, nc):
        nc.all_engine_barrier()
        for s in self.all:
            nc.sync.sem_clear(s)
        nc.all_engine_barrier()
        self.stack.close()


def program(nc, w, out):
    def scratch(name, width):
        return nc.dram_tensor(name, (B, P, width), F32, kind="Internal").ap()

    x1_dram, x2_dram, o_dram = scratch("x1_scratch", DM), scratch("x2_scratch", DM), scratch("o_scratch", DM)
    kv_dram = scratch("kv_scratch", 2 * KVD)
    with ExitStack() as ctx:
        keep = ctx.enter_context(nc.sbuf_tensor("x1_moments", [P, B, 2], F32))
        rows = ctx.enter_context(nc.sbuf_tensor("x1_rows", [P, B, 3], F32))
        for part, args in ((layer0_attention, (w["x"], w["ctx_4096"], w, keep, x1_dram, kv_dram)),
                           (between_layers, (keep, rows, w)),
                           (layer0_ffn_layer1_heads, (w, rows, x1_dram, kv_dram, x2_dram, o_dram)),
                           (layer1_out_and_ffn, (w, x2_dram, o_dram, out))):
            sems = Semaphores()
            part(nc, sems, *args)
            sems.zero_and_free(nc)


def kernel(**inputs):
    import numpy as _np
    import concourse.bacc as _bacc
    from concourse import mybir as _mybir
    from concourse.bass_utils import run_bass_kernel_spmd as _run

    nc = _bacc.Bacc("TRN2", target_bir_lowering=False, num_devices=1)
    arrays, args = {}, {}
    for name in _INS:
        a = _np.ascontiguousarray(inputs[name])
        if a.ndim == 0:
            a = a.reshape(1)
        arrays[f"in_{name}_dram"] = a
        args[name] = nc.dram_tensor(f"in_{name}_dram", a.shape, _mybir.dt.from_np(a.dtype), kind="ExternalInput").ap()
    out = nc.dram_tensor("out_0_dram", (B, P, DM), F32, kind="ExternalOutput").ap()
    program(nc, args, out)
    r = _run(nc, [arrays], core_ids=[0])
    return r.results[0]["out_0_dram"]
```

```python
from contextlib import ExitStack

import concourse.bass as bass
from concourse import mybir

F32 = mybir.dt.float32
F32R = mybir.dt.float32r
ALU = mybir.AluOpType
ACT = mybir.ActivationFunctionType
AX = mybir.AxisListType

P = 128
B = 32
DM = 1024
KT = DM // P
HALF = 512
EPS = 1e-5
H0, D0 = 8, 64
HD0 = H0 * D0
T0 = HD0 // P
SLOTS, BOT, RDIM, UH = 256, 64, 48, 256
TOPK = 8
TAU_LOW, TAU_HIGH, EARLY_EXIT = 0.5, 2.0, 0.05
H1, KV1, D1 = 32, 8, 32
REP = H1 // KV1
KVD = KV1 * D1
UQ = UH + BOT
MASKED = 1e30
GELU_C = 0.7978845608028654
GELU_A = 0.044715


class Batch:

    def __init__(self, pair, odd):
        self.pair, self.odd = pair, odd

    def count(self, per_batch, k):
        return self.pair * (2 * per_batch) + (self.odd * per_batch + k)

    def before(self, n):
        at = self.odd - n
        return Batch(self.pair + (at // 2) if at // 2 else self.pair, at % 2)

    def after(self):
        return Batch(self.pair + 1, 0) if self.odd else Batch(self.pair, 1)

    @property
    def index(self):
        return self.pair * 2 + self.odd


class Signal:

    def __init__(self, sem, per_batch):
        self.sem, self.per_batch = sem, per_batch


class DmaSignal:

    def __init__(self, sems, per_batch):
        self.sems, self.per_batch = sems, per_batch


def need(eng, signal, batch, k):
    if isinstance(signal, DmaSignal):
        value = batch.pair * (16 * signal.per_batch) + 16 * k
        sem = signal.sems[batch.odd]
    else:
        value = batch.count(signal.per_batch, k)
        sem = signal.sem
    if isinstance(value, int) and value <= 0:
        return
    if isinstance(batch.pair, int) and batch.pair < 0:
        return
    eng.wait_ge(sem, value)


def product(nc, out, lhs, rhs, first, last):
    nc.tensor.matmul(out, lhs[0], rhs[0], start=first, stop=False)
    nc.tensor.matmul(out, lhs[0], rhs[1], start=False, stop=False)
    return nc.tensor.matmul(out, lhs[1], rhs[0], start=False, stop=last)


def make_identity(nc, eng, ident, made):
    nc.gpsimd.memset(ident[:, :], 0.0).then_inc(made, 1)
    eng.wait_ge(made, 1)
    nc.gpsimd.affine_select(out=ident[:, :], in_=ident[:, :], compare_op=ALU.not_equal, fill=1.0, base=0,
                            pattern=[[-1, P]], channel_multiplier=1).then_inc(made, 1)


def layer0_attention(nc, sems, x, ctx_in, w, keep, x1_dram, kv_dram):
    with ExitStack() as ctx:
        def sb(name, shape, dt=F32):
            return ctx.enter_context(nc.sbuf_tensor(f"a_{name}", shape, dt))

        def sem(name):
            return sems.new(nc.semaphore(f"a_{name}"))

        def signal(name, n):
            return Signal(sem(name), n)

        def dma_signal(name, n=1):
            return DmaSignal([sem(f"{name}_{p}") for p in "eo"], n)

        def both(name, shape):
            return sb(f"{name}_hi", shape, F32R), sb(f"{name}_lo", shape, F32R)

        bank = [ctx.enter_context(nc.psum_tensor(f"a_ps{i}", [P, HALF], F32)) for i in range(8)]

        ident = sb("ident", [P, P])
        ones = sb("ones", [P, P])
        w_rows = sb("w_rows", [P, 4, T0, P])
        wqT = both("wqT", [P, HD0])
        wkT = both("wkT", [P, HD0])
        woT = sb("woT", [P, T0, P])
        vo = sb("vo", [P, H0, P])
        wkv_raw = sb("wkv_raw", [P, KT, 2 * KVD])
        wkv = both("wkv", [P, KT, 2 * KVD])
        bo = sb("bo", [P, 1])
        g = sb("g", [P, 1])
        g_scaled = sb("g_scaled", [P, 1])
        minus_half = sb("minus_half", [P, KT])
        consts = sb("consts", [P, 2])
        carrier = sb("carrier", [P, 1])

        x_sb = [sb(f"x{p}", [P, DM]) for p in range(2)]
        ctx_sb = [sb(f"ctx{p}", [P, DM]) for p in range(2)]
        ctx_hl = both("ctx_hl", [P, DM])
        ctxT = sb("ctxT", [P, KT, P])
        ctxT_hl = both("ctxT_hl", [P, KT, P])
        xn = sb("xn", [P, DM])
        xn_hl = both("xn_hl", [P, DM])
        ln_stats = sb("ln_stats", [P, 2, 6])
        ln_mv = sb("ln_mv", [P, 2])
        ln_ve = sb("ln_ve", [P, 1])
        ln_r = sb("ln_r", [P, 1])
        ln_nmr = sb("ln_nmr", [P, 1])
        k_two = sb("k_two", [P, 2 * T0])
        k_half = [sb(f"k_half{p}", [P, 2, T0]) for p in range(2)]
        x1_mv = [sb(f"x1_mv{p}", [P, 2]) for p in range(2)]
        k_neg = sb("k_neg", [P, T0])
        k_sum = [sb(f"k_sum{p}", [P, T0]) for p in range(2)]
        k_inv = sb("k_inv", [P, T0])
        k_exp = sb("k_exp", [P, T0, DM])
        k_expT = [sb(f"k_expT{r}", [P, HD0]) for r in range(3)]
        kv_sb = [sb(f"kv{p}", [P, 2 * KVD]) for p in range(2)]
        q_max = [sb(f"q_max{r}", [P, H0]) for r in range(2)]
        q_sm = [sb(f"q_sm{r}", [P, HD0]) for r in range(4)]
        q_sum = [sb(f"q_sum{r}", [P, H0]) for r in range(2)]
        q_inv = [sb(f"q_inv{r}", [P, H0]) for r in range(2)]
        q_T = sb("q_T", [P, T0, DM])
        c_sb = sb("c_sb", [P, HD0])
        mix = sb("mix", [P, T0, P])
        o_sb = sb("o_sb", [P, DM])
        sq = sb("sq", [P, DM])
        n_max = sb("n_max", [P, KT])
        n_inv = sb("n_inv", [P, KT])
        n_diag = sb("n_diag", [P, KT, P])
        x1_sb = [sb(f"x1_{p}", [P, DM]) for p in range(2)]
        x1_stats = sb("x1_stats", [P, 2, 6])

        s_load = sem("weights_loaded")
        s_ident = sem("ident_made")
        s_const = sem("constants_made")
        s_wT = sem("weights_transposed")
        s_wev = sem("weights_copied")
        s_whi = sem("weights_high")
        s_wlo = sem("weights_low")
        s_vo = sem("vo_made")

        x_in = dma_signal("x_in")
        ctx_read = dma_signal("ctx_in")
        x1_out = dma_signal("x1_out")
        kv_out = dma_signal("kv_out")
        ln_step = signal("ln_step", 3)
        ln_rs = signal("ln_rs", 3)
        ln_nm = signal("ln_nm", 1)
        xn_made = signal("xn_made", 2)
        xn_low = signal("xn_low", 1)
        ctx_high = signal("ctx_high", 1)
        ctx_low = signal("ctx_low", 2)
        ctx_turned = signal("ctx_turned", 2)
        ctxT_copied = signal("ctxT_copied", 2)
        ctxT_split = signal("ctxT_split", 2)
        k_ready = signal("k_ready", T0)
        k_maxed = signal("k_maxed", T0)
        k_negated = signal("k_negated", T0)
        k_exped = signal("k_exped", T0)
        kv_ready = signal("kv_ready", 1)
        kv_copied = signal("kv_copied", 1)
        q_ready = signal("q_ready", KT)
        q_maxed = signal("q_maxed", KT)
        q_less = signal("q_less", KT)
        q_exped = signal("q_exped", KT)
        q_summed = signal("q_summed", KT)
        q_inverted = signal("q_inverted", KT)
        q_normed = signal("q_normed", KT)
        q_turned = signal("q_turned", KT)
        q_stored = signal("q_stored", KT)
        kx_turned = signal("kx_turned", KT)
        kx_stored = signal("kx_stored", KT)
        c_step = signal("c_step", KT)
        c_copied = signal("c_copied", 1)
        k_inverted = signal("k_inverted", 2)
        mix_ready = signal("mix_ready", 1)
        mix_scaled = signal("mix_scaled", 1)
        o_ready = signal("o_ready", 2)
        o_biased = signal("o_biased", 2)
        o_squared = signal("o_squared", 2)
        n_ready = signal("n_ready", 1)
        n_floored = signal("n_floored", 1)
        n_powed = signal("n_powed", 1)
        n_placed = signal("n_placed", 1)
        n_spread = signal("n_spread", 2)
        o_normed = signal("o_normed", 2)
        x1_added = signal("x1_added", 1)
        x1_seen = signal("x1_seen", 3)

        Q_LAG = 3
        C_LAG = 2

        block = ctx.enter_context(nc.Block())

        def schedule(front, middle, tail, finish):
            def run(eng):
                def one(i, before, after):
                    middle(eng, i, before, after)
                    tail(eng, i, before, after)

                front(eng, Batch(0, 0))
                one(Batch(0, 0), None, Batch(0, 1))
                one(Batch(0, 1), Batch(0, 0), Batch(1, 0))
                with eng.Fori(1, B // 2 - 1) as pair:
                    one(Batch(pair, 0), Batch(pair, 0).before(1), Batch(pair, 1))
                    one(Batch(pair, 1), Batch(pair, 0), Batch(pair + 1, 0))
                last = B // 2 - 1
                one(Batch(last, 0), Batch(last - 1, 1), Batch(last, 1))
                one(Batch(last, 1), Batch(last, 0), None)
                finish(eng, Batch(last, 1))
            return run

        @block.sync
        def _(sp):
            for n, name in enumerate(("L0_xattn_Wq", "L0_xattn_Wk", "L0_xattn_Wv")):
                sp.dma_start(w_rows[:, n], w[name].rearrange("(t p) c -> p t c", p=P)).then_inc(s_load, 16)
            sp.dma_start(w_rows[:, 3], w["L0_xattn_Wo"].rearrange("o (t e) -> o t e", e=P)).then_inc(s_load, 16)
            sp.dma_start(wkv_raw[:, :, 0:KVD], w["L1_xattn_Wk"].rearrange("(t p) m -> p t m", p=P)).then_inc(s_load, 16)
            sp.dma_start(wkv_raw[:, :, KVD:2 * KVD], w["L1_xattn_Wv"].rearrange("(t p) m -> p t m", p=P)).then_inc(s_load, 16)
            sp.dma_start(bo[:, :], w["L0_xattn_bo"].rearrange("(p a) -> p a", a=1)).then_inc(s_load, 16)
            sp.dma_start(g[:, :], w["L0_xattn_g"].rearrange("a p b -> p (a b)")).then_inc(s_load, 16)

            def load_x(i):
                need(sp, x1_added, i.before(2), 1)
                sp.dma_start(x_sb[i.odd][:, :], x[i.index]).then_inc(x_in.sems[i.odd], 16)

            def load_ctx(i):
                need(sp, ctx_low, i.before(2), 2)
                need(sp, ctx_turned, i.before(2), 2)
                sp.dma_start(ctx_sb[i.odd][:, :], ctx_in[i.index]).then_inc(ctx_read.sems[i.odd], 16)

            def store_kv(i):
                need(sp, kv_copied, i, 1)
                sp.dma_start(kv_dram[i.index], kv_sb[i.odd][:, :]).then_inc(kv_out.sems[i.odd], 16)

            def store_x1(i):
                need(sp, x1_added, i, 1)
                sp.dma_start(x1_dram[i.index], x1_sb[i.odd][:, :]).then_inc(x1_out.sems[i.odd], 16)

            def one(i, loads, stores_kv):
                if loads:
                    load_ctx(i.after().after())
                if stores_kv:
                    store_kv(i.after())
                store_x1(i)
                if loads:
                    load_x(i.after().after())

            for i in (Batch(0, 0), Batch(0, 1)):
                load_ctx(i)
                load_x(i)
            store_kv(Batch(0, 0))
            with sp.Fori(0, B // 2 - 1) as pair:
                one(Batch(pair, 0), True, True)
                one(Batch(pair, 1), True, True)
            one(Batch(B // 2 - 1, 0), False, True)
            one(Batch(B // 2 - 1, 1), False, False)
            for p in range(2):
                sp.wait_ge(x1_out.sems[p], 16 * (B // 2))
                sp.wait_ge(kv_out.sems[p], 16 * (B // 2))

        @block.gpsimd
        def _(pool):
            make_identity(nc, pool, ident, s_ident)
            nc.gpsimd.memset(ones[:, :], 1.0).then_inc(s_const, 1)
            nc.gpsimd.memset(minus_half[:, :], -0.5).then_inc(s_const, 1)
            nc.gpsimd.memset(consts[:, 0:1], EPS).then_inc(s_const, 1)
            nc.gpsimd.memset(consts[:, 1:2], -1.0).then_inc(s_const, 1)
            pool.wait_ge(s_load, 16 * 8)
            nc.gpsimd.tensor_scalar(g_scaled[:, :], g[:, :], float(P) ** 0.5, None, ALU.mult).then_inc(s_const, 1)
            pool.wait_ge(s_const, 5)

            def row_scale(i):
                need(pool, ln_step, i, 3)
                need(pool, xn_made, i.before(1), 2)
                nc.gpsimd.tensor_tensor(ln_ve[:, :], ln_mv[:, 1:2], consts[:, 0:1], ALU.add).then_inc(ln_rs.sem, 1)
                need(pool, ln_rs, i, 1)
                nc.gpsimd.tensor_tensor(ln_r[:, :], ln_ve[:, :], minus_half[:, 0:1], ALU.pow).then_inc(ln_rs.sem, 1)
                need(pool, ln_rs, i, 2)
                nc.gpsimd.tensor_tensor(ln_nmr[:, :], ln_mv[:, 0:1], consts[:, 1:2], ALU.mult).then_inc(ln_rs.sem, 1)
                need(pool, ln_rs, i, 3)
                nc.gpsimd.tensor_tensor(ln_nmr[:, :], ln_nmr[:, :], ln_r[:, :], ALU.mult).then_inc(ln_nm.sem, 1)

            def low_ctx(i, half):
                need(pool, ctx_high, i, 1)
                need(pool, k_ready, i.before(1), T0)
                cols = slice(half * HALF, (half + 1) * HALF)
                nc.gpsimd.tensor_tensor(ctx_hl[1][:, cols], ctx_sb[i.odd][:, cols], ctx_hl[0][:, cols].bitcast(F32),
                                        ALU.subtract).then_inc(ctx_low.sem, 1)

            def low_xn(i):
                need(pool, xn_made, i, 2)
                need(pool, q_ready, i.before(1), KT)
                nc.gpsimd.tensor_tensor(xn_hl[1][:, :], xn[:, :], xn_hl[0][:, :].bitcast(F32),
                                        ALU.subtract).then_inc(xn_low.sem, 1)

            def front(eng, i):
                low_ctx(i, 0)
                low_ctx(i, 1)
                row_scale(i)
                low_xn(i)

            def middle(eng, i, before, after):
                for m in range(KT):
                    need(pool, q_inverted, i, m + 1)
                    sm = q_sm[m % 4][:, :].rearrange("p (h d) -> p h d", d=D0)
                    nc.gpsimd.tensor_tensor(sm, sm, q_inv[m % 2][:, :].unsqueeze(2).to_broadcast([P, H0, D0]),
                                            ALU.mult).then_inc(q_normed.sem, 1)
                    if after is not None and m in (2, 4):
                        low_ctx(after, m // 4)

            def tail(eng, i, before, after):
                if after is not None:
                    row_scale(after)
                    low_xn(after)
                need(pool, n_floored, i, 1)
                nc.gpsimd.tensor_tensor(n_inv[:, :], n_max[:, :], minus_half[:, :], ALU.pow).then_inc(n_powed.sem, 1)

            def finish(eng, i):
                pass

            schedule(front, middle, tail, finish)(pool)

        @block.tensor
        def _(pe):
            pe.wait_ge(s_load, 16 * 8)
            pe.wait_ge(s_ident, 2)
            for n, at in ((0, 0), (1, 1), (3, 2)):
                for t in range(T0):
                    mm = nc.tensor.transpose(bank[at][:, t * P:(t + 1) * P], w_rows[:, n, t], ident[:, :])
                mm.then_inc(s_wT, 1)
            pe.wait_ge(s_wev, 1)
            for h in range(H0):
                lo = D0 * (h % 2)
                mm = nc.tensor.matmul(bank[4 + h % 2][:, (h // 2) * P:(h // 2 + 1) * P], w_rows[lo:lo + D0, 2, h // 2],
                                      woT[lo:lo + D0, h // 2], start=True, stop=True)
            mm.then_inc(s_wT, 1)
            pe.wait_ge(s_whi, 3)
            pe.wait_ge(s_wlo, 3)
            pe.wait_ge(s_vo, 2)

            def turn_ctx(i, half):
                need(pe, ctx_read, i, 1)
                need(pe, q_less, i.before(1), KT)
                for j in range(4 * half, 4 * half + 4):
                    mm = nc.tensor.transpose(bank[half][:, (j % 4) * P:(j % 4 + 1) * P],
                                             ctx_sb[i.odd][:, j * P:(j + 1) * P], ident[:, :])
                mm.then_inc(ctx_turned.sem, 1)

            def make_k(i, t):
                pair = 2 - 2 * (t % 2)
                if t == 0:
                    need(pe, ctx_low, i, 2)
                    need(pe, kx_stored, i.before(1), KT)
                elif t == 1:
                    need(pe, ctxT_copied, i, 2)
                else:
                    need(pe, k_exped, i, t - 1)
                for half in range(2):
                    cols = slice(half * HALF, (half + 1) * HALF)
                    mm = product(nc, bank[pair + half][:, :], [m[:, t * P:(t + 1) * P] for m in wkT],
                                 [m[:, cols] for m in ctx_hl], True, True)
                mm.then_inc(k_ready.sem, 1)

            def make_kv(i, tiles):
                if tiles[0] == 0:
                    need(pe, ctxT_split, i, 2)
                    need(pe, kv_copied, i.before(1), 1)
                for j in tiles:
                    mm = product(nc, bank[5][:, :], [m[:, j] for m in ctxT_hl], [m[:, j] for m in wkv],
                                 j == 0, j == KT - 1)
                if tiles[-1] == KT - 1:
                    mm.then_inc(kv_ready.sem, 1)

            def add_to_c(i, m):
                need(pe, kx_stored, i, m + 1)
                if m == 0:
                    need(pe, o_normed, i.before(1), 1)
                nc.tensor.matmul(bank[4][:, :], ctxT[:, m], k_expT[m % 3][:, :], start=(m == 0),
                                 stop=(m == KT - 1)).then_inc(c_step.sem, 1)

            def turn_q(i, m):
                need(pe, q_normed, i, m + 1)
                if m < 2:
                    need(pe, o_normed, i.before(1), 2)
                else:
                    need(pe, q_stored, i, m - 1)
                for t in range(T0):
                    mm = nc.tensor.transpose(bank[6 + m % 2][:, t * P:(t + 1) * P],
                                             q_sm[m % 4][:, t * P:(t + 1) * P], ident[:, :])
                mm.then_inc(q_turned.sem, 1)

            def mix_heads(i):
                need(pe, c_copied, i, 1)
                for h in range(H0):
                    lo = D0 * (h % 2)
                    mm = nc.tensor.matmul(bank[4][lo:lo + D0, (h // 2) * P:(h // 2 + 1) * P],
                                          c_sb[:, h * D0:(h + 1) * D0], vo[:, h], start=True, stop=True)
                mm.then_inc(mix_ready.sem, 1)

            def make_out(i, half):
                need(pe, q_stored, i, KT)
                need(pe, mix_scaled, i, 1)
                cols = slice(half * HALF, (half + 1) * HALF)
                for t in range(T0):
                    mm = nc.tensor.matmul(bank[6 + half][:, :], mix[:, t], q_T[:, t, cols], start=(t == 0),
                                          stop=(t == T0 - 1))
                mm.then_inc(o_ready.sem, 1)

            def sum_squares(i):
                need(pe, o_squared, i, 2)
                for j in range(KT):
                    mm = nc.tensor.matmul(bank[4][:, j:j + 1], sq[:, j * P:(j + 1) * P], ones[:, 0:1], start=True, stop=True)
                mm.then_inc(n_ready.sem, 1)

            def spread_norms(i):
                need(pe, n_placed, i, 1)
                for half in range(2):
                    nc.tensor.matmul(bank[4 + 2 * half][:, :], ones[:, :],
                                     n_diag[:, 4 * half:4 * half + 4].rearrange("p a b -> p (a b)"),
                                     start=True, stop=True).then_inc(n_spread.sem, 1)

            def front(eng, i):
                for half in range(2):
                    turn_ctx(i, half)
                for t in range(T0):
                    make_k(i, t)
                    make_kv(i, (2 * t, 2 * t + 1))

            def middle(eng, i, before, after):
                need(pe, xn_low, i, 1)
                need(pe, k_exped, i, T0)
                for j in range(KT):
                    if j >= 2:
                        need(pe, q_less, i, j - 1)
                    mm = product(nc, bank[j % 2][:, :], [m[:, j * P:(j + 1) * P] for m in xn_hl],
                                 [m[:, :] for m in wqT], True, True)
                    mm.then_inc(q_ready.sem, 1)
                    if j == 0 and before is not None:
                        spread_norms(before)
                    if j >= 2:
                        need(pe, kx_stored, i, j - 1)
                    for t in range(T0):
                        mm = nc.tensor.transpose(bank[2 + j % 2][:, t * P:(t + 1) * P],
                                                 k_exp[:, t, j * P:(j + 1) * P], ident[:, :])
                    mm.then_inc(kx_turned.sem, 1)
                    if j >= C_LAG:
                        add_to_c(i, j - C_LAG)
                    if j >= Q_LAG:
                        turn_q(i, j - Q_LAG)

            def tail(eng, i, before, after):
                for m in range(KT - C_LAG, KT):
                    add_to_c(i, m)
                for n, m in enumerate(range(KT - Q_LAG, KT)):
                    if after is not None:
                        if n < 2:
                            turn_ctx(after, n)
                        else:
                            make_k(after, 0)
                    turn_q(i, m)
                mix_heads(i)
                if after is not None:
                    make_k(after, 1)
                if after is not None:
                    make_kv(after, (0, 1))
                make_out(i, 0)
                if after is not None:
                    make_k(after, 2)
                make_out(i, 1)
                if after is not None:
                    make_kv(after, (2, 3))
                    make_k(after, 3)
                sum_squares(i)
                if after is not None:
                    make_kv(after, (4, 5, 6, 7))

            def finish(eng, i):
                spread_norms(i)

            schedule(front, middle, tail, finish)(pe)

        @block.scalar
        def _(act):
            act.wait_ge(s_load, 16 * 8)
            act.wait_ge(s_wT, 1)
            nc.scalar.copy(wqT[0][:, :], bank[0][:, :]).then_inc(s_whi, 1)
            act.wait_ge(s_wT, 2)
            nc.scalar.copy(wkT[0][:, :], bank[1][:, :]).then_inc(s_whi, 1)
            act.wait_ge(s_wT, 3)
            nc.scalar.copy(woT[:, :, :].rearrange("p t o -> p (t o)"), bank[2][:, :]).then_inc(s_wev, 1)
            nc.scalar.copy(wkv[0][:, :, :], wkv_raw[:, :, :]).then_inc(s_whi, 1)
            act.wait_ge(s_wT, 4)
            for n in range(2):
                nc.scalar.copy(vo[:, n::2], bank[4 + n][:, :].rearrange("p (h o) -> p h o", o=P)).then_inc(s_vo, 1)

            def high_ctx(i):
                need(act, ctx_read, i, 1)
                need(act, k_ready, i.before(1), T0)
                nc.scalar.copy(ctx_hl[0][:, :], ctx_sb[i.odd][:, :]).then_inc(ctx_high.sem, 1)

            def copy_ctxT(i, half):
                need(act, c_step, i.before(1), KT)
                need(act, ctxT_split, i.before(1), 2)
                need(act, ctx_turned, i, half + 1)
                nc.scalar.copy(ctxT[:, 4 * half:4 * half + 4].rearrange("p a b -> p (a b)"),
                               bank[half][:, :]).then_inc(ctxT_copied.sem, 1)

            def make_xn(i):
                need(act, ln_nm, i, 1)
                need(act, x_in, i, 1)
                need(act, xn_low, i.before(1), 1)
                nc.scalar.activation(xn[:, :], x_sb[i.odd][:, :], ACT.Identity, bias=ln_nmr[:, :],
                                     scale=ln_r[:, :]).then_inc(xn_made.sem, 1)
                need(act, q_ready, i.before(1), KT)
                nc.scalar.activation(xn_hl[0][:, :], x_sb[i.odd][:, :], ACT.Identity, bias=ln_nmr[:, :],
                                     scale=ln_r[:, :]).then_inc(xn_made.sem, 1)

            def exp_k(i, t):
                pair = 2 - 2 * (t % 2)
                need(act, kx_turned, i.before(1), KT)
                need(act, k_negated, i, t + 1)
                need(act, k_inverted, i.before(2), 2)
                nc.scalar.activation(k_exp[:, t, 0:HALF], bank[pair][:, :], ACT.Exp, bias=k_neg[:, t:t + 1],
                                     accum_out=k_half[i.odd][:, 0, t:t + 1])
                nc.scalar.activation(k_exp[:, t, HALF:DM], bank[pair + 1][:, :], ACT.Exp, bias=k_neg[:, t:t + 1],
                                     accum_out=k_half[i.odd][:, 1, t:t + 1]).then_inc(k_exped.sem, 1)

            def copy_kv(i):
                need(act, kv_ready, i, 1)
                need(act, kv_out, i.before(2), 1)
                nc.scalar.copy(kv_sb[i.odd][:, :], bank[5][:, :]).then_inc(kv_copied.sem, 1)

            def copy_q(i, m):
                need(act, q_turned, i, m + 1)
                if m == 0:
                    need(act, o_ready, i.before(1), 2)
                nc.scalar.copy(q_T[:, :, m * P:(m + 1) * P],
                               bank[6 + m % 2][:, :].rearrange("p (t n) -> p t n", t=T0)).then_inc(q_stored.sem, 1)

            def bias_and_square(i, half):
                cols = slice(half * HALF, (half + 1) * HALF)
                need(act, o_ready, i, half + 1)
                if half == 0:
                    need(act, x1_added, i.before(1), 1)
                    need(act, n_ready, i.before(1), 1)
                nc.scalar.activation(sq[:, cols], bank[6 + half][:, :], ACT.Square, bias=bo[:, :]).then_inc(o_squared.sem, 1)
                nc.scalar.activation(o_sb[:, cols], bank[6 + half][:, :], ACT.Identity, bias=bo[:, :]).then_inc(o_biased.sem, 1)

            def front(eng, i):
                high_ctx(i)
                for half in range(2):
                    copy_ctxT(i, half)
                make_xn(i)
                for t in range(T0):
                    exp_k(i, t)
                copy_kv(i)

            def middle(eng, i, before, after):
                for j in range(KT):
                    need(act, kx_turned, i, j + 1)
                    if j < 3:
                        need(act, c_step, i.before(1), KT)
                    else:
                        need(act, c_step, i, j - 2)
                    nc.scalar.copy(k_expT[j % 3][:, :], bank[2 + j % 2][:, :]).then_inc(kx_stored.sem, 1)
                    need(act, q_less, i, j + 1)
                    nc.scalar.activation(q_sm[j % 4][:, :], q_sm[j % 4][:, :], ACT.Exp).then_inc(q_exped.sem, 1)
                    if j >= Q_LAG:
                        copy_q(i, j - Q_LAG)
                    elif j == 1 and after is not None:
                        high_ctx(after)

            def tail(eng, i, before, after):
                for n, m in enumerate(range(KT - Q_LAG, KT)):
                    if after is not None and n < 2:
                        copy_ctxT(after, n)
                    copy_q(i, m)
                    if n == 0:
                        need(act, c_step, i, KT)
                        need(act, mix_ready, i.before(1), 1)
                        nc.scalar.copy(c_sb[:, :], bank[4][:, :]).then_inc(c_copied.sem, 1)
                if after is not None:
                    exp_k(after, 0)
                    exp_k(after, 1)
                    make_xn(after)
                bias_and_square(i, 0)
                if after is not None:
                    exp_k(after, 2)
                bias_and_square(i, 1)
                if after is not None:
                    exp_k(after, 3)
                    copy_kv(after)

            def finish(eng, i):
                pass

            schedule(front, middle, tail, finish)(act)

        @block.vector
        def _(dve):
            dve.wait_ge(s_whi, 1)
            nc.vector.tensor_tensor(wqT[1][:, :], bank[0][:, :], wqT[0][:, :].bitcast(F32), ALU.subtract).then_inc(s_wlo, 1)
            dve.wait_ge(s_whi, 2)
            nc.vector.tensor_tensor(wkT[1][:, :], bank[1][:, :], wkT[0][:, :].bitcast(F32), ALU.subtract).then_inc(s_wlo, 1)
            dve.wait_ge(s_whi, 3)
            nc.vector.tensor_tensor(wkv[1][:, :, :], wkv_raw[:, :, :], wkv[0][:, :, :].bitcast(F32), ALU.subtract).then_inc(s_wlo, 1)
            dve.wait_ge(s_const, 5)

            def row_stats(i):
                need(dve, x_in, i, 1)
                need(dve, ln_nm, i.before(1), 1)
                for half in range(2):
                    nc.vector.bn_stats(ln_stats[:, half], x_sb[i.odd][:, half * HALF:(half + 1) * HALF]).then_inc(ln_step.sem, 1)
                need(dve, ln_step, i, 2)
                nc.vector.memset(carrier[:, :], 0.0)
                nc.vector.bn_aggr(ln_mv[:, :], ln_stats[:, :, :]).then_inc(ln_step.sem, 1)

            def split_ctxT(i):
                need(dve, ctxT_copied, i, 2)
                need(dve, kv_ready, i.before(1), 1)
                nc.vector.tensor_copy(ctxT_hl[0][:, :, :], ctxT[:, :, :]).then_inc(ctxT_split.sem, 1)
                need(dve, ctxT_split, i, 1)
                nc.vector.tensor_tensor(ctxT_hl[1][:, :, :], ctxT[:, :, :], ctxT_hl[0][:, :, :].bitcast(F32),
                                        ALU.subtract).then_inc(ctxT_split.sem, 1)

            def max_k(i, t):
                pair = 2 - 2 * (t % 2)
                need(dve, k_ready, i, t + 1)
                need(dve, k_exped, i.before(1), t + 1)
                nc.vector.tensor_reduce(k_two[:, 2 * t:2 * t + 1], bank[pair][:, :], AX.X, ALU.max)
                nc.vector.tensor_reduce(k_two[:, 2 * t + 1:2 * t + 2], bank[pair + 1][:, :], AX.X, ALU.max).then_inc(k_maxed.sem, 1)
                need(dve, k_maxed, i, t + 1)
                nc.vector.tensor_scalar(k_neg[:, t:t + 1], k_two[:, 2 * t:2 * t + 1], k_two[:, 2 * t + 1:2 * t + 2],
                                        -1.0, ALU.max, ALU.mult).then_inc(k_negated.sem, 1)

            def invert_k_sums(i):
                need(dve, k_exped, i, T0)
                nc.vector.tensor_tensor(k_sum[i.odd][:, :], k_half[i.odd][:, 0], k_half[i.odd][:, 1], ALU.add).then_inc(k_inverted.sem, 1)
                need(dve, k_inverted, i, 1)
                need(dve, mix_scaled, i.before(1), 1)
                nc.vector.reciprocal(k_inv[:, :], k_sum[i.odd][:, :]).then_inc(k_inverted.sem, 1)

            def norm_and_add(i):
                for half in range(2):
                    cols = slice(half * HALF, (half + 1) * HALF)
                    need(dve, n_spread, i, half + 1)
                    need(dve, o_biased, i, half + 1)
                    nc.vector.scalar_tensor_tensor(o_sb[:, cols], o_sb[:, cols], g_scaled[:, :], bank[4 + 2 * half][:, :],
                                                   ALU.mult, ALU.mult).then_inc(o_normed.sem, 1)

            def add_x(i):
                need(dve, o_normed, i, 2)
                need(dve, x1_out, i.before(2), 1)
                nc.vector.tensor_tensor(x1_sb[i.odd][:, :], x_sb[i.odd][:, :], o_sb[:, :], ALU.add).then_inc(x1_added.sem, 1)

            def x1_row_stats(i):
                need(dve, x1_added, i, 1)
                for half in range(2):
                    nc.vector.bn_stats(x1_stats[:, half], x1_sb[i.odd][:, half * HALF:(half + 1) * HALF]).then_inc(x1_seen.sem, 1)
                need(dve, x1_seen, i, 2)
                nc.vector.memset(carrier[:, :], 0.0)
                nc.vector.bn_aggr(x1_mv[i.odd][:, :], x1_stats[:, :, :]).then_inc(x1_seen.sem, 1)
                need(dve, x1_seen, i, 3)
                nc.vector.tensor_copy(keep[:, i_slice(i), :], x1_mv[i.odd][:, :].unsqueeze(1))

            def front(eng, i):
                row_stats(i)
                split_ctxT(i)
                for t in range(T0):
                    max_k(i, t)

            def middle(eng, i, before, after):
                for j in range(KT + 1):
                    if j < KT:
                        need(dve, q_ready, i, j + 1)
                        qv = bank[j % 2][:, :].rearrange("p (h d) -> p h d", d=D0)
                        nc.vector.tensor_reduce(q_max[j % 2][:, :], qv, AX.X, ALU.max).then_inc(q_maxed.sem, 1)
                        need(dve, q_maxed, i, j + 1)
                        if j < 4:
                            need(dve, q_turned, i.before(1), KT)
                        else:
                            need(dve, q_turned, i, j - 3)
                        nc.vector.tensor_tensor(q_sm[j % 4][:, :].rearrange("p (h d) -> p h d", d=D0), qv,
                                                q_max[j % 2][:, :].unsqueeze(2).to_broadcast([P, H0, D0]),
                                                ALU.subtract).then_inc(q_less.sem, 1)
                    if before is not None and j == 0:
                        norm_and_add(before)
                    if before is not None and j == 1:
                        add_x(before)
                    if j >= 1:
                        m = j - 1
                        need(dve, q_exped, i, m + 1)
                        nc.vector.tensor_reduce(q_sum[m % 2][:, :], q_sm[m % 4][:, :].rearrange("p (h d) -> p h d", d=D0),
                                                AX.X, ALU.add).then_inc(q_summed.sem, 1)
                        need(dve, q_summed, i, m + 1)
                        if m >= 2:
                            need(dve, q_normed, i, m - 1)
                        nc.vector.reciprocal(q_inv[m % 2][:, :], q_sum[m % 2][:, :]).then_inc(q_inverted.sem, 1)
                    if j == 3:
                        invert_k_sums(i)

            def tail(eng, i, before, after):
                if after is not None:
                    row_stats(after)
                    split_ctxT(after)
                    max_k(after, 0)
                need(dve, mix_ready, i, 1)
                need(dve, k_inverted, i, 2)
                need(dve, o_ready, i.before(1), 2)
                for t in range(T0):
                    op = nc.vector.tensor_scalar(mix[:, t], bank[4][:, t * P:(t + 1) * P], k_inv[:, t:t + 1],
                                                 float(D0) ** -0.5, ALU.mult, ALU.mult)
                op.then_inc(mix_scaled.sem, 1)
                if after is not None:
                    max_k(after, 1)
                if before is not None:
                    x1_row_stats(before)
                if after is not None:
                    for t in range(2, T0):
                        max_k(after, t)
                need(dve, n_ready, i, 1)
                nc.vector.tensor_scalar(n_max[:, :], bank[4][:, 0:KT], 1e-24, None, ALU.max).then_inc(n_floored.sem, 1)
                need(dve, n_powed, i, 1)
                need(dve, n_spread, i.before(1), 2)
                nc.vector.tensor_tensor(n_diag[:, :, :], ident[:, :].unsqueeze(1).to_broadcast([P, KT, P]),
                                        n_inv[:, :].unsqueeze(2).to_broadcast([P, KT, P]), ALU.mult).then_inc(n_placed.sem, 1)

            def finish(eng, i):
                norm_and_add(i)
                add_x(i)
                x1_row_stats(i)

            def i_slice(i):
                return bass.ds(i.index, 1) if not isinstance(i.pair, int) else slice(i.index, i.index + 1)

            schedule(front, middle, tail, finish)(dve)


def row_moments(nc, sb, sem, total, ones, keep, rows):
    var_eps = sb("var_eps", [P, B])
    minus_half = sb("minus_half", [P, B])
    inv_var = sb("inv_var", [P, B])
    var_n = sb("var_n", [P, B])
    log_var = sb("log_var", [P, B])
    log_sum = sb("log_sum", [P, 1])
    mean_n = sb("mean_n", [P, 1])
    inv_mean = sb("inv_mean", [P, 1])
    s_pool, s_dve, s_act, s_pe = sem("moments_pool"), sem("moments_dve"), sem("moments_act"), sem("moments_pe")

    def on_pool(pool):
        nc.gpsimd.memset(minus_half[:, :], -0.5).then_inc(s_pool, 1)
        nc.gpsimd.memset(ones[:, :], 1.0).then_inc(s_pool, 1)
        pool.wait_ge(s_pool, 2)
        pool.wait_ge(s_dve, 1)
        nc.gpsimd.tensor_tensor(rows[:, :, 0], var_eps[:, :], minus_half[:, :], ALU.pow).then_inc(s_pool, 1)

    def on_dve(dve):
        nc.vector.tensor_scalar(var_eps[:, :], keep[:, :, 1], EPS, None, ALU.add).then_inc(s_dve, 1)
        dve.wait_ge(s_dve, 1)
        nc.vector.reciprocal(inv_var[:, :], var_eps[:, :]).then_inc(s_dve, 1)
        dve.wait_ge(s_dve, 2)
        nc.vector.tensor_tensor(var_n[:, :], keep[:, :, 1], inv_var[:, :], ALU.mult).then_inc(s_dve, 1)
        dve.wait_ge(s_pool, 3)
        nc.vector.scalar_tensor_tensor(rows[:, :, 1], keep[:, :, 0], -1.0, rows[:, :, 0], ALU.mult, ALU.mult).then_inc(s_dve, 1)
        dve.wait_ge(s_pe, 1)
        nc.vector.tensor_scalar(mean_n[:, :], total, 1.0 / (B * P), 1e-6, ALU.mult, ALU.add).then_inc(s_dve, 1)
        dve.wait_ge(s_dve, 5)
        nc.vector.reciprocal(inv_mean[:, :], mean_n[:, :]).then_inc(s_dve, 1)
        dve.wait_ge(s_dve, 6)
        nc.vector.tensor_scalar(rows[:, :, 2], log_var[:, :], inv_mean[:, :], 0.5, ALU.mult, ALU.mult).then_inc(s_dve, 1)
        dve.wait_ge(s_dve, 7)

    def on_act(act):
        act.wait_ge(s_dve, 3)
        nc.scalar.activation(log_var[:, :], var_n[:, :], ACT.Ln, bias=1.0, accum_out=log_sum[:, :]).then_inc(s_act, 1)

    def on_pe(pe):
        pe.wait_ge(s_act, 1)
        pe.wait_ge(s_pool, 2)
        nc.tensor.matmul(total, ones[:, :], log_sum[:, :], start=True, stop=True).then_inc(s_pe, 1)

    return on_pool, on_dve, on_act, on_pe


def layer0_ffn_layer1_heads(nc, sems, w, keep, rows, x1_dram, kv_dram, x2_dram, o_dram):
    with ExitStack() as ctx:
        def sb(name, shape, dt=F32):
            return ctx.enter_context(nc.sbuf_tensor(f"b_{name}", shape, dt))

        def sem(name):
            return sems.new(nc.semaphore(f"b_{name}"))

        def signal(name, n):
            return Signal(sem(name), n)

        def dma_signal(name, n=1):
            return DmaSignal([sem(f"{name}_{p}") for p in "eo"], n)

        def both(name, shape):
            return sb(f"{name}_hi", shape, F32R), sb(f"{name}_lo", shape, F32R)

        score_bank = [ctx.enter_context(nc.psum_tensor(f"b_score{i}", [P, HALF], F32)) for i in range(2)]
        turn_bank = ctx.enter_context(nc.psum_tensor("b_turn", [P, HALF], F32))
        out_bank = ctx.enter_context(nc.psum_tensor("b_out", [P, HALF], F32))
        q_bank = [ctx.enter_context(nc.psum_tensor(f"b_q{i}", [P, HALF], F32)) for i in range(2)]
        wide = ctx.enter_context(nc.psum_tensor("b_wide", [P, DM], F32))
        GCOL = REP * P
        NG = KV1

        ident = sb("ident", [P, P])
        wq = both("wq", [P, KT, DM])
        wuq = both("wuq", [P, KT, UQ])
        route = sb("route", [BOT + 1, 2 * SLOTS])
        values = sb("values", [P, 2, BOT])
        wvuT = sb("wvuT", [BOT, DM])
        bu1 = sb("bu1", [P, UH])
        wu2 = sb("wu2", [P, UH])
        tiny = sb("tiny", [P, 6])

        x1 = [sb(f"x1_{p}", [P, DM]) for p in range(2)]
        kv = [sb(f"kv{p}", [P, 2 * KVD]) for p in range(2)]
        row = [sb(f"row{p}", [P, 3]) for p in range(2)]
        h = sb("h", [P, DM])
        xh = sb("xh", [P, DM])
        hT = both("hT", [P, KT, P])
        z = sb("z", [P, UH])
        zt = sb("zt", [P, UH])
        query = sb("query", [P, P])
        queryT = sb("queryT", [BOT + 1, P])
        top = sb("top", [P, TOPK])
        left = sb("left", [P, SLOTS])
        picked = sb("picked", [P, SLOTS])
        pickedT = sb("pickedT", [P, 2, P])
        mixT = sb("mixT", [BOT, P])
        peak = sb("peak", [P, 2])
        esum = sb("esum", [P, 2])
        gate = sb("gate", [P, 12])
        x2 = [sb(f"x2_{p}", [P, DM]) for p in range(2)]
        ln_stats = sb("ln_stats", [P, 2, 6])
        ln_mv = sb("ln_mv", [P, 2])
        ln = sb("ln", [P, 4])
        consts = sb("consts", [P, 3])
        carrier = sb("carrier", [P, 1])
        q = sb("q", [P, DM])
        qT = both("qT", [P, NG, P])
        k_rep = sb("k_rep", [P, NG, REP, D1])
        k_diag = both("k_diag", [P, NG, GCOL])
        s_max = [sb(f"s_max{r}", [P, REP]) for r in range(2)]
        s_sum = [sb(f"s_sum{r}", [P, REP]) for r in range(2)]
        s_inv = [sb(f"s_inv{r}", [P, REP]) for r in range(2)]
        prob = sb("prob", [P, 4, GCOL])
        probT = [sb(f"probT{r}", [P, GCOL]) for r in range(4)]
        o_sb = sb("o", [P, 2, HALF])

        s_load = sem("loaded")
        s_raw = [sem(f"raw_loaded{n}") for n in range(6 + KT)]
        s_const = sem("consts_made")
        s_ident = sem("ident_made")
        s_high = sem("weights_high")
        s_low = sem("weights_low")
        s_turned = sem("weights_turned")
        s_setup = sem("weights_placed")
        s_wq_high, s_wq_low = sem("wq_high"), sem("wq_low")
        s_zero = sem("query_zeroed")
        s_diag = sem("diag_zeroed")
        s_tiny = sem("tiny_halved")

        x1_in, kv_in = dma_signal("x1_in"), dma_signal("kv_in")
        x2_out, o_out = dma_signal("x2_out"), dma_signal("o_out")
        row_taken = signal("row_taken", 1)
        h_made = signal("h_made", 1)
        xh_added = signal("xh_added", 1)
        h_turned = signal("h_turned", 2)
        hT_high, hT_low = signal("hT_high", 2), signal("hT_low", 2)
        uq_ready = signal("uq_ready", 1)
        z_step = signal("z_step", 5)
        query_copied = signal("query_copied", 1)
        z_tanh = signal("z_tanh", 1)
        learned = signal("learned", 1)
        learned_tanh = signal("learned_tanh", 1)
        u_step = signal("u_step", 5)
        gate_tanh = signal("gate_tanh", 1)
        g_step = signal("g_step", 5)
        query_turned = signal("query_turned", 1)
        queryT_copied = signal("queryT_copied", 1)
        scored = signal("scored", 1)
        pick_step = signal("pick_step", 6)
        picked_exp = signal("picked_exp", 1)
        picked_turned = signal("picked_turned", 1)
        pickedT_copied = signal("pickedT_copied", 1)
        mixed = signal("mixed", 1)
        mixT_copied = signal("mixT_copied", 1)
        aux_ready = signal("aux_ready", 1)
        x2_made = signal("x2_made", 1)
        ln_step = signal("ln_step", 3)
        ln_rs = signal("ln_rs", 4)
        h2_made = signal("h2_made", 1)
        h2_turned = signal("h2_turned", 2)
        h2T_high, h2T_low = signal("h2T_high", 2), signal("h2T_low", 2)
        k_repeated = signal("k_repeated", 1)
        k_turned = signal("k_turned", 2)
        k_high, k_low = signal("k_high", 2), signal("k_low", 2)
        q_ready = signal("q_ready", 2)
        q_copied = signal("q_copied", 2)
        q_turned = signal("q_turned", 2)
        qT_high, qT_low = signal("qT_high", 2), signal("qT_low", 2)
        s_ready = signal("s_ready", NG)
        s_maxed = signal("s_maxed", NG)
        s_less = signal("s_less", NG)
        s_exped = signal("s_exped", NG)
        s_summed = signal("s_summed", NG)
        s_inverted = signal("s_inverted", NG)
        s_normed = signal("s_normed", NG)
        p_turned = signal("p_turned", NG)
        p_stored = signal("p_stored", NG)
        o_ready = signal("o_ready", 2)
        o_copied = signal("o_copied", 2)

        raw = [x1[0], x1[1], x2[0], x2[1], xh, o_sb[:, :, :].rearrange("p a c -> p (a c)")]
        raw += [prob[:, 2 * n:2 * n + 2].rearrange("p a c -> p (a c)") for n in range(2)]
        NS = len(raw)

        moments_pool, moments_dve, moments_act, moments_pe = row_moments(
            nc, sb, sem, out_bank[:, 0:1], sb("ones", [P, P]), keep, rows)
        block = ctx.enter_context(nc.Block())

        LAG = 3
        STEPS = NG + LAG - 1

        def schedule(start, turn):
            def run(eng):
                def numbered(n):
                    turn(eng, *[Batch(m // 2, m % 2) if 0 <= m < B else None for m in range(n - 1, n + 4)])

                start(eng, Batch(0, 0))
                for n in range(-2, 2):
                    numbered(n)
                with eng.Fori(1, B // 2 - 2) as pair:
                    for odd in range(2):
                        turn(eng, Batch(pair, odd).before(1),
                             *[Batch(pair + m // 2 if m > 1 else pair, m % 2) for m in range(odd, odd + 4)])
                for n in range(B - 4, B + 1):
                    numbered(n)
            return run

        small = [("L0_ffn_Wu1", 2), ("L0_ffn_Wq", 1), ("L0_ffn_Wvd", 1), ("L0_ffn_aux_values", 2)]
        pieces = []
        for name, n in small:
            height = w[name].shape[0] // n
            pieces += [(w[name][k * height:(k + 1) * height, :], height) for k in range(n)]
        NT = len(pieces)
        pieces += [(w["L1_xattn_Wq"][k * P:(k + 1) * P, :], P) for k in range(KT)]

        @block.sync
        def _(sp):
            def load_piece(n):
                src, height = pieces[n]
                sp.dma_start(raw[n % NS][0:height, :], src).then_inc(s_raw[n], 16)

            for n in range(NS):
                load_piece(n)
            sp.dma_start(q[:, 0:BOT], w["L0_ffn_aux_keys"][0:P, :]).then_inc(s_load, 16)
            sp.dma_start(q[:, BOT:2 * BOT], w["L0_ffn_aux_keys"][P:2 * P, :]).then_inc(s_load, 16)
            sp.dma_start(q[0:RDIM, 2 * BOT:3 * BOT], w["L0_ffn_Wr"]).then_inc(s_load, 16)
            sp.dma_start(q[:, 4 * BOT:12 * BOT].rearrange("p (t b) -> p t b", b=BOT),
                         w["L0_ffn_Wvu"].rearrange("(t p) b -> p t b", p=P)).then_inc(s_load, 16)
            for half in range(2):
                sp.dma_start(route[BOT:BOT + 1, half * SLOTS:(half + 1) * SLOTS],
                             w["L0_ffn_log_rel"].rearrange("(a s) -> a s", a=1)).then_inc(s_load, 16)
            sp.dma_start(bu1[:, :], w["L0_ffn_bu1"].partition_broadcast(P)).then_inc(s_load, 16)
            sp.dma_start(wu2[:, :], w["L0_ffn_Wu2"][0].partition_broadcast(P)).then_inc(s_load, 16)
            for n, name in enumerate(("L0_ffn_bu2", "L0_ffn_gate_w1", "L0_ffn_gate_bias")):
                sp.dma_start(tiny[:, n:n + 1], w[name].partition_broadcast(P)).then_inc(s_load, 16)
            for n in range(NS, len(pieces)):
                sp.wait_ge(s_turned, n - NS + 1)
                load_piece(n)
            sp.wait_ge(s_wq_low, NS + 2 - NT)

            def load_x1(i):
                need(sp, xh_added, i.before(2), 1)
                sp.dma_start(x1[i.odd][:, :], x1_dram[i.index]).then_inc(x1_in.sems[i.odd], 16)

            def load_kv(i):
                need(sp, o_ready, i.before(2), 2)
                sp.dma_start(kv[i.odd][:, :], kv_dram[i.index]).then_inc(kv_in.sems[i.odd], 16)

            def start(eng, i):
                load_x1(i)
                load_kv(i)
                load_kv(i.after())

            def turn(eng, before, i, qk, ffn, first):
                if first is not None:
                    load_x1(first)
                if before is not None:
                    if qk is not None:
                        load_kv(qk)
                    need(sp, o_copied, before, 2)
                    sp.dma_start(o_dram[before.index], o_sb[:, :, :].rearrange("p a b -> p (a b)")).then_inc(o_out.sems[before.odd], 16)
                if ffn is not None:
                    need(sp, x2_made, ffn, 1)
                    sp.dma_start(x2_dram[ffn.index], x2[ffn.odd][:, :]).then_inc(x2_out.sems[ffn.odd], 16)

            schedule(start, turn)(sp)
            for p in range(2):
                sp.wait_ge(x2_out.sems[p], 16 * (B // 2))
                sp.wait_ge(o_out.sems[p], 16 * (B // 2))

        @block.gpsimd
        def _(pool):
            make_identity(nc, pool, ident, s_ident)
            moments_pool(pool)
            for n, value in enumerate((EPS, -0.5, -1.0)):
                nc.gpsimd.memset(consts[:, n:n + 1], value).then_inc(s_const, 1)
            pool.wait_ge(s_const, 3)

            def add_h(i):
                need(pool, h_made, i, 1)
                need(pool, x1_in, i, 1)
                need(pool, x2_made, i.before(1), 1)
                nc.gpsimd.tensor_tensor(xh[:, :], x1[i.odd][:, :], h[:, :], ALU.add).then_inc(xh_added.sem, 1)

            def row_scale(i):
                need(pool, ln_step, i, 3)
                need(pool, h2_made, i.before(1), 1)
                nc.gpsimd.tensor_tensor(ln[:, 0:1], ln_mv[:, 1:2], consts[:, 0:1], ALU.add).then_inc(ln_rs.sem, 1)
                need(pool, ln_rs, i, 1)
                nc.gpsimd.tensor_tensor(ln[:, 1:2], ln[:, 0:1], consts[:, 1:2], ALU.pow).then_inc(ln_rs.sem, 1)
                need(pool, ln_rs, i, 2)
                nc.gpsimd.tensor_tensor(ln[:, 2:3], ln_mv[:, 0:1], consts[:, 2:3], ALU.mult).then_inc(ln_rs.sem, 1)
                need(pool, ln_rs, i, 3)
                nc.gpsimd.tensor_tensor(ln[:, 3:4], ln[:, 2:3], ln[:, 1:2], ALU.mult).then_inc(ln_rs.sem, 1)

            def start(eng, i):
                add_h(i)

            def turn(eng, before, i, qk, ffn, first):
                if i is not None:
                    for g in range(NG):
                        need(pool, s_inverted, i, g + 1)
                        pr = prob[:, g % 4].rearrange("p (r k) -> p r k", r=REP)
                        nc.gpsimd.tensor_tensor(pr, pr, s_inv[g % 2][:, :].unsqueeze(2).to_broadcast([P, REP, P]),
                                                ALU.mult).then_inc(s_normed.sem, 1)
                if first is not None:
                    add_h(first)
                if ffn is not None:
                    row_scale(ffn)

            schedule(start, turn)(pool)

        @block.tensor
        def _(pe):
            moments_pe(pe)
            pe.wait_ge(s_ident, 2)
            for n in range(NT):
                height = pieces[n][1]
                pe.wait_ge(s_raw[n], 16)
                if n in (1, 2, 3):
                    pe.wait_ge(s_low, n)
                elif n > 3:
                    pe.wait_ge(s_setup, n - 3)
                for t in range(KT):
                    mm = nc.tensor.transpose(wide[:, t * P:t * P + height], raw[n][0:height, t * P:(t + 1) * P],
                                             ident[0:height, 0:height])
                mm.then_inc(s_turned, 1)
            pe.wait_ge(s_setup, 3)
            for s in range(2):
                for t in range(KT):
                    mm = nc.tensor.matmul(score_bank[0][:, s * BOT:(s + 1) * BOT],
                                          probT[2 * s + t // 4][:, (t % 4) * P:(t % 4 + 1) * P],
                                          k_rep[:, t].rearrange("p r d -> p (r d)")[:, 0:BOT], start=(t == 0), stop=(t == KT - 1))
            mm.then_inc(s_turned, 1)
            pe.wait_ge(s_load, 16 * 11)
            for s in range(2):
                nc.tensor.transpose(q_bank[0][0:BOT, s * P:(s + 1) * P], q[:, s * BOT:(s + 1) * BOT], ident[:, :])
            mm = nc.tensor.transpose(q_bank[0][0:BOT, 2 * P:2 * P + RDIM], q[0:RDIM, 2 * BOT:3 * BOT], ident[0:RDIM, 0:RDIM])
            for t in range(KT):
                mm = nc.tensor.transpose(wide[0:BOT, t * P:(t + 1) * P], q[:, (4 + t) * BOT:(5 + t) * BOT], ident[:, :])
            mm.then_inc(s_turned, 1)
            pe.wait_ge(s_setup, 6)
            nc.tensor.matmul(score_bank[1][0:RDIM, 0:SLOTS], h[0:BOT, SLOTS:SLOTS + RDIM], h[0:BOT, 0:SLOTS],
                             start=True, stop=True).then_inc(s_turned, 1)
            pe.wait_ge(s_setup, 7)
            nc.tensor.matmul(q_bank[1][0:BOT, 0:SLOTS], q[0:RDIM, 2 * BOT:3 * BOT], h[0:RDIM, HALF:HALF + SLOTS],
                             start=True, stop=True).then_inc(s_turned, 1)
            pe.wait_ge(s_setup, 8)
            pe.wait_ge(s_low, 3)
            pe.wait_ge(s_high, 3)
            pe.wait_ge(s_zero, 2)

            def turn_h(i):
                need(pe, h_made, i, 1)
                need(pe, x2_made, i.before(1), 1)
                for t in range(KT):
                    mm = nc.tensor.transpose(wide[:, t * P:(t + 1) * P], h[:, t * P:(t + 1) * P], ident[:, :])
                    if t % 4 == 3:
                        mm.then_inc(h_turned.sem, 1)

            def up_and_query(i):
                need(pe, hT_low, i, 2)
                for t in range(KT):
                    mm = product(nc, wide[:, 0:UQ], [m[:, t] for m in hT], [m[:, t] for m in wuq], t == 0, t == KT - 1)
                mm.then_inc(uq_ready.sem, 1)

            def turn_query(i):
                need(pe, query_copied, i, 1)
                nc.tensor.transpose(wide[:, HALF:HALF + P], query[:, :], ident[:, :]).then_inc(query_turned.sem, 1)

            def score_slots(i):
                need(pe, queryT_copied, i, 1)
                nc.tensor.matmul(wide[:, HALF:DM], queryT[:, :], route[:, :], start=True, stop=True).then_inc(scored.sem, 1)

            def turn_picked(i):
                need(pe, picked_exp, i, 1)
                need(pe, z_step, i, 1)
                for s in range(2):
                    mm = nc.tensor.transpose(wide[:, s * P:(s + 1) * P], picked[:, s * P:(s + 1) * P], ident[:, :])
                mm.then_inc(picked_turned.sem, 1)

            def mix_values(i):
                need(pe, pickedT_copied, i, 1)
                for s in range(2):
                    mm = nc.tensor.matmul(wide[0:BOT, HALF:HALF + P], values[:, s], pickedT[:, s], start=(s == 0), stop=(s == 1))
                mm.then_inc(mixed.sem, 1)

            def up_values(i):
                need(pe, mixT_copied, i, 1)
                for half in range(2):
                    cols = slice(half * HALF, (half + 1) * HALF)
                    mm = nc.tensor.matmul(wide[:, cols], mixT[:, :], wvuT[:, cols], start=True, stop=True)
                mm.then_inc(aux_ready.sem, 1)

            def turn_h2(i):
                need(pe, h2_made, i, 1)
                need(pe, qT_low, i.before(1), 2)
                for t in range(KT):
                    mm = nc.tensor.transpose(q_bank[t // 4][:, (t % 4) * P:(t % 4 + 1) * P], h[:, t * P:(t + 1) * P], ident[:, :])
                    if t % 4 == 3:
                        mm.then_inc(h2_turned.sem, 1)

            def make_q(i, half, part):
                need(pe, h2T_low, i, part + 1)
                cols = slice(half * HALF, (half + 1) * HALF)
                for t in range(4 * part, 4 * part + 4):
                    mm = product(nc, q_bank[half][:, :], [m[:, t] for m in hT], [m[:, t, cols] for m in wq],
                                 t == 0, t == KT - 1)
                if part == 1:
                    mm.then_inc(q_ready.sem, 1)

            def turn_qT(i):
                for half in range(2):
                    need(pe, q_copied, i, half + 1)
                    for g in range(4 * half, 4 * half + 4):
                        mm = nc.tensor.transpose(q_bank[half][:, (g % 4) * P:(g % 4 + 1) * P], q[:, g * P:(g + 1) * P], ident[:, :])
                    mm.then_inc(q_turned.sem, 1)

            def turn_k(i, n):
                need(pe, k_repeated, i, 1)
                if n == 0:
                    need(pe, o_copied, i.before(1).before(1), 2)
                else:
                    need(pe, o_copied, i.before(1), 1)
                    need(pe, k_low, i, 1)
                for g in range(4 * n, 4 * n + 4):
                    mm = nc.tensor.transpose(out_bank[:, (g % 4) * P:(g % 4 + 1) * P],
                                             k_rep[:, g].rearrange("p r d -> p (r d)"), ident[:, :])
                mm.then_inc(k_turned.sem, 1)

            def score(i, g):
                if g % 4 == 0:
                    need(pe, qT_low, i, g // 4 + 1)
                    need(pe, k_low, i, g // 4 + 1)
                if g >= 2:
                    need(pe, s_less, i, g - 1)
                else:
                    need(pe, s_less, i.before(1), NG - 1 + g)
                product(nc, score_bank[g % 2][:, :], [m[:, g] for m in qT], [m[:, g] for m in k_diag],
                        True, True).then_inc(s_ready.sem, 1)

            def turn_probs(i, g):
                need(pe, s_normed, i, g + 1)
                if g > 0:
                    need(pe, p_stored, i, g)
                else:
                    need(pe, p_stored, i.before(1), NG)
                for r in range(REP):
                    mm = nc.tensor.transpose(turn_bank[:, r * P:(r + 1) * P], prob[:, g % 4, r * P:(r + 1) * P], ident[:, :])
                mm.then_inc(p_turned.sem, 1)

            def weigh_values(i, qk, n):
                need(pe, p_stored, i, 4 * n + 4)
                if qk is not None:
                    need(pe, k_low, qk, n + 1)
                elif n == 0:
                    need(pe, o_copied, i.before(1), 2)
                else:
                    need(pe, o_copied, i, 1)
                for c in range(4):
                    g = 4 * n + c
                    mm = nc.tensor.matmul(out_bank[c * D1:(c + 1) * D1, :],
                                          kv[i.odd][:, KVD + g * D1:KVD + (g + 1) * D1],
                                          probT[c][:, :], start=True, stop=True, tile_position=(0, c * D1))
                mm.then_inc(o_ready.sem, 1)

            def start(eng, i):
                turn_h(i)

            def turn(eng, before, i, qk, ffn, first):
                for s in range(STEPS):
                    if i is not None and s == 0:
                        score(i, 0)
                    if i is not None and s < NG - 1:
                        score(i, s + 1)
                    if before is not None and s == 0:
                        turn_probs(before, NG - 1)
                    if qk is not None and s == 7:
                        turn_qT(qk)
                    if i is not None and s >= LAG:
                        turn_probs(i, s - LAG)
                    if i is not None and s == LAG + 4:
                        weigh_values(i, qk, 0)
                    if ffn is not None:
                        if s == 0:
                            up_and_query(ffn)
                        elif s == 2:
                            score_slots(ffn)
                        elif s == 5:
                            turn_picked(ffn)
                        elif s == 6:
                            mix_values(ffn)
                        elif s == 7:
                            up_values(ffn)
                    if qk is not None:
                        if s == 0:
                            turn_h2(qk)
                        elif 2 <= s <= 5:
                            make_q(qk, (s - 2) // 2, s % 2)
                            if s == 4:
                                turn_k(qk, 0)
                        elif s == 8:
                            turn_k(qk, 1)
                    if ffn is not None and s == 0:
                        turn_query(ffn)
                    if before is not None and s == 0:
                        weigh_values(before, i, 1)
                    if first is not None and s == STEPS - 1:
                        turn_h(first)

            schedule(start, turn)(pe)

        @block.scalar
        def _(act):
            moments_act(act)
            wuq_at = [(0, 0, P), (0, P, P), (0, UH, BOT)]

            def high_wq(n):
                act.wait_ge(s_raw[NT + n], 16)
                nc.scalar.copy(wq[0][:, n], raw[(NT + n) % NS][:, :]).then_inc(s_wq_high, 1)

            for n in range(NT):
                act.wait_ge(s_turned, n + 1)
                src = wide[:, :].rearrange("p (t c) -> p t c", t=KT)
                if n < 3:
                    _, at, height = wuq_at[n]
                    nc.scalar.copy(wuq[0][:, :, at:at + height], src[:, :, 0:height]).then_inc(s_high, 1)
                elif n == 3:
                    nc.scalar.copy(k_rep[:, :, :, :].rearrange("p t r d -> p t (r d)")[:, :, 0:BOT], src[:, :, 0:BOT]).then_inc(s_setup, 1)
                else:
                    s = n - 4
                    nc.scalar.copy(probT[2 * s][:, :], wide[:, 0:HALF])
                    nc.scalar.copy(probT[2 * s + 1][:, :], wide[:, HALF:DM]).then_inc(s_setup, 1)
                if n >= 3:
                    high_wq(n - 3)
            for n in range(NT - 3, KT):
                high_wq(n)
            act.wait_ge(s_turned, NT + 1)
            nc.scalar.copy(values[:, :, :].rearrange("p s b -> p (s b)"), score_bank[0][:, 0:2 * BOT]).then_inc(s_setup, 1)
            act.wait_ge(s_turned, NT + 2)
            nc.scalar.copy(h[0:BOT, 0:SLOTS + RDIM], q_bank[0][0:BOT, 0:SLOTS + RDIM]).then_inc(s_setup, 1)
            nc.scalar.copy(wvuT[:, :], wide[0:BOT, :]).then_inc(s_setup, 1)
            act.wait_ge(s_turned, NT + 3)
            nc.scalar.copy(h[0:RDIM, HALF:HALF + SLOTS], score_bank[1][0:RDIM, 0:SLOTS]).then_inc(s_setup, 1)
            act.wait_ge(s_turned, NT + 4)
            nc.scalar.mul(route[0:BOT, 0:SLOTS], q_bank[1][0:BOT, 0:SLOTS], float(RDIM) ** -0.5)
            nc.scalar.mul(route[0:BOT, SLOTS:2 * SLOTS], q_bank[0][0:BOT, 0:SLOTS], float(BOT) ** -0.5).then_inc(s_setup, 1)
            act.wait_ge(s_tiny, 1)
            act.wait_ge(s_diag, 2)

            def make_h(i):
                need(act, row_taken, i, 1)
                need(act, x1_in, i, 1)
                if isinstance(i.pair, int) and i.index < 2:
                    need(act, xh_added, i.before(1), 1)
                    need(act, h_turned, i.before(1), 2)
                else:
                    need(act, h2_turned, i.before(2), 2)
                nc.scalar.activation(h[:, :], x1[i.odd][:, :], ACT.Identity, bias=row[i.odd][:, 1:2],
                                     scale=row[i.odd][:, 0:1]).then_inc(h_made.sem, 1)

            def high_h(i):
                need(act, q_ready, i.before(2), 2)
                for half in range(2):
                    need(act, h_turned, i, half + 1)
                    nc.scalar.copy(hT[0][:, 4 * half:4 * half + 4].rearrange("p t c -> p (t c)"),
                                   wide[:, half * HALF:(half + 1) * HALF]).then_inc(hT_high.sem, 1)

            def copy_query(i):
                need(act, uq_ready, i, 1)
                nc.scalar.copy(query[:, 0:BOT], wide[:, UH:UQ]).then_inc(query_copied.sem, 1)

            def copy_queryT(i):
                need(act, query_turned, i, 1)
                nc.scalar.copy(queryT[:, :], wide[0:BOT + 1, HALF:HALF + P]).then_inc(queryT_copied.sem, 1)

            def tanh_z(i):
                need(act, z_step, i, 4)
                nc.scalar.activation(zt[:, :], zt[:, :], ACT.Tanh, scale=GELU_C).then_inc(z_tanh.sem, 1)

            def exp_picked(i):
                need(act, pick_step, i, 6)
                nc.scalar.activation(picked[:, :], picked[:, :], ACT.Exp, bias=peak[:, 1:2],
                                     accum_out=esum[:, 0:1]).then_inc(picked_exp.sem, 1)

            def tanh_learned(i):
                need(act, learned, i, 1)
                nc.scalar.activation(gate[:, 1:2], gate[:, 0:1], ACT.Tanh, bias=tiny[:, 3:4], scale=0.5).then_inc(learned_tanh.sem, 1)

            def copy_picked(i):
                need(act, picked_turned, i, 1)
                nc.scalar.copy(pickedT[:, :, :].rearrange("p s c -> p (s c)"), wide[:, 0:SLOTS]).then_inc(pickedT_copied.sem, 1)
                need(act, u_step, i, 5)
                nc.scalar.activation(gate[:, 7:8], gate[:, 6:7], ACT.Tanh, bias=tiny[:, 5:6], scale=tiny[:, 4:5]).then_inc(gate_tanh.sem, 1)

            def copy_mix(i):
                need(act, mixed, i, 1)
                nc.scalar.copy(mixT[:, :], wide[0:BOT, HALF:HALF + P]).then_inc(mixT_copied.sem, 1)

            def make_h2(i, first):
                need(act, ln_rs, i, 4)
                last_h = i if first is None else first
                need(act, xh_added, last_h, 1)
                need(act, h_turned, last_h, 2)
                if first is None:
                    need(act, h2_turned, i.before(1), 2)
                nc.scalar.activation(h[:, :], x2[i.odd][:, :], ACT.Identity, bias=ln[:, 3:4], scale=ln[:, 1:2]).then_inc(h2_made.sem, 1)

            def high_h2(i, ffn):
                need(act, uq_ready, i if ffn is None else ffn, 1)
                if ffn is None:
                    need(act, q_ready, i.before(1), 2)
                for half in range(2):
                    need(act, h2_turned, i, half + 1)
                    nc.scalar.copy(hT[0][:, 4 * half:4 * half + 4].rearrange("p t c -> p (t c)"),
                                   q_bank[half][:, :]).then_inc(h2T_high.sem, 1)

            def repeat_k(i):
                need(act, kv_in, i, 1)
                need(act, k_turned, i.before(1), 2)
                nc.scalar.copy(k_rep[:, :, :, :],
                               kv[i.odd][:, 0:KVD].rearrange("p (g d) -> p g d", d=D1).unsqueeze(2).to_broadcast([P, NG, REP, D1])
                               ).then_inc(k_repeated.sem, 1)

            def high_k(i, n):
                need(act, k_turned, i, n + 1)
                need(act, s_ready, i.before(1), 4 * n + 4)
                for r in range(REP):
                    rows_r = slice(r * D1, (r + 1) * D1)
                    op = nc.scalar.copy(k_diag[0][rows_r, 4 * n:4 * n + 4, r * P:(r + 1) * P],
                                        out_bank[rows_r, :].rearrange("p (g k) -> p g k", k=P))
                op.then_inc(k_high.sem, 1)

            def copy_q(i, half):
                need(act, q_ready, i, half + 1)
                need(act, q_turned, i.before(1), 2)
                nc.scalar.copy(q[:, half * HALF:(half + 1) * HALF], q_bank[half][:, :]).then_inc(q_copied.sem, 1)

            def high_qT(i):
                need(act, s_ready, i.before(1), NG)
                for half in range(2):
                    need(act, q_turned, i, half + 1)
                    nc.scalar.copy(qT[0][:, 4 * half:4 * half + 4].rearrange("p t c -> p (t c)"),
                                   q_bank[half][:, :]).then_inc(qT_high.sem, 1)

            def exp_scores(i, g):
                need(act, s_less, i, g + 1)
                nc.scalar.activation(prob[:, g % 4], prob[:, g % 4], ACT.Exp, scale=float(D1) ** -0.5).then_inc(s_exped.sem, 1)

            def copy_probT(i, g):
                need(act, p_turned, i, g + 1)
                if g == 4:
                    need(act, o_ready, i, 1)
                elif g == 0:
                    need(act, o_ready, i.before(1), 2)
                nc.scalar.copy(probT[g % 4][:, :], turn_bank[:, :]).then_inc(p_stored.sem, 1)

            def copy_out(i, n):
                need(act, o_ready, i, n + 1)
                need(act, o_out, i.before(1), 1)
                nc.scalar.copy(o_sb[:, n], out_bank[:, :]).then_inc(o_copied.sem, 1)

            def start(eng, i):
                make_h(i)
                high_h(i)

            def turn(eng, before, i, qk, ffn, first):
                for s in range(STEPS):
                    if before is not None and s == 0:
                        copy_probT(before, NG - 1)
                    if qk is not None and s == 6:
                        copy_q(qk, 1)
                    if before is not None and s == 1:
                        copy_out(before, 1)
                    if i is not None and s == LAG + 4:
                        copy_out(i, 0)
                    if i is not None and s < NG and s != LAG + 3:
                        exp_scores(i, s)
                    if i is not None and s >= LAG:
                        copy_probT(i, s - LAG)
                    if i is not None and s == LAG + 3:
                        exp_scores(i, s)
                    if ffn is not None:
                        if s == 0:
                            copy_query(ffn)
                        elif s == 2:
                            tanh_z(ffn)
                        elif s == 3:
                            tanh_learned(ffn)
                        elif s == 4:
                            exp_picked(ffn)
                        elif s == 5:
                            copy_picked(ffn)
                        elif s == 6:
                            copy_mix(ffn)
                    if qk is not None:
                        if s == 0:
                            high_h2(qk, ffn)
                        elif s == 3:
                            repeat_k(qk)
                        elif s == 4:
                            copy_q(qk, 0)
                            high_k(qk, 0)
                        elif s == 8:
                            high_k(qk, 1)
                    if ffn is not None and s == 0:
                        copy_queryT(ffn)
                    if qk is not None and s == 7:
                        high_qT(qk)
                    if first is not None:
                        if s == 6:
                            make_h(first)
                        elif s == STEPS - 1:
                            high_h(first)
                if ffn is not None:
                    make_h2(ffn, first)

            schedule(start, turn)(act)

        @block.vector
        def _(dve):
            moments_dve(dve)
            for n in range(3):
                at, height = (0, P, UH)[n], (P, P, BOT)[n]
                dve.wait_ge(s_high, n + 1)
                nc.vector.tensor_tensor(wuq[1][:, :, at:at + height],
                                        wide[:, :].rearrange("p (t c) -> p t c", t=KT)[:, :, 0:height],
                                        wuq[0][:, :, at:at + height].bitcast(F32), ALU.subtract).then_inc(s_low, 1)
            for part in range(2):
                nc.vector.memset(k_diag[part][:, :, :].bitcast(F32), 0.0).then_inc(s_diag, 1)
            dve.wait_ge(s_load, 16 * 11)
            nc.vector.tensor_scalar(tiny[:, 3:6], tiny[:, 0:3], 0.5, None, ALU.mult).then_inc(s_tiny, 1)
            nc.vector.tensor_scalar(wu2[:, :], wu2[:, :], 0.5, None, ALU.mult).then_inc(s_tiny, 1)
            nc.vector.memset(query[:, BOT:P], 0.0).then_inc(s_zero, 1)
            dve.wait_ge(s_zero, 1)
            nc.vector.memset(query[:, BOT:BOT + 1], 1.0).then_inc(s_zero, 1)
            for n in range(KT):
                dve.wait_ge(s_wq_high, n + 1)
                nc.vector.tensor_tensor(wq[1][:, n], raw[(NT + n) % NS][:, :], wq[0][:, n].bitcast(F32), ALU.subtract).then_inc(s_wq_low, 1)
            dve.wait_ge(s_tiny, 2)

            def take_row(i):
                nc.vector.tensor_copy(row[i.odd][:, :].unsqueeze(1), rows[:, index_of(i), :]).then_inc(row_taken.sem, 1)

            def low_h(i):
                for half in range(2):
                    part = slice(4 * half, 4 * half + 4)
                    need(dve, hT_high, i, half + 1)
                    nc.vector.tensor_tensor(hT[1][:, part].rearrange("p t c -> p (t c)"), wide[:, half * HALF:(half + 1) * HALF],
                                            hT[0][:, part].rearrange("p t c -> p (t c)").bitcast(F32), ALU.subtract).then_inc(hT_low.sem, 1)

            def low_h2(i):
                for half in range(2):
                    part = slice(4 * half, 4 * half + 4)
                    need(dve, h2T_high, i, half + 1)
                    nc.vector.tensor_tensor(hT[1][:, part].rearrange("p t c -> p (t c)"), q_bank[half][:, :],
                                            hT[0][:, part].rearrange("p t c -> p (t c)").bitcast(F32), ALU.subtract).then_inc(h2T_low.sem, 1)

            def low_qT(i):
                for half in range(2):
                    part = slice(4 * half, 4 * half + 4)
                    need(dve, qT_high, i, half + 1)
                    nc.vector.tensor_tensor(qT[1][:, part].rearrange("p t c -> p (t c)"), q_bank[half][:, :],
                                            qT[0][:, part].rearrange("p t c -> p (t c)").bitcast(F32), ALU.subtract).then_inc(qT_low.sem, 1)

            def low_k(i, n):
                need(dve, k_high, i, n + 1)
                for r in range(REP):
                    rows_r = slice(r * D1, (r + 1) * D1)
                    blk = [m[rows_r, 4 * n:4 * n + 4, r * P:(r + 1) * P] for m in k_diag]
                    op = nc.vector.tensor_tensor(blk[1], out_bank[rows_r, :].rearrange("p (g k) -> p g k", k=P),
                                                 blk[0].bitcast(F32), ALU.subtract)
                op.then_inc(k_low.sem, 1)

            def add_bu1(i):
                need(dve, uq_ready, i, 1)
                need(dve, query_copied, i, 1)
                nc.vector.tensor_tensor(z[:, :], wide[:, 0:UH], bu1[:, :], ALU.add).then_inc(z_step.sem, 1)

            def gelu(i):
                need(dve, z_step, i, 1)
                nc.vector.tensor_tensor(zt[:, :], z[:, :], z[:, :], ALU.mult).then_inc(z_step.sem, 1)
                need(dve, z_step, i, 2)
                nc.vector.tensor_scalar(zt[:, :], zt[:, :], GELU_A, 1.0, ALU.mult, ALU.add).then_inc(z_step.sem, 1)
                need(dve, z_step, i, 3)
                nc.vector.tensor_tensor(zt[:, :], zt[:, :], z[:, :], ALU.mult).then_inc(z_step.sem, 1)

            def pick(i):
                need_first(scored, i, 1)
                nc.vector.max(top[:, :], wide[:, HALF:HALF + SLOTS]).then_inc(pick_step.sem, 1)
                need_first(pick_step, i, 1)
                nc.vector.match_replace(left[:, :], top[:, :], wide[:, HALF:HALF + SLOTS], -3e38).then_inc(pick_step.sem, 1)
                need(dve, pick_step, i, 2)
                nc.vector.tensor_tensor(left[:, :], left[:, :], wide[:, HALF:HALF + SLOTS], ALU.is_equal).then_inc(pick_step.sem, 1)
                need(dve, pick_step, i, 3)
                nc.vector.scalar_tensor_tensor(picked[:, :], left[:, :], -MASKED, wide[:, HALF + SLOTS:DM],
                                               ALU.mult, ALU.add).then_inc(pick_step.sem, 1)
                need(dve, pick_step, i, 4)
                nc.vector.tensor_reduce(peak[:, 0:1], picked[:, :], AX.X, ALU.max).then_inc(pick_step.sem, 1)
                need(dve, pick_step, i, 5)
                nc.vector.tensor_scalar(peak[:, 1:2], peak[:, 0:1], -1.0, None, ALU.mult).then_inc(pick_step.sem, 1)

            def learn(i):
                need(dve, z_tanh, i, 1)
                nc.vector.scalar_tensor_tensor(z[:, :], zt[:, :], 1.0, z[:, :], ALU.add, ALU.mult).then_inc(z_step.sem, 1)
                need(dve, z_step, i, 5)
                nc.vector.tensor_tensor_reduce(zt[:, :], z[:, :], wu2[:, :], 1.0, 0.0, ALU.mult, ALU.add,
                                               gate[:, 0:1]).then_inc(learned.sem, 1)

            def uncertainty(i):
                need(dve, learned_tanh, i, 1)
                nc.vector.tensor_scalar(gate[:, 2:3], gate[:, 1:2], 1.25, 1.25, ALU.mult, ALU.add).then_inc(u_step.sem, 1)
                need(dve, u_step, i, 1)
                nc.vector.tensor_scalar(gate[:, 3:4], gate[:, 2:3], row[i.odd][:, 2:3], 0.0, ALU.add, ALU.max).then_inc(u_step.sem, 1)
                need(dve, u_step, i, 2)
                nc.vector.tensor_scalar(gate[:, 4:5], gate[:, 3:4], 5.0, -TAU_LOW, ALU.min, ALU.add).then_inc(u_step.sem, 1)
                need(dve, u_step, i, 3)
                nc.vector.tensor_scalar(gate[:, 5:6], gate[:, 4:5], 1.0 / (TAU_HIGH - TAU_LOW), 0.0, ALU.mult, ALU.max).then_inc(u_step.sem, 1)
                need(dve, u_step, i, 4)
                nc.vector.tensor_scalar(gate[:, 6:7], gate[:, 5:6], 1.0, None, ALU.min).then_inc(u_step.sem, 1)

            def gates(i):
                need(dve, gate_tanh, i, 1)
                nc.vector.tensor_scalar(gate[:, 8:9], gate[:, 7:8], 0.5, 0.5, ALU.mult, ALU.add).then_inc(g_step.sem, 1)
                need(dve, g_step, i, 1)
                nc.vector.tensor_scalar(gate[:, 9:10], gate[:, 8:9], EARLY_EXIT, None, ALU.is_ge).then_inc(g_step.sem, 1)
                need(dve, picked_exp, i, 1)
                nc.vector.reciprocal(esum[:, 1:2], esum[:, 0:1]).then_inc(g_step.sem, 1)
                need(dve, g_step, i, 3)
                nc.vector.tensor_tensor(gate[:, 10:11], gate[:, 8:9], gate[:, 9:10], ALU.mult).then_inc(g_step.sem, 1)
                need(dve, g_step, i, 4)
                nc.vector.tensor_tensor(gate[:, 11:12], gate[:, 10:11], esum[:, 1:2], ALU.mult).then_inc(g_step.sem, 1)

            def index_of(i):
                return slice(i.index, i.index + 1) if isinstance(i.pair, int) else bass.ds(i.index, 1)

            def need_first(signal, i, k):
                need(dve, signal, i, k)
                nc.vector.memset(carrier[:, :], 0.0)

            def add_ffn(i):
                need(dve, aux_ready, i, 1)
                need(dve, xh_added, i, 1)
                need(dve, x2_out, i.before(2), 1)
                if not (isinstance(i.pair, int) and i.index < 2):
                    need(dve, h2_made, i.before(2), 1)
                need(dve, g_step, i, 5)
                nc.vector.scalar_tensor_tensor(x2[i.odd][:, :], wide[:, :], gate[:, 11:12], xh[:, :], ALU.mult, ALU.add).then_inc(x2_made.sem, 1)

            def row_stats(i):
                need(dve, x2_made, i, 1)
                need(dve, ln_rs, i.before(1), 4)
                for half in range(2):
                    nc.vector.bn_stats(ln_stats[:, half], x2[i.odd][:, half * HALF:(half + 1) * HALF]).then_inc(ln_step.sem, 1)
                need_first(ln_step, i, 2)
                nc.vector.bn_aggr(ln_mv[:, :], ln_stats[:, :, :]).then_inc(ln_step.sem, 1)

            def less_max(i, g):
                need(dve, s_ready, i, g + 1)
                sv = score_bank[g % 2][:, :].rearrange("p (r k) -> p r k", r=REP)
                nc.vector.tensor_reduce(s_max[g % 2][:, :], sv, AX.X, ALU.max).then_inc(s_maxed.sem, 1)
                need(dve, s_maxed, i, g + 1)
                if g >= 4:
                    need(dve, p_turned, i, g - 3)
                else:
                    need(dve, p_turned, i.before(1), g + 5)
                nc.vector.tensor_tensor(prob[:, g % 4].rearrange("p (r k) -> p r k", r=REP), sv,
                                        s_max[g % 2][:, :].unsqueeze(2).to_broadcast([P, REP, P]),
                                        ALU.subtract).then_inc(s_less.sem, 1)

            def invert_sum(i, g):
                need(dve, s_exped, i, g + 1)
                nc.vector.tensor_reduce(s_sum[g % 2][:, :], prob[:, g % 4].rearrange("p (r k) -> p r k", r=REP),
                                        AX.X, ALU.add).then_inc(s_summed.sem, 1)
                need(dve, s_summed, i, g + 1)
                if g >= 2:
                    need(dve, s_normed, i, g - 1)
                nc.vector.reciprocal(s_inv[g % 2][:, :], s_sum[g % 2][:, :]).then_inc(s_inverted.sem, 1)

            def start(eng, i):
                dve.wait_ge(s_wq_low, KT)
                take_row(i)
                low_h(i)

            def turn(eng, before, i, qk, ffn, first):
                for s in range(STEPS):
                    if i is not None and s < NG and s != 1:
                        less_max(i, s)
                    if i is not None and s == 0:
                        less_max(i, 1)
                    if i is not None and 1 <= s <= NG:
                        invert_sum(i, s - 1)
                    if ffn is not None and s == 0:
                        add_bu1(ffn)
                    if qk is not None:
                        if s == 0:
                            low_h2(qk)
                        elif s == 5:
                            low_k(qk, 0)
                    if ffn is not None:
                        if s == 1:
                            gelu(ffn)
                        elif s == 2:
                            learn(ffn)
                        elif s == 3:
                            pick(ffn)
                        elif s == 4:
                            uncertainty(ffn)
                        elif s == 6:
                            gates(ffn)
                        elif s == 8:
                            add_ffn(ffn)
                    if qk is not None and s == 8:
                        low_qT(qk)
                    if first is not None:
                        if s == 5:
                            take_row(first)
                        elif s == STEPS - 1:
                            low_h(first)
                if ffn is not None:
                    row_stats(ffn)
                if qk is not None:
                    low_k(qk, 1)

            schedule(start, turn)(dve)


def layer1_out_and_ffn(nc, sems, w, x2_dram, o_dram, out):
    with ExitStack() as ctx:
        def sb(name, shape, dt=F32):
            return ctx.enter_context(nc.sbuf_tensor(f"c_{name}", shape, dt))

        def sem(name):
            return sems.new(nc.semaphore(f"c_{name}"))

        def signal(name, n):
            return Signal(sem(name), n)

        def dma_signal(name, n=1):
            return DmaSignal([sem(f"{name}_{p}") for p in "eo"], n)

        def both(name, shape):
            return sb(f"{name}_hi", shape, F32R), sb(f"{name}_lo", shape, F32R)

        def wide_bank(name):
            return ctx.enter_context(nc.psum_tensor(f"c_{name}", [P, DM], F32))

        o_wide, t_wide, s_wide = wide_bank("o_wide"), wide_bank("t_wide"), wide_bank("s_wide")
        ident = sb("ident", [P, P])
        consts = sb("consts", [P, 3])
        wo = both("wo", [P, KT, DM])
        sign = both("sign", [P, KT, DM])
        soft = sb("soft", [P, 5])
        raw = [sb(f"raw{n}", [P, DM]) for n in range(2)]
        carrier = sb("carrier", [P, 1])

        o_in_sb = [sb(f"o{p}", [P, DM]) for p in range(2)]
        o_hl = both("o_hl", [P, KT, P])
        x2 = [sb(f"x2_{p}", [P, DM]) for p in range(2)]
        x3 = [sb(f"x3_{p}", [P, DM]) for p in range(2)]
        h = sb("h", [P, DM])
        hT = both("hT", [P, KT, P])
        ln_stats = sb("ln_stats", [P, 2, 6])
        ln_mv = sb("ln_mv", [P, 2])
        ln = sb("ln", [P, 4])
        y = [sb(f"y{p}", [P, DM]) for p in range(2)]


        slots = [raw[0], raw[1], y[0], y[1], x3[1]]
        NS = len(slots)
        s_raw = [sem(f"raw_loaded{n}") for n in range(NS)]
        s_scale = sem("scale_loaded")
        s_ident, s_const = sem("ident_made"), sem("consts_made")
        s_high, s_low = sem("weights_high"), sem("weights_low")
        s_soft_dve, s_soft_act = sem("softplus_dve"), sem("softplus_act")
        o_in, x2_in, y_out = dma_signal("o_in"), dma_signal("x2_in"), dma_signal("y_out")
        o_high, o_low = signal("o_high", 1), signal("o_low", 1)
        o_ready = signal("o_ready", 1)
        x3_made = signal("x3_made", 1)
        ln_step = signal("ln_step", 3)
        ln_rs = signal("ln_rs", 4)
        h_made = signal("h_made", 1)
        h_turned = signal("h_turned", 1)
        hT_high, hT_low = signal("hT_high", 1), signal("hT_low", 1)
        f_ready = signal("f_ready", 1)
        y_made = signal("y_made", 1)
        block = ctx.enter_context(nc.Block())

        def schedule(fill, step):
            def run(eng):
                fill(eng, Batch(0, 0))
                step(eng, Batch(0, 0), Batch(0, 1))
                step(eng, Batch(0, 1), Batch(1, 0))
                with eng.Fori(1, B // 2 - 1) as pair:
                    step(eng, Batch(pair, 0), Batch(pair, 1))
                    step(eng, Batch(pair, 1), Batch(pair + 1, 0))
                step(eng, Batch(B // 2 - 1, 0), Batch(B // 2 - 1, 1))
                step(eng, Batch(B // 2 - 1, 1), None)
            return run

        @block.sync
        def _(sp):
            sp.dma_start(soft[:, 0:1], w["L1_ffn_scale"].partition_broadcast(P)).then_inc(s_scale, 16)

            def load(i):
                need(sp, o_low, i.before(2), 1)
                need(sp, o_high, i.before(2), 1)
                sp.dma_start(o_in_sb[i.odd][:, :], o_dram[i.index]).then_inc(o_in.sems[i.odd], 16)
                need(sp, x3_made, i.before(2), 1)
                sp.dma_start(x2[i.odd][:, :], x2_dram[i.index]).then_inc(x2_in.sems[i.odd], 16)

            load(Batch(0, 0))
            for n in range(2 * KT):
                if n >= NS:
                    sp.wait_ge(s_low, n - NS + 1)
                slot, loaded = slots[n % NS], s_raw[n % NS]
                if n < KT:
                    src = w["L1_xattn_Wo"].rearrange("(a g r d) n -> a r g d n", a=2, g=4, r=REP)[n // 4, n % 4]
                    for grp in range(4):
                        sp.dma_start(slot[grp * D1:(grp + 1) * D1, :], src[grp]).then_inc(loaded, 16)
                else:
                    sp.dma_start(slot[:, :], w["L1_ffn_sign"][(n - KT) * P:(n - KT + 1) * P, :]).then_inc(loaded, 64)

            def fill(eng, i):
                load(i.after())

            def step(eng, i, nxt):
                if nxt is not None and not (isinstance(nxt.pair, int) and nxt.pair == B // 2 - 1 and nxt.odd):
                    load(nxt.after())
                need(sp, y_made, i, 1)
                sp.dma_start(out[i.index], y[i.odd][:, :]).then_inc(y_out.sems[i.odd], 16)

            schedule(fill, step)(sp)
            for p in range(2):
                sp.wait_ge(y_out.sems[p], 16 * (B // 2))

        @block.gpsimd
        def _(pool):
            make_identity(nc, pool, ident, s_ident)
            for n, value in enumerate((EPS, -0.5, -1.0)):
                nc.gpsimd.memset(consts[:, n:n + 1], value).then_inc(s_const, 1)
            pool.wait_ge(s_const, 3)

            def split_o(i):
                need(pool, o_high, i, 1)
                need(pool, o_in, i, 1)
                need(pool, o_ready, i.before(1), 1)
                nc.gpsimd.tensor_tensor(o_hl[1][:, :, :].rearrange("p t c -> p (t c)"), o_in_sb[i.odd][:, :],
                                        o_hl[0][:, :, :].rearrange("p t c -> p (t c)").bitcast(F32), ALU.subtract).then_inc(o_low.sem, 1)

            def norm(i):
                need(pool, ln_step, i, 3)
                need(pool, h_made, i.before(1), 1)
                nc.gpsimd.tensor_tensor(ln[:, 0:1], ln_mv[:, 1:2], consts[:, 0:1], ALU.add).then_inc(ln_rs.sem, 1)
                need(pool, ln_rs, i, 1)
                nc.gpsimd.tensor_tensor(ln[:, 1:2], ln[:, 0:1], consts[:, 1:2], ALU.pow).then_inc(ln_rs.sem, 1)
                need(pool, ln_rs, i, 2)
                nc.gpsimd.tensor_tensor(ln[:, 2:3], ln_mv[:, 0:1], consts[:, 2:3], ALU.mult).then_inc(ln_rs.sem, 1)
                need(pool, ln_rs, i, 3)
                nc.gpsimd.tensor_tensor(ln[:, 3:4], ln[:, 2:3], ln[:, 1:2], ALU.mult).then_inc(ln_rs.sem, 1)

            def fill(eng, i):
                split_o(i)

            def step(eng, i, nxt):
                norm(i)
                if nxt is not None:
                    split_o(nxt)

            schedule(fill, step)(pool)

        @block.tensor
        def _(pe):
            pe.wait_ge(s_ident, 2)

            def out_proj(i, half):
                if half == 0:
                    need(pe, o_low, i, 1)
                    need(pe, x3_made, i.before(1), 1)
                cols = slice(half * HALF, (half + 1) * HALF)
                for t in range(KT):
                    if isinstance(i.pair, int) and i.index == 0 and half == 0:
                        pe.wait_ge(s_low, t + 1)
                    mm = product(nc, o_wide[:, cols], [m[:, t] for m in o_hl], [m[:, t, cols] for m in wo],
                                 t == 0, t == KT - 1)
                if half:
                    mm.then_inc(o_ready.sem, 1)

            def fill(eng, i):
                out_proj(i, 0)
                out_proj(i, 1)

            def step(eng, i, nxt):
                if nxt is not None:
                    out_proj(nxt, 0)
                need(pe, h_made, i, 1)
                need(pe, hT_low, i.before(1), 1)
                for t in range(KT):
                    mm = nc.tensor.transpose(t_wide[:, t * P:(t + 1) * P], h[:, t * P:(t + 1) * P], ident[:, :])
                mm.then_inc(h_turned.sem, 1)
                if nxt is not None:
                    out_proj(nxt, 1)
                if isinstance(i.pair, int) and i.index == 0:
                    pe.wait_ge(s_low, 2 * KT)
                need(pe, hT_low, i, 1)
                need(pe, y_made, i.before(1), 1)
                for half in range(2):
                    cols = slice(half * HALF, (half + 1) * HALF)
                    for t in range(KT):
                        mm = product(nc, s_wide[:, cols], [m[:, t] for m in hT], [m[:, t, cols] for m in sign],
                                     t == 0, t == KT - 1)
                mm.then_inc(f_ready.sem, 1)

            schedule(fill, step)(pe)

        @block.scalar
        def _(act):
            def split_o(i):
                need(act, o_in, i, 1)
                need(act, o_ready, i.before(1), 1)
                nc.scalar.copy(o_hl[0][:, :, :].rearrange("p t c -> p (t c)"), o_in_sb[i.odd][:, :]).then_inc(o_high.sem, 1)

            act.wait_ge(s_soft_dve, 2)
            nc.scalar.activation(soft[:, 2:3], soft[:, 1:2], ACT.Exp, scale=-1.0).then_inc(s_soft_act, 1)
            act.wait_ge(s_soft_act, 1)
            nc.scalar.activation(soft[:, 3:4], soft[:, 2:3], ACT.Ln, bias=1.0).then_inc(s_soft_act, 1)
            for n in range(2 * KT):
                act.wait_ge(s_raw[n % NS], 64 * (n // NS + 1))
                nc.scalar.copy((wo if n < KT else sign)[0][:, n % KT], slots[n % NS][:, :]).then_inc(s_high, 1)
                if n == 0:
                    split_o(Batch(0, 0))

            def fill(eng, i):
                pass

            def step(eng, i, nxt):
                need(act, ln_rs, i, 4)
                need(act, h_turned, i.before(1), 1)
                nc.scalar.activation(h[:, :], x3[i.odd][:, :], ACT.Identity, bias=ln[:, 3:4], scale=ln[:, 1:2]).then_inc(h_made.sem, 1)
                if nxt is not None:
                    split_o(nxt)
                need(act, h_turned, i, 1)
                need(act, f_ready, i.before(1), 1)
                nc.scalar.copy(hT[0][:, :, :].rearrange("p t c -> p (t c)"), t_wide[:, :]).then_inc(hT_high.sem, 1)

            schedule(fill, step)(act)

        @block.vector
        def _(dve):
            def add_o(i):
                need(dve, o_ready, i, 1)
                need(dve, x2_in, i, 1)
                need(dve, y_made, i.before(2), 1)
                nc.vector.tensor_tensor(x3[i.odd][:, :], o_wide[:, :], x2[i.odd][:, :], ALU.add).then_inc(x3_made.sem, 1)
                need(dve, x3_made, i, 1)
                need(dve, ln_rs, i.before(1), 4)
                for half in range(2):
                    nc.vector.bn_stats(ln_stats[:, half], x3[i.odd][:, half * HALF:(half + 1) * HALF]).then_inc(ln_step.sem, 1)
                need(dve, ln_step, i, 2)
                nc.vector.memset(carrier[:, :], 0.0)
                nc.vector.bn_aggr(ln_mv[:, :], ln_stats[:, :, :]).then_inc(ln_step.sem, 1)

            dve.wait_ge(s_scale, 16)
            nc.vector.tensor_scalar(soft[:, 4:5], soft[:, 0:1], -1.0, None, ALU.mult).then_inc(s_soft_dve, 1)
            dve.wait_ge(s_soft_dve, 1)
            nc.vector.tensor_tensor(soft[:, 1:2], soft[:, 0:1], soft[:, 4:5], ALU.max).then_inc(s_soft_dve, 1)
            dve.wait_ge(s_soft_act, 2)
            nc.vector.tensor_scalar(soft[:, 4:5], soft[:, 0:1], 0.0, soft[:, 3:4], ALU.max, ALU.add).then_inc(s_soft_dve, 1)
            for n in range(2 * KT):
                dve.wait_ge(s_high, n + 1)
                pair = wo if n < KT else sign
                nc.vector.tensor_tensor(pair[1][:, n % KT], slots[n % NS][:, :], pair[0][:, n % KT].bitcast(F32),
                                        ALU.subtract).then_inc(s_low, 1)
                if n == 2 * KT - 4:
                    add_o(Batch(0, 0))
            dve.wait_ge(s_soft_dve, 3)
            dve.wait_ge(s_low, 2 * KT)

            def fill(eng, i):
                pass

            def step(eng, i, nxt):
                need(dve, hT_high, i, 1)
                nc.vector.tensor_tensor(hT[1][:, :, :].rearrange("p t c -> p (t c)"), t_wide[:, :],
                                        hT[0][:, :, :].rearrange("p t c -> p (t c)").bitcast(F32), ALU.subtract).then_inc(hT_low.sem, 1)
                if nxt is not None:
                    add_o(nxt)
                need(dve, f_ready, i, 1)
                need(dve, y_out, i.before(2), 1)
                nc.vector.scalar_tensor_tensor(y[i.odd][:, :], s_wide[:, :], soft[:, 4:5], x3[i.odd][:, :],
                                               ALU.mult, ALU.add).then_inc(y_made.sem, 1)

            schedule(fill, step)(dve)


_INS = ['x', 'ctx_4096', 'L0_xattn_Wq', 'L0_xattn_Wk', 'L0_xattn_Wv', 'L0_xattn_Wo', 'L0_xattn_bo', 'L0_xattn_g',
        'L0_ffn_Wq', 'L0_ffn_Wr', 'L0_ffn_aux_keys', 'L0_ffn_aux_values', 'L0_ffn_Wvd', 'L0_ffn_Wvu', 'L0_ffn_Wu1',
        'L0_ffn_bu1', 'L0_ffn_Wu2', 'L0_ffn_bu2', 'L0_ffn_gate_w1', 'L0_ffn_gate_bias', 'L0_ffn_log_rel',
        'L1_xattn_Wq', 'L1_xattn_Wk', 'L1_xattn_Wv', 'L1_xattn_Wo', 'L1_ffn_sign', 'L1_ffn_scale']


class Semaphores:

    def __init__(self):
        self.stack, self.all = ExitStack(), []

    def new(self, made):
        self.all.append(self.stack.enter_context(made))
        return self.all[-1]

    def zero_and_free(self, nc):
        nc.all_engine_barrier()
        for s in self.all:
            nc.sync.sem_clear(s)
        nc.all_engine_barrier()
        self.stack.close()


def program(nc, w, out):
    def scratch(name, width):
        return nc.dram_tensor(name, (B, P, width), F32, kind="Internal").ap()

    x1_dram, x2_dram, o_dram = scratch("x1_scratch", DM), scratch("x2_scratch", DM), scratch("o_scratch", DM)
    kv_dram = scratch("kv_scratch", 2 * KVD)
    with ExitStack() as ctx:
        keep = ctx.enter_context(nc.sbuf_tensor("x1_moments", [P, B, 2], F32))
        rows = ctx.enter_context(nc.sbuf_tensor("x1_rows", [P, B, 3], F32))
        for part, args in ((layer0_attention, (w["x"], w["ctx_4096"], w, keep, x1_dram, kv_dram)),
                           (layer0_ffn_layer1_heads, (w, keep, rows, x1_dram, kv_dram, x2_dram, o_dram)),
                           (layer1_out_and_ffn, (w, x2_dram, o_dram, out))):
            sems = Semaphores()
            part(nc, sems, *args)
            sems.zero_and_free(nc)


def kernel(**inputs):
    import numpy as _np
    import concourse.bacc as _bacc
    from concourse import mybir as _mybir
    from concourse.bass_utils import run_bass_kernel_spmd as _run

    nc = _bacc.Bacc("TRN2", target_bir_lowering=False, num_devices=1)
    arrays, args = {}, {}
    for name in _INS:
        a = _np.ascontiguousarray(inputs[name])
        if a.ndim == 0:
            a = a.reshape(1)
        arrays[f"in_{name}_dram"] = a
        args[name] = nc.dram_tensor(f"in_{name}_dram", a.shape, _mybir.dt.from_np(a.dtype), kind="ExternalInput").ap()
    out = nc.dram_tensor("out_0_dram", (B, P, DM), F32, kind="ExternalOutput").ap()
    program(nc, args, out)
    r = _run(nc, [arrays], core_ids=[0])
    return r.results[0]["out_0_dram"]
```
